# Optimizing a Trainium2 kernel written in Bass

```python
import numpy as np
import jax
import jax.numpy as jnp

def _softmax(x, axis=-1):
    return jax.nn.softmax(x, axis=axis)

def _gelu(x):
    return jax.nn.gelu(x, approximate=True)

def _silu(x):
    return jax.nn.silu(x)

def _sigmoid(x):
    return jax.nn.sigmoid(x)

def _layernorm(x, axis=-1, eps=1e-05):
    m = jnp.mean(x, axis=axis, keepdims=True)
    v = jnp.var(x, axis=axis, keepdims=True)
    return (x - m) / jnp.sqrt(v + eps)

def _scatter_add(tgt, idx, src, axis=0):
    return tgt.at[idx].add(src)

def _segment_sum(src, seg, n):
    return jax.ops.segment_sum(src, seg, n)
kernel_name = 'mk_audio_tower_d2_tok_audfeat512_r4_c8bde2'

def setup_inputs(seed: int=0):
    np.random.seed(seed)
    _w = jnp.asarray

    def _rec_inputs():
        import jax
        import jax.numpy as jnp
        _rk = jax.random.key(seed)
        x = 3.78913e-05 + 1.00016 * jax.random.normal(jax.random.fold_in(_rk, 1), (16, 750, 64), jnp.float32)
        return x
    x = _rec_inputs()

    def _L0_tok_setup():
        import jax, jax.numpy as jnp
        import numpy as np
        CONTEXT = 5
        DILATION = 1
        EPS = 1e-05
        key = jax.random.key(seed)
        k1, k2, k3 = jax.random.split(key, 3)
        B, T, D, O = (64, 500, 64, 128)
        x = jax.random.normal(k1, (B, T, D), dtype=jnp.float32)
        K = D * CONTEXT
        W = jax.random.normal(k2, (O, K), dtype=jnp.float32) / np.sqrt(K).astype(np.float32)
        b = jax.random.normal(k3, (O,), dtype=jnp.float32) * 0.01
        gamma = jnp.ones((O,), dtype=jnp.float32)
        beta = jnp.zeros((O,), dtype=jnp.float32)
        return {'x': x, 'W': W, 'b': b, 'gamma': gamma, 'beta': beta}
    _L0_tok_all = _L0_tok_setup()
    _L0_tok_in = {k: v for k, v in _L0_tok_all.items() if k in ('W', 'b', 'gamma', 'beta')}
    del _L0_tok_all

    def _L0_attn_setup():
        import jax, jax.numpy as jnp
        import numpy as np
        N, T, C = (8, 512, 128)
        key = jax.random.key(seed)
        ks = jax.random.split(key, 7)
        s = 1.0 / np.sqrt(C)
        return {'x': jax.random.normal(ks[0], (N, T, C), dtype=jnp.float32), 'Wg': jax.random.uniform(ks[1], (3 * C, C), jnp.float32, -s, s), 'bg': jax.random.uniform(ks[2], (3 * C,), jnp.float32, -s, s), 'Wlr': jax.random.uniform(ks[3], (1, C), jnp.float32, -s, s), 'blr': jax.random.uniform(ks[4], (1,), jnp.float32, -s, s), 'Wo': jax.random.uniform(ks[5], (C, C), jnp.float32, -s, s), 'bo': jax.random.uniform(ks[6], (C,), jnp.float32, -s, s)}
    _L0_attn_all = _L0_attn_setup()
    _L0_attn_in = {k: v for k, v in _L0_attn_all.items() if k in ('Wg', 'bg', 'Wlr', 'blr', 'Wo', 'bo')}
    del _L0_attn_all

    def _L0_ffn_setup():
        import jax, jax.numpy as jnp
        import numpy as np
        B, S, D = (8, 2048, 128)
        E, DFF = (16, 128)
        CAPACITY = 2
        key = jax.random.key(seed)
        ks = jax.random.split(key, 4)
        x = jax.random.normal(ks[0], (B, S, D), dtype=jnp.float32)
        gate_weight = jax.random.normal(ks[1], (D, E), dtype=jnp.float32) * 0.006
        w1 = jax.random.normal(ks[2], (E, D, DFF), dtype=jnp.float32) * 0.02
        b1 = jnp.zeros((E, DFF), dtype=jnp.float32)
        w2 = jax.random.normal(ks[3], (E, DFF, D), dtype=jnp.float32) * 0.02
        b2 = jnp.zeros((E, D), dtype=jnp.float32)
        return {'x': x, 'gate_weight': gate_weight, 'w1': w1, 'b1': b1, 'w2': w2, 'b2': b2}
    _L0_ffn_all = _L0_ffn_setup()
    _L0_ffn_in = {k: v for k, v in _L0_ffn_all.items() if k in ('gate_weight', 'w1', 'b1', 'w2', 'b2')}
    del _L0_ffn_all

    def _L1_attn_setup():
        import jax, jax.numpy as jnp
        import numpy as np
        import math
        EMBED = 128
        HEADS = 2
        HEAD_DIM = EMBED // HEADS
        EPS = 1e-05

        def layer_norm(x, g, b):
            mu = jnp.mean(x, axis=-1, keepdims=True)
            var = jnp.var(x, axis=-1, keepdims=True)
            return (x - mu) * jax.lax.rsqrt(var + EPS) * g + b
        key = jax.random.key(seed)
        ks = jax.random.split(key, 16)
        s = 0.02
        inp = {'text_embeds': jax.random.normal(ks[0], (128, 32, EMBED), jnp.float32), 'video_embeds': jax.random.normal(ks[1], (64, 12, EMBED), jnp.float32), 'ln1_g': jnp.ones((EMBED,), jnp.float32), 'ln1_b': jnp.zeros((EMBED,), jnp.float32), 'Wq': jax.random.normal(ks[2], (EMBED, EMBED), jnp.float32) * s, 'bq': jnp.zeros((EMBED,), jnp.float32), 'Wk': jax.random.normal(ks[3], (EMBED, EMBED), jnp.float32) * s, 'bk': jnp.zeros((EMBED,), jnp.float32), 'Wv': jax.random.normal(ks[4], (EMBED, EMBED), jnp.float32) * s, 'bv': jnp.zeros((EMBED,), jnp.float32), 'Wo': jax.random.normal(ks[5], (EMBED, EMBED), jnp.float32) * s, 'bo': jnp.zeros((EMBED,), jnp.float32), 'Wl': jax.random.normal(ks[6], (EMBED, EMBED), jnp.float32) * s, 'bl': jnp.zeros((EMBED,), jnp.float32), 'ln2_g': jnp.ones((EMBED,), jnp.float32), 'ln2_b': jnp.zeros((EMBED,), jnp.float32), 'ln3_g': jnp.ones((EMBED,), jnp.float32), 'ln3_b': jnp.zeros((EMBED,), jnp.float32)}
        return inp
    _L1_attn_all = _L1_attn_setup()
    _L1_attn_in = {k: v for k, v in _L1_attn_all.items() if k in ('video_embeds', 'ln1_g', 'ln1_b', 'Wq', 'bq', 'Wk', 'bk', 'Wv', 'bv', 'Wo', 'bo', 'Wl', 'bl', 'ln2_g', 'ln2_b', 'ln3_g', 'ln3_b')}
    del _L1_attn_all

    def _L1_ffn_setup():
        import jax, jax.numpy as jnp
        import numpy as np
        B, S, H, E, K = (8, 1024, 128, 8, 2)
        key = jax.random.key(seed)
        ks = jax.random.split(key, 7)
        s_h = 1.0 / np.sqrt(H)
        s_2h = 1.0 / np.sqrt(2 * H)
        return {'x': jax.random.normal(ks[0], (B, S, H), dtype=jnp.float32), 'gate_w': jax.random.uniform(ks[1], (H, E), minval=-s_h, maxval=s_h, dtype=jnp.float32), 'gate_b': jax.random.uniform(ks[2], (E,), minval=-s_h, maxval=s_h, dtype=jnp.float32), 'w1': jax.random.uniform(ks[3], (E, H, 2 * H), minval=-s_h, maxval=s_h, dtype=jnp.float32), 'b1': jax.random.uniform(ks[4], (E, 2 * H), minval=-s_h, maxval=s_h, dtype=jnp.float32), 'w2': jax.random.uniform(ks[5], (E, 2 * H, H), minval=-s_2h, maxval=s_2h, dtype=jnp.float32), 'b2': jax.random.uniform(ks[6], (E, H), minval=-s_2h, maxval=s_2h, dtype=jnp.float32)}
    _L1_ffn_all = _L1_ffn_setup()
    _L1_ffn_in = {k: v for k, v in _L1_ffn_all.items() if k in ('gate_w', 'gate_b', 'w1', 'b1', 'w2', 'b2')}
    del _L1_ffn_all
    return {'x': x, 'L0_tok_W': _L0_tok_in['W'], 'L0_tok_b': _L0_tok_in['b'], 'L0_tok_gamma': _L0_tok_in['gamma'], 'L0_tok_beta': _L0_tok_in['beta'], 'L0_attn_Wg': _L0_attn_in['Wg'], 'L0_attn_bg': _L0_attn_in['bg'], 'L0_attn_Wlr': _L0_attn_in['Wlr'], 'L0_attn_blr': _L0_attn_in['blr'], 'L0_attn_Wo': _L0_attn_in['Wo'], 'L0_attn_bo': _L0_attn_in['bo'], 'L0_ffn_gate_weight': _L0_ffn_in['gate_weight'], 'L0_ffn_w1': _L0_ffn_in['w1'], 'L0_ffn_b1': _L0_ffn_in['b1'], 'L0_ffn_w2': _L0_ffn_in['w2'], 'L0_ffn_b2': _L0_ffn_in['b2'], 'L1_attn_video_embeds': _L1_attn_in['video_embeds'], 'L1_attn_ln1_g': _L1_attn_in['ln1_g'], 'L1_attn_ln1_b': _L1_attn_in['ln1_b'], 'L1_attn_Wq': _L1_attn_in['Wq'], 'L1_attn_bq': _L1_attn_in['bq'], 'L1_attn_Wk': _L1_attn_in['Wk'], 'L1_attn_bk': _L1_attn_in['bk'], 'L1_attn_Wv': _L1_attn_in['Wv'], 'L1_attn_bv': _L1_attn_in['bv'], 'L1_attn_Wo': _L1_attn_in['Wo'], 'L1_attn_bo': _L1_attn_in['bo'], 'L1_attn_Wl': _L1_attn_in['Wl'], 'L1_attn_bl': _L1_attn_in['bl'], 'L1_attn_ln2_g': _L1_attn_in['ln2_g'], 'L1_attn_ln2_b': _L1_attn_in['ln2_b'], 'L1_attn_ln3_g': _L1_attn_in['ln3_g'], 'L1_attn_ln3_b': _L1_attn_in['ln3_b'], 'L1_ffn_gate_w': _L1_ffn_in['gate_w'], 'L1_ffn_gate_b': _L1_ffn_in['gate_b'], 'L1_ffn_w1': _L1_ffn_in['w1'], 'L1_ffn_b1': _L1_ffn_in['b1'], 'L1_ffn_w2': _L1_ffn_in['w2'], 'L1_ffn_b2': _L1_ffn_in['b2']}

def reference(x, L0_tok_W, L0_tok_b, L0_tok_gamma, L0_tok_beta, L0_attn_Wg, L0_attn_bg, L0_attn_Wlr, L0_attn_blr, L0_attn_Wo, L0_attn_bo, L0_ffn_gate_weight, L0_ffn_w1, L0_ffn_b1, L0_ffn_w2, L0_ffn_b2, L1_attn_video_embeds, L1_attn_ln1_g, L1_attn_ln1_b, L1_attn_Wq, L1_attn_bq, L1_attn_Wk, L1_attn_bk, L1_attn_Wv, L1_attn_bv, L1_attn_Wo, L1_attn_bo, L1_attn_Wl, L1_attn_bl, L1_attn_ln2_g, L1_attn_ln2_b, L1_attn_ln3_g, L1_attn_ln3_b, L1_ffn_gate_w, L1_ffn_gate_b, L1_ffn_w1, L1_ffn_b1, L1_ffn_w2, L1_ffn_b2):
    import jax
    import jax.numpy as jnp

    def _L0_tok_ref(x, W, b, gamma, beta):
        import jax, jax.numpy as jnp
        import numpy as np
        CONTEXT = 5
        DILATION = 1
        EPS = 1e-05
        B, T, D = x.shape
        new_T = T - DILATION * (CONTEXT - 1)
        win = jnp.concatenate([x[:, i * DILATION:i * DILATION + new_T, :] for i in range(CONTEXT)], axis=-1)
        y = jnp.einsum('btk,ok->bto', win, W) + b
        y = jax.nn.relu(y)
        mean = jnp.mean(y, axis=(0, 1))
        var = jnp.mean(jnp.square(y - mean), axis=(0, 1))
        y = (y - mean) * jax.lax.rsqrt(var + EPS) * gamma + beta
        return y

    def _L0_attn_ref(x, Wg, bg, Wlr, blr, Wo, bo):
        import jax, jax.numpy as jnp
        import numpy as np
        N, T, C = (8, 512, 128)
        g = x @ Wg.T + bg
        q, k, v = jnp.split(g, 3, axis=-1)
        lr = x @ Wlr.T + blr
        k = k / jnp.linalg.norm(k, axis=-1, keepdims=True)

        def step(S, kv_t):
            k_t, v_t = kv_t
            u_t = v_t - jnp.einsum('nc,ncd->nd', k_t, S)
            S = S + k_t[:, :, None] * u_t[:, None, :]
            return (S, u_t)
        S0 = jnp.zeros((x.shape[0], C, C), dtype=x.dtype)
        _, u = jax.lax.scan(step, S0, (k.transpose(1, 0, 2), v.transpose(1, 0, 2)))
        u = u.transpose(1, 0, 2)
        kv = jnp.einsum('ntk,ntv->nkv', k, lr * u)
        y = jnp.einsum('nsk,nkv->nsv', q, kv)
        return y @ Wo.T + bo

    def _L0_ffn_ref(x, gate_weight, w1, b1, w2, b2):
        import jax, jax.numpy as jnp
        import numpy as np
        B, S, D = (8, 2048, 128)
        E, DFF = (16, 128)
        CAPACITY = 2
        Bx, Sx, Dx = x.shape
        num_experts = gate_weight.shape[1]
        k = Sx // num_experts * CAPACITY
        logits = jnp.einsum('bsd,de->bse', x, gate_weight)
        affinity = jax.nn.softmax(logits, axis=-1).transpose(0, 2, 1)
        gating, index = jax.lax.top_k(affinity, k)
        x_in = jnp.take_along_axis(x[:, None, :, :], index[..., None], axis=2)
        h = jax.nn.gelu(jnp.einsum('bekd,edh->bekh', x_in, w1) + b1[None, :, None, :])
        x_e = jnp.einsum('bekh,ehd->bekd', h, w2) + b2[None, :, None, :]
        weighted = gating[..., None] * x_e
        out = jnp.zeros_like(x)
        idx_flat = index.reshape(Bx, num_experts * k)
        vals_flat = weighted.reshape(Bx, num_experts * k, Dx)
        out = out.at[jnp.arange(Bx)[:, None], idx_flat].add(vals_flat)
        return out

    def _L1_attn_ref(text_embeds, video_embeds, ln1_g, ln1_b, Wq, bq, Wk, bk, Wv, bv, Wo, bo, Wl, bl, ln2_g, ln2_b, ln3_g, ln3_b):
        import jax, jax.numpy as jnp
        import numpy as np
        import math
        EMBED = 128
        HEADS = 2
        HEAD_DIM = EMBED // HEADS
        EPS = 1e-05

        def layer_norm(x, g, b):
            mu = jnp.mean(x, axis=-1, keepdims=True)
            var = jnp.var(x, axis=-1, keepdims=True)
            return (x - mu) * jax.lax.rsqrt(var + EPS) * g + b
        t = layer_norm(text_embeds, ln1_g, ln1_b)
        vd = layer_norm(video_embeds, ln1_g, ln1_b)
        T, Nw, _ = t.shape
        V, Fr, _ = vd.shape
        q = (t @ Wq.T + bq).reshape(T, Nw, HEADS, HEAD_DIM)
        k = (vd @ Wk.T + bk).reshape(V, Fr, HEADS, HEAD_DIM)
        v = (vd @ Wv.T + bv).reshape(V, Fr, HEADS, HEAD_DIM)
        logits = jnp.einsum('avhd,bthd->abhvt', k, q) / math.sqrt(HEAD_DIM)
        weights = jax.nn.softmax(logits, axis=3)
        attn = jnp.einsum('avhd,abhvt->abhtd', v, weights)
        attn = attn.transpose(0, 1, 3, 2, 4).reshape(V, T, Nw, EMBED)
        attn = attn.mean(axis=0)
        o = attn @ Wo.T + bo
        o = layer_norm(o, ln2_g, ln2_b)
        lin = o @ Wl.T + bl
        out = layer_norm(o + lin, ln3_g, ln3_b)
        return out

    def _L1_ffn_ref(x, gate_w, gate_b, w1, b1, w2, b2):
        import jax, jax.numpy as jnp
        import numpy as np
        B, S, H, E, K = (8, 1024, 128, 8, 2)
        logits = jnp.einsum('bsh,he->bse', x, gate_w) + gate_b
        topk_vals, topk_idx = jax.lax.top_k(logits, K)
        topk_weights = jax.nn.softmax(topk_vals, axis=-1)
        mask = jax.nn.one_hot(topk_idx, E, dtype=topk_weights.dtype)
        weights = jnp.einsum('bske,bsk->bse', mask, topk_weights)
        h = jax.nn.relu(jnp.einsum('bsh,ehf->bsef', x, w1) + b1)
        expert_out = jnp.einsum('bsef,efh->bseh', h, w2) + b2
        return jnp.einsum('bseh,bse->bsh', expert_out, weights)
    h = _L0_tok_ref(x, L0_tok_W, L0_tok_b, L0_tok_gamma, L0_tok_beta)
    h = h + _L0_attn_ref(_layernorm(h, axis=-1), L0_attn_Wg, L0_attn_bg, L0_attn_Wlr, L0_attn_blr, L0_attn_Wo, L0_attn_bo)
    h = h + _L0_ffn_ref(_layernorm(h, axis=-1), L0_ffn_gate_weight, L0_ffn_w1, L0_ffn_b1, L0_ffn_w2, L0_ffn_b2)
    h = h + _L1_attn_ref(_layernorm(h, axis=-1), L1_attn_video_embeds, L1_attn_ln1_g, L1_attn_ln1_b, L1_attn_Wq, L1_attn_bq, L1_attn_Wk, L1_attn_bk, L1_attn_Wv, L1_attn_bv, L1_attn_Wo, L1_attn_bo, L1_attn_Wl, L1_attn_bl, L1_attn_ln2_g, L1_attn_ln2_b, L1_attn_ln3_g, L1_attn_ln3_b)
    h = h + _L1_ffn_ref(_layernorm(h, axis=-1), L1_ffn_gate_w, L1_ffn_gate_b, L1_ffn_w1, L1_ffn_b1, L1_ffn_w2, L1_ffn_b2)
    return h

_drawn_inputs = setup_inputs


def setup_inputs(seed=0):
    import zlib

    import numpy as np

    out = dict(_drawn_inputs(seed))
    spreads = {'L0_tok_gamma': (1.0, 0.2),
     'L0_tok_beta': (0.0, 0.1),
     'L0_ffn_b1': (0.0, 0.8),
     'L0_ffn_b2': (0.0, 0.8),
     'L1_attn_ln1_g': (1.0, 0.6),
     'L1_attn_ln1_b': (0.0, 0.402),
     'L1_attn_bq': (0.0, 0.8),
     'L1_attn_bk': (0.0, 0.8),
     'L1_attn_bv': (0.0, 0.1),
     'L1_attn_bo': (0.0, 0.1),
     'L1_attn_bl': (0.0, 0.1),
     'L1_attn_ln2_g': (1.0, 0.2),
     'L1_attn_ln2_b': (0.0, 0.1),
     'L1_attn_ln3_g': (1.0, 0.2),
     'L1_attn_ln3_b': (0.0, 0.1)}
    factors = {'L0_tok_b': 4.088,
     'L0_ffn_gate_weight': 8.0,
     'L0_ffn_w1': 8.0,
     'L0_ffn_w2': 8.0,
     'L1_attn_video_embeds': 7.487,
     'L1_attn_Wq': 8.0,
     'L1_attn_Wk': 8.0,
     'L1_attn_Wv': 2.88,
     'L1_ffn_gate_b': 3.655,
     'L1_ffn_b1': 8.0,
     'L1_ffn_b2': 5.737}
    for name, (base, spread) in spreads.items():
        noise = np.random.default_rng([zlib.crc32(name.encode()), seed]).standard_normal(out[name].shape)
        drawn = base * np.exp(spread * noise) if base else spread * noise
        out[name] = jnp.asarray(drawn.astype(out[name].dtype))
    for name, factor in factors.items():
        out[name] = (out[name] * factor).astype(out[name].dtype)
    return out
```

```python
from contextlib import ExitStack

import numpy as np

import concourse.bass as bass
from concourse import mybir

ALU = mybir.AluOpType
ACT = mybir.ActivationFunctionType
F32 = mybir.dt.float32
BF16 = mybir.dt.bfloat16
AX_X = mybir.AxisListType.X

P = 128
B = 16
T_IN = 750
CTX = 5
T = T_IN - CTX + 1
C = 128
NC = 6
LAST = T - (NC - 1) * P
TP = NC * P
NCH = B * NC
PAIRS = B // 2
HALF_T = T // 2
GC = 3
GW = GC * P
LEVELS = (2, 4, 8, 16, 32, 64)
NL = len(LEVELS)
E0 = 16
CAP = T // E0 * 2
E1 = 8
NV = 64
FR = 12
NFREE = (384, T - 384)
EPS = 1e-5
DEBUG_STOP = 99


def rows(c):
    return P if c < NC - 1 else LAST


class Ctx:
    pass


def phase_scope(nc):
    stack = ExitStack()

    def sb(name, shape, dt=F32):
        return stack.enter_context(nc.sbuf_tensor(name, shape, dt))

    def sem(name):
        return stack.enter_context(nc.semaphore(name))

    return stack, sb, sem


def conv_phase(nc, k):
    stack, sb, sem = phase_scope(nc)
    with stack:
        yT = sb("yT", [P, B, T])
        yn = sb("yn", [P, 2, TP])
        bst = sb("bst", [P, 2 * B, 6])
        bmv = sb("bmv", [P, 2])
        bsc = sb("bsc", [P, 4])
        xw = k.h[:].rearrange("p b c d -> p (b c d)")[:, 0:B * T_IN].rearrange("p (b t) -> p b t", t=T_IN)
        x_in = [sem(f"x_in{q}") for q in range(4)]
        w_in, rest_in = k.w_in, k.rest_in
        conv_ps, conv_relu, stats = sem("conv_ps"), sem("conv_relu"), sem("conv_stats")
        bn_chain, bn_sqrt = sem("bn_chain"), sem("bn_sqrt")
        yn_ready, tr_ps, h_stored, pads = sem("yn_ready"), sem("tr_ps"), sem("h_stored"), sem("pads")
        qb = B // 4

        with nc.Block() as block:
            @block.sync
            def _(sp):
                for ap, dram in k.first_loads:
                    sp.dma_start(ap, dram).then_inc(w_in, 16)
                for q in range(4):
                    s = slice(q * qb, (q + 1) * qb)
                    sp.dma_start(xw[0:64, s, :], k.xT[:, s, :]).then_inc(x_in[q], 16)
                    sp.dma_start(xw[64:128, s, 0:T_IN - 1], k.xT[:, s, 1:T_IN]).then_inc(x_in[q], 16)
                for ap, dram in k.rest_loads:
                    sp.dma_start(ap, dram).then_inc(rest_in, 16)

            @block.tensor
            def _(pe):
                pe.wait_ge(w_in, 16 * len(k.first_loads))
                for q in range(4):
                    pe.wait_ge(x_in[q], 32)
                    with pe.Fori(q * qb // 2, (q + 1) * qb // 2) as i:
                        for par in range(2):
                            b = i * 2 + par
                            for half in range(2):
                                pe.wait_ge(conv_relu, i * 4 + (par * 2 + half + 1))
                                ps = k.ps[:, par * 2 + half, 0:HALF_T]
                                t0 = half * HALF_T
                                nc.tensor.matmul(ps, k.wc01[:, :], xw[:, b, t0:t0 + HALF_T], start=True, stop=False)
                                nc.tensor.matmul(ps, k.wc23[:, :], xw[:, b, t0 + 2:t0 + 2 + HALF_T],
                                                 start=False, stop=False)
                                nc.tensor.matmul(ps, k.wc4[:, :], xw[0:64, b, t0 + 4:t0 + 4 + HALF_T],
                                                 start=False, stop=True).then_inc(conv_ps, 1)

            @block.scalar
            def _(act):
                act.wait_ge(w_in, 16 * len(k.first_loads))
                act.sem_inc(conv_relu, 4)
                with act.Fori(0, PAIRS) as i:
                    for par in range(2):
                        b = i * 2 + par
                        for half in range(2):
                            act.wait_ge(conv_ps, i * 4 + (par * 2 + half + 1))
                            nc.scalar.activation(yT[:, b, half * HALF_T:(half + 1) * HALF_T],
                                                 k.ps[:, par * 2 + half, 0:HALF_T], ACT.Relu,
                                                 bias=k.conv_b[:, 0:1]).then_inc(conv_relu, 1)
                act.wait_ge(bn_chain, 1)
                nc.scalar.activation(bsc[:, 0:1], bmv[:, 1:2], ACT.Sqrt, bias=k.eps[:, 0:1]).then_inc(bn_sqrt, 1)

            @block.vector
            def _(dve):
                nc.vector.memset(k.eps[:], EPS)
                with dve.Fori(0, PAIRS) as i:
                    for par in range(2):
                        b = i * 2 + par
                        for half in range(2):
                            dve.wait_ge(conv_relu, i * 4 + (par * 2 + half + 5))
                            nc.vector.bn_stats(bst[:, i * 4 + (par * 2 + half), :],
                                               yT[:, b, half * HALF_T:(half + 1) * HALF_T]).then_inc(stats, 1)
                dve.wait_ge(stats, 2 * B)
                nc.vector.bn_aggr(bmv[:, :], bst[:].rearrange("p a s -> p (a s)")).then_inc(bn_chain, 1)
                dve.wait_ge(bn_sqrt, 1)
                nc.vector.reciprocal(bsc[:, 1:2], bsc[:, 0:1]).then_inc(bn_chain, 1)
                dve.wait_ge(bn_chain, 2)
                nc.vector.tensor_tensor(bsc[:, 2:3], bsc[:, 1:2], k.gamma[:, 0:1], ALU.mult).then_inc(bn_chain, 1)
                dve.wait_ge(bn_chain, 3)
                nc.vector.tensor_tensor(bsc[:, 0:1], bmv[:, 0:1], bsc[:, 2:3], ALU.mult).then_inc(bn_chain, 1)
                dve.wait_ge(bn_chain, 4)
                nc.vector.tensor_tensor(bsc[:, 3:4], k.beta[:, 0:1], bsc[:, 0:1], ALU.subtract).then_inc(bn_chain, 1)
                dve.wait_ge(bn_chain, 5)

        with nc.Block() as block:
            @block.sync
            def _(sp):
                sp.wait_ge(rest_in, 16 * len(k.rest_loads))

            @block.gpsimd
            def _(pool):
                nc.gpsimd.memset(k.h[96:128, :, NC - 1, :], 0.0).then_inc(pads, 1)

            @block.vector
            def _(dve):
                with dve.Fori(0, PAIRS) as i:
                    for par in range(2):
                        b = i * 2 + par
                        dve.wait_ge(tr_ps, i * 2 + (par + 1))
                        nc.vector.tensor_scalar(yn[:, par, 0:T], yT[:, b, :], bsc[:, 2:3], bsc[:, 3:4],
                                                ALU.mult, ALU.add).then_inc(yn_ready, 1)

            @block.tensor
            def _(pe):
                pe.sem_inc(tr_ps, 2)
                with pe.Fori(0, PAIRS) as i:
                    for par in range(2):
                        pe.wait_ge(yn_ready, i * 2 + (par + 1))
                        pe.wait_ge(h_stored, i * 2 + (par + 1))
                        for c in range(NC):
                            n = rows(c)
                            last = nc.tensor.transpose(k.psf[0:n, par * 1024 + c * P:par * 1024 + (c + 1) * P],
                                                       yn[:, par, c * P:c * P + n], k.ident[:, :])
                        last.then_inc(tr_ps, 1)

            @block.scalar
            def _(act):
                act.sem_inc(h_stored, 2)
                act.wait_ge(pads, 1)
                with act.Fori(0, PAIRS) as i:
                    for par in range(2):
                        b = i * 2 + par
                        act.wait_ge(tr_ps, i * 2 + (par + 3))
                        o = par * 1024
                        nc.scalar.activation(k.h[:, b, 0:NC - 1, :],
                                             k.psf[:, o:o + 5 * P].rearrange("p (c d) -> p c d", d=P), ACT.Copy)
                        nc.scalar.activation(k.h[0:LAST, b, NC - 1, :],
                                             k.psf[0:LAST, o + 5 * P:o + 6 * P], ACT.Copy).then_inc(h_stored, 1)


def norm_phase(nc, k, tag, src, twice=False):
    stack, sb, sem = phase_scope(nc)
    with stack:
        st = sb(tag + "st", [P, NCH, 6])
        tmp = sb(tag + "tmp", [P, 4, NCH])
        seen, chain, rooted = sem(tag + "seen"), sem(tag + "chain"), sem(tag + "rooted")
        with nc.Block() as block:
            @block.vector
            def _(dve):
                with dve.Fori(0, B) as b:
                    for c in range(NC):
                        last = nc.vector.bn_stats(st[:, b * NC + c, :], src[:, b, c, :])
                    last.then_inc(seen, 1)
                dve.wait_ge(seen, B)
                n = [0]

                def link(ins):
                    n[0] += 1
                    ins.then_inc(chain, 1)
                    dve.wait_ge(chain, n[0])

                me, ve, mo, vo = (st[:, :, q] for q in (1, 2, 4, 5))
                link(nc.vector.tensor_tensor(tmp[:, 0, :], me, mo, ALU.add))
                link(nc.vector.tensor_tensor(tmp[:, 1, :], me, mo, ALU.subtract))
                link(nc.vector.tensor_tensor(tmp[:, 2, :], ve, vo, ALU.add))
                link(nc.vector.tensor_scalar(k.mean[:, :], tmp[:, 0, :], 0.5, None, ALU.mult))
                link(nc.vector.tensor_tensor(tmp[:, 3, :], tmp[:, 1, :], tmp[:, 1, :], ALU.mult))
                link(nc.vector.tensor_scalar(tmp[:, 0, :], tmp[:, 2, :], 1.0 / C, None, ALU.mult))
                link(nc.vector.scalar_tensor_tensor(out=tmp[:, 1, :], in0=tmp[:, 3, :], scalar=0.25,
                                                    in1=tmp[:, 0, :], op0=ALU.mult, op1=ALU.add))
                var_at = n[0]
                dve.wait_ge(rooted, 1)
                link(nc.vector.reciprocal(k.rstd[:, :], tmp[:, 2, :]))
                if twice:
                    link(nc.vector.tensor_tensor(tmp[:, 0, :], k.rstd[:, :], k.rstd[:, :], ALU.mult))
                    link(nc.vector.tensor_tensor(tmp[:, 3, :], tmp[:, 0, :], tmp[:, 1, :], ALU.mult))
                    dve.wait_ge(rooted, 2)
                    link(nc.vector.reciprocal(tmp[:, 0, :], tmp[:, 2, :]))
                    link(nc.vector.tensor_tensor(k.rstd[:, :], k.rstd[:, :], tmp[:, 0, :], ALU.mult))
                assert var_at == 7

            @block.scalar
            def _(act):
                act.wait_ge(chain, 7)
                nc.scalar.activation(tmp[:, 2, :], tmp[:, 1, :], ACT.Sqrt, bias=k.eps[:, 0:1]).then_inc(rooted, 1)
                if twice:
                    act.wait_ge(chain, 10)
                    nc.scalar.activation(tmp[:, 2, :], tmp[:, 3, :], ACT.Sqrt, bias=k.eps[:, 0:1]).then_inc(rooted, 1)


class NormTranspose:

    def __init__(self, nc, k, tag, sb, sem):
        self.nc, self.k = nc, k
        self.base = 0
        self.xl = sb(tag + "xl", [P, 4, GC, P])
        self.xT = sb(tag + "xT", [P, 2, TP])
        self.normed, self.turned, self.moved = sem(tag + "normed"), sem(tag + "turned"), sem(tag + "moved")

    def vector(self, dve, i, src):
        for g in range(4):
            b = i * 2 + g // 2
            for j in range(GC):
                c = (g % 2) * GC + j
                at = i * (2 * NC) + ((g // 2) * NC + c)
                last = self.nc.vector.tensor_scalar(
                    self.xl[:, g, j, :], src[:, b, c, :], self.k.mean[:, bass.ds(at, 1)],
                    self.k.rstd[:, bass.ds(at, 1)], ALU.subtract, ALU.mult)
            last.then_inc(self.normed, 1)

    def tensor(self, pe, i):
        for g in range(4):
            pe.wait_ge(self.normed, i * 4 + (self.base + g + 1))
            for j in range(GC):
                last = self.nc.tensor.transpose(self.k.ps[:, g, j * P:(j + 1) * P], self.xl[:, g, j, :],
                                                self.k.ident[:, :])
            last.then_inc(self.turned, 1)

    def scalar(self, act, i, scale=None, bias=None):
        for g in range(4):
            act.wait_ge(self.turned, i * 4 + (self.base + g + 1))
            out = self.xT[:, g // 2, (g % 2) * GW:(g % 2 + 1) * GW]
            if scale is None:
                ins = self.nc.scalar.activation(out, self.k.ps[:, g, 0:GW], ACT.Copy)
            else:
                ins = self.nc.scalar.activation(out, self.k.ps[:, g, 0:GW], ACT.Identity, scale=scale, bias=bias)
            ins.then_inc(self.moved, 1)


def delta_phase(nc, k):
    stack, sb, sem = phase_scope(nc)
    with stack:
        nt = NormTranspose(nc, k, "d_", sb, sem)
        kvl = sb("kvl", [P, 12, 2 * C + 1])
        junk = sb("junk", [P, 12, C])
        nk = sb("nk", [P, 12])
        nks = sb("nks", [P, 12])
        rk = sb("rk", [P, 12])
        kh = sb("kh", [P, 12, P])
        kT = sb("kT", [P, 12, P])
        NT = sb("NT", [P, 4, GC, P])
        D = sb("D", [P, 4, GC, P])
        DT = sb("DT", [P, 4, GC, P])
        W = sb("W", [P, 4, GC, P])
        R = sb("R", [P, 2, P])
        UU = sb("UU", [P, 2, 2 * P])
        S = sb("S", [P, 2, P])
        kvs = sb("kvs", [P, 2, P])
        PT = sb("PT", [P, 2, P + 1])
        M = sb("M", [P, 2, P])
        bb = sb("bb", [P, 2, P])
        kv_ps, kv_ready, squared, rooted, rk_ready = (sem(x) for x in ("kv_ps", "kv_ready", "k_sq", "k_root", "rk_ready"))
        kh_ready, kT_ps, kT_ready, gram_ps, nt_ready = (sem(x) for x in ("kh_ready", "kT_ps", "kT_ready", "gram_ps", "nt_ready"))
        m0, dt0, d0_ps, d0 = (sem(x) for x in ("m0", "dt0", "d0_ps", "d0"))
        w_ps, w_ready, x_ps, d_ready, t_ps, dt_ready = (sem(x) for x in ("w_ps", "w_ready", "x_ps", "d_ready", "t_ps", "dt_ready"))
        r_ps, r_ready, u_ps, u_ready, sk_ps, s_ready = (
            sem(x) for x in ("r_ps", "r_ready", "u_ps", "u_ready", "sk_ps", "s_ready"))
        kvs_ready, pt_ps, pt_ready, m_ps, m_ready, bb_ready, y_ps, hb_ready, h_ready = (
            sem(x) for x in ("kvs_ready", "pt_ps", "pt_ready", "m_ps", "m_ready", "bb_ready", "y_ps", "hb_ready", "dh_ready"))
        zeroed = sem("rk_zeroed")

        def kv_bank(m):
            return (4 + m) % 8

        def y_bank(g):
            return (2, 3, 6, 7)[g]

        def bc(row, n):
            return row[:, None, :].to_broadcast([P, n, P])

        with nc.Block() as block:
            @block.vector
            def _(dve):
                nc.vector.memset(rk[:], 0.0).then_inc(zeroed, 1)
                dve.wait_ge(zeroed, 1)
                with dve.Fori(0, PAIRS) as i:
                    nt.vector(dve, i, k.h)
                    for m in range(12):
                        dve.wait_ge(kv_ps, i * 12 + (m + 1))
                        nc.vector.tensor_tensor(kvl[:, m, :], k.ps[:, kv_bank(m), 0:2 * C + 1], k.kvl_b[:, :],
                                                ALU.add).then_inc(kv_ready, 1)
                    dve.wait_ge(rooted, i + 1)
                    rk2 = rk[:].rearrange("p (s c) -> p s c", c=NC)
                    nks2 = nks[:].rearrange("p (s c) -> p s c", c=NC)
                    nc.vector.reciprocal(rk2[:, :, 0:NC - 1], nks2[:, :, 0:NC - 1])
                    nc.vector.reciprocal(rk2[0:LAST, :, NC - 1], nks2[0:LAST, :, NC - 1]).then_inc(rk_ready, 1)
                    for g in range(4):
                        dve.wait_ge(gram_ps, i * 4 + (g + 1))
                        nc.vector.tensor_tensor(NT[:, g], k.ps[:, 4 + g, 0:GW].rearrange("p (c t) -> p c t", t=P),
                                                bc(k.upper, GC), ALU.mult).then_inc(nt_ready, 1)
                    for lv in range(NL):
                        for g in range(4):
                            dve.wait_ge(w_ps, i * (4 * NL) + (lv * 4 + g + 1))
                            nc.vector.tensor_tensor(W[:, g], k.ps[:, 4 + g, 0:GW].rearrange("p (c t) -> p c t", t=P),
                                                    bc(k.lmask[:, lv + 1, :], GC), ALU.mult).then_inc(w_ready, 1)
                        for g in range(4):
                            dve.wait_ge(x_ps, i * (4 * NL) + (lv * 4 + g + 1))
                            nc.vector.tensor_tensor(D[:, g], D[:, g],
                                                    k.ps[:, g, 0:GW].rearrange("p (c t) -> p c t", t=P),
                                                    ALU.subtract).then_inc(d_ready, 1)
                    for c in range(NC):
                        for par in range(2):
                            m = par * NC + c
                            if c:
                                dve.wait_ge(r_ps, i * 10 + ((c - 1) * 2 + par + 1))
                                nc.vector.tensor_tensor(R[:, par, :], kvl[:, m, C:2 * C], k.ps[:, par, 0:P],
                                                        ALU.subtract).then_inc(r_ready, 1)
                        for par in range(2):
                            m = par * NC + c
                            dve.wait_ge(u_ps, i * 12 + (c * 2 + par + 1))
                            nc.vector.tensor_scalar(UU[:, par, P:2 * P], k.ps[:, 2 + par, 0:P],
                                                    kvl[:, m, 2 * C:2 * C + 1], None, ALU.mult)
                            nc.vector.tensor_copy(UU[:, par, 0:P], k.ps[:, 2 + par, 0:P]).then_inc(u_ready, 1)
                    for par in range(2):
                        dve.wait_ge(m_ps, i * 2 + (par + 1))
                        nc.vector.tensor_tensor(bb[:, par, :], k.ps[:, 4 + par, 0:P], k.bo0[:, :],
                                                ALU.add).then_inc(bb_ready, 1)
                    for g in range(4):
                        b, c0 = i * 2 + g // 2, (g % 2) * GC
                        dve.wait_ge(y_ps, i * 4 + (g + 1))
                        dve.wait_ge(hb_ready, i * 4 + (g + 1))
                        nc.vector.tensor_tensor(k.h[:, b, c0:c0 + GC, :], k.h[:, b, c0:c0 + GC, :],
                                                k.ps[:, y_bank(g), 0:GW].rearrange("p (c t) -> p c t", t=P),
                                                ALU.add).then_inc(h_ready, 1)

            @block.gpsimd
            def _(pool):
                with pool.Fori(0, PAIRS) as i:
                    for g in range(4):
                        m0_ = (g // 2) * NC + (g % 2) * GC
                        if g == 0:
                            pool.wait_ge(rk_ready, i + 1)
                        nc.gpsimd.tensor_tensor(kh[:, m0_:m0_ + GC, :], kvl[:, m0_:m0_ + GC, 0:C],
                                                rk[:, m0_:m0_ + GC, None].to_broadcast([P, GC, P]),
                                                ALU.mult).then_inc(kh_ready, 1)
                    for g in range(4):
                        pool.wait_ge(nt_ready, i * 4 + (g + 1))
                        nc.gpsimd.tensor_tensor(W[:, g], NT[:, g], bc(k.umask1, GC), ALU.mult).then_inc(m0, 1)
                        pool.wait_ge(m0, i * 4 + (g + 1))
                        nc.gpsimd.tensor_tensor(DT[:, g], bc(k.ident, GC), W[:, g], ALU.subtract).then_inc(dt0, 1)
                    for g in range(4):
                        b, c0 = i * 2 + g // 2, (g % 2) * GC
                        pool.wait_ge(bb_ready, i * 2 + (g // 2 + 1))
                        nc.gpsimd.tensor_tensor(k.h[:, b, c0:c0 + GC, :], k.h[:, b, c0:c0 + GC, :],
                                                bb[:, g // 2, None, :].to_broadcast([P, GC, P]),
                                                ALU.add).then_inc(hb_ready, 1)

            @block.scalar
            def _(act):
                with act.Fori(0, PAIRS) as i:
                    nt.scalar(act, i)
                    for m in range(12):
                        act.wait_ge(kv_ready, i * 12 + (m + 1))
                        nc.scalar.activation(junk[:, m, :], kvl[:, m, 0:C], ACT.Square,
                                             accum_out=nk[:, m:m + 1]).then_inc(squared, 1)
                    act.wait_ge(squared, i * 12 + 12)
                    nc.scalar.activation(nks[:, :], nk[:, :], ACT.Sqrt).then_inc(rooted, 1)
                    for g in range(4):
                        act.wait_ge(kT_ps, i * 4 + (g + 1))
                        m = (g // 2) * NC + (g % 2) * GC
                        nc.scalar.activation(kT[:, m:m + GC, :].rearrange("p c t -> p (c t)"), k.ps[:, g, 0:GW],
                                             ACT.Copy).then_inc(kT_ready, 1)
                    for g in range(4):
                        act.wait_ge(d0_ps, i * 4 + (g + 1))
                        nc.scalar.activation(D[:, g].rearrange("p c t -> p (c t)"), k.ps[:, g, 0:GW],
                                             ACT.Copy).then_inc(d0, 1)
                    for lv in range(NL):
                        for g in range(4):
                            act.wait_ge(t_ps, i * (4 * NL) + (lv * 4 + g + 1))
                            nc.scalar.activation(DT[:, g].rearrange("p c t -> p (c t)"), k.ps[:, 4 + g, 0:GW],
                                                 ACT.Copy).then_inc(dt_ready, 1)
                    for c in range(NC):
                        for par in range(2):
                            act.wait_ge(sk_ps, i * 12 + (c * 2 + par + 1))
                            if c < NC - 1:
                                nc.scalar.activation(S[:, par, :], k.ps[:, 4 + par, 0:P], ACT.Copy).then_inc(s_ready, 1)
                            else:
                                nc.scalar.activation(kvs[:, par, :], k.ps[:, 4 + par, P:2 * P],
                                                     ACT.Copy).then_inc(kvs_ready, 1)
                    for par in range(2):
                        act.wait_ge(pt_ps, i * 2 + (par + 1))
                        nc.scalar.activation(PT[:, par, :], k.ps[:, 6 + par, 0:P + 1], ACT.Copy).then_inc(pt_ready, 1)
                    for par in range(2):
                        act.wait_ge(m_ps, i * 2 + (par + 1))
                        nc.scalar.activation(M[:, par, :], k.ps[:, par, 0:P], ACT.Copy).then_inc(m_ready, 1)

            @block.tensor
            def _(pe):
                with pe.Fori(0, PAIRS) as i:
                    nt.tensor(pe, i)
                    for m in range(12):
                        pe.wait_ge(nt.moved, i * 4 + (min(m // GC, 3) + 1 if m < 4 else 4))
                        if m >= 8:
                            pe.wait_ge(kv_ready, i * 12 + (m - 7))
                        par, c = m // NC, m % NC
                        nc.tensor.matmul(k.ps[:, kv_bank(m), 0:2 * C + 1], nt.xT[:, par, c * P:(c + 1) * P],
                                         k.wkvl[:, :], start=True, stop=True).then_inc(kv_ps, 1)
                    for g in range(4):
                        pe.wait_ge(kh_ready, i * 4 + (g + 1))
                        for j in range(GC):
                            m = (g // 2) * NC + (g % 2) * GC + j
                            last = nc.tensor.transpose(k.ps[:, g, j * P:(j + 1) * P], kh[:, m, :], k.ident[:, :])
                        last.then_inc(kT_ps, 1)
                    for g in range(4):
                        pe.wait_ge(kT_ready, i * 4 + (g + 1))
                        for j in range(GC):
                            m = (g // 2) * NC + (g % 2) * GC + j
                            last = nc.tensor.matmul(k.ps[:, 4 + g, j * P:(j + 1) * P], kT[:, m, :], kT[:, m, :],
                                                    start=True, stop=True)
                        last.then_inc(gram_ps, 1)
                    for g in range(4):
                        pe.wait_ge(dt0, i * 4 + (g + 1))
                        for j in range(GC):
                            last = nc.tensor.transpose(k.ps[:, g, j * P:(j + 1) * P], DT[:, g, j, :], k.ident[:, :])
                        last.then_inc(d0_ps, 1)
                    for lv in range(NL):
                        for g in range(4):
                            if lv == 0:
                                pe.wait_ge(d0, i * 4 + (g + 1))
                            else:
                                pe.wait_ge(dt_ready, i * (4 * NL) + ((lv - 1) * 4 + g + 1))
                            for j in range(GC):
                                last = nc.tensor.matmul(k.ps[:, 4 + g, j * P:(j + 1) * P], NT[:, g, j, :],
                                                        D[:, g, j, :], start=True, stop=True)
                            last.then_inc(w_ps, 1)
                        for g in range(4):
                            pe.wait_ge(w_ready, i * (4 * NL) + (lv * 4 + g + 1))
                            for j in range(GC):
                                last = nc.tensor.matmul(k.ps[:, g, j * P:(j + 1) * P], DT[:, g, j, :],
                                                        W[:, g, j, :], start=True, stop=True)
                            last.then_inc(x_ps, 1)
                        for g in range(4):
                            pe.wait_ge(d_ready, i * (4 * NL) + (lv * 4 + g + 1))
                            for j in range(GC):
                                last = nc.tensor.transpose(k.ps[:, 4 + g, j * P:(j + 1) * P], D[:, g, j, :],
                                                           k.ident[:, :])
                            last.then_inc(t_ps, 1)
                    for c in range(NC):
                        n = rows(c)
                        if c:
                            for par in range(2):
                                pe.wait_ge(s_ready, i * 10 + ((c - 1) * 2 + par + 1))
                                nc.tensor.matmul(k.ps[:, par, 0:P], kT[:, par * NC + c, :], S[:, par, :],
                                                 start=True, stop=True).then_inc(r_ps, 1)
                        for par in range(2):
                            g = par * 2 + c // GC
                            if c == 0:
                                pe.wait_ge(dt_ready, i * (4 * NL) + 4 * NL)
                                rhs = kvl[:, par * NC, C:2 * C]
                            else:
                                pe.wait_ge(r_ready, i * 10 + ((c - 1) * 2 + par + 1))
                                rhs = R[:, par, :]
                            nc.tensor.matmul(k.ps[:, 2 + par, 0:P], DT[:, g, c % GC, :], rhs,
                                             start=True, stop=True).then_inc(u_ps, 1)
                        for par in range(2):
                            pe.wait_ge(u_ready, i * 12 + (c * 2 + par + 1))
                            nc.tensor.matmul(k.ps[:, 4 + par, 0:2 * P], kh[0:n, par * NC + c, :], UU[0:n, par, :],
                                             start=(c == 0), stop=True, skip_group_check=True).then_inc(sk_ps, 1)
                    for par in range(2):
                        pe.wait_ge(kvs_ready, i * 2 + (par + 1))
                        nc.tensor.matmul(k.ps[:, 6 + par, 0:P + 1], kvs[:, par, :], k.wqb[:, :],
                                         start=True, stop=True).then_inc(pt_ps, 1)
                    for par in range(2):
                        pe.wait_ge(pt_ready, i * 2 + (par + 1))
                        nc.tensor.matmul(k.ps[:, par, 0:P], PT[:, par, 0:P], k.wo0[:, :], start=True, stop=True)
                        nc.tensor.matmul(k.ps[:, 4 + par, 0:P], PT[:, par, P:P + 1].to_broadcast([P, P]), k.wo0[:, :],
                                         start=True, stop=True).then_inc(m_ps, 1)
                    for g in range(4):
                        pe.wait_ge(m_ready, i * 2 + (g // 2 + 1))
                        for j in range(GC):
                            c = (g % 2) * GC + j
                            last = nc.tensor.matmul(k.ps[:, y_bank(g), j * P:(j + 1) * P],
                                                    nt.xT[:, g // 2, c * P:(c + 1) * P], M[:, g // 2, :],
                                                    start=True, stop=True)
                        last.then_inc(y_ps, 1)


def expert_choice_phase(nc, k):
    stack, sb, sem = phase_scope(nc)
    with stack:
        nt = NormTranspose(nc, k, "r_", sb, sem)
        aff = sb("aff", [P, NC, B * E0])
        z = sb("z", [P, 12, E0])
        ez = sb("ez", [P, 12, E0])
        zs = sb("zs", [P, 3, 12])
        AF = sb("AF", [P, 2, T])
        work = sb("work", [P, 2, T])
        top = sb("top", [P, 2, 8])
        G = sb("G", [P, 2, T])
        Gt = sb("Gt", [P, NC, B * E0])
        gb = sb("gb", [P, 2, TP])
        lg_ps, chain, expd = (sem(x) for x in ("lg_ps", "sm_chain", "sm_exp"))
        tk = [sem("topk0"), sem("topk1")]
        af_ps, af_ready, g_ready, gt_ps, gt_ready = (
            sem(x) for x in ("af_ps", "af_ready", "g_ready", "gt_ps", "gt_ready"))
        PER = 5

        with nc.Block() as block:
            @block.vector
            def _(dve):
                with dve.Fori(0, PAIRS) as i:
                    nt.vector(dve, i, k.h)
                    ps = k.ps[:, 4, 0:12 * E0].rearrange("p (m e) -> p m e", e=E0)
                    dve.wait_ge(lg_ps, i + 1)
                    nc.vector.tensor_reduce(zs[:, 0, :], ps, AX_X, ALU.max).then_inc(chain, 1)
                    dve.wait_ge(chain, i * PER + 1)
                    nc.vector.tensor_tensor(z[:], ps, zs[:, 0, :, None].to_broadcast([P, 12, E0]),
                                            ALU.subtract).then_inc(chain, 1)
                    dve.wait_ge(expd, i + 1)
                    nc.vector.tensor_reduce(zs[:, 1, :], ez[:], AX_X, ALU.add).then_inc(chain, 1)
                    dve.wait_ge(chain, i * PER + 3)
                    nc.vector.reciprocal(zs[:, 2, :], zs[:, 1, :]).then_inc(chain, 1)
                    dve.wait_ge(chain, i * PER + 4)
                    for par in range(2):
                        last = nc.vector.tensor_tensor(
                            aff[:, :, bass.ds(i * (2 * E0) + par * E0, E0)], ez[:, par * NC:(par + 1) * NC, :],
                            zs[:, 2, par * NC:(par + 1) * NC, None].to_broadcast([P, NC, E0]), ALU.mult)
                    last.then_inc(chain, 1)
                n = [0, 0]

                def chained(hf, ins):
                    n[hf] += 1
                    ins.then_inc(tk[hf], 1)

                rounds = (CAP + 7) // 8
                for r in range(rounds):
                    src = AF if r == 0 else work
                    for hf in range(2):
                        if r == 0:
                            dve.wait_ge(af_ready, hf + 1)
                        else:
                            dve.wait_ge(tk[hf], n[hf])
                        chained(hf, nc.vector.max(top[:, hf, :], src[:, hf, :]))
                    if r == rounds - 1 and CAP % 8:
                        for hf in range(2):
                            dve.wait_ge(tk[hf], n[hf])
                            chained(hf, nc.vector.memset(top[:, hf, CAP % 8:8], -1.0))
                    for hf in range(2):
                        dve.wait_ge(tk[hf], n[hf])
                        chained(hf, nc.vector.match_replace(work[:, hf, :], top[:, hf, :], src[:, hf, :], -1.0))
                for hf in range(2):
                    dve.wait_ge(tk[hf], n[hf])
                    nc.vector.scalar_tensor_tensor(out=G[:, hf, :], in0=work[:, hf, :], scalar=0.0,
                                                   in1=AF[:, hf, :], op0=ALU.is_lt, op1=ALU.mult).then_inc(g_ready, 1)

            @block.scalar
            def _(act):
                with act.Fori(0, PAIRS) as i:
                    nt.scalar(act, i)
                    act.wait_ge(chain, i * PER + 2)
                    nc.scalar.activation(ez[:], z[:], ACT.Exp).then_inc(expd, 1)
                for hf in range(2):
                    act.wait_ge(af_ps, hf + 1)
                    nc.scalar.activation(AF[:, hf, :], k.psf[:, hf * 1024:hf * 1024 + T], ACT.Copy).then_inc(af_ready, 1)
                for hf in range(2):
                    act.wait_ge(gt_ps, hf + 1)
                    o = 2048 + hf * 1024
                    nc.scalar.activation(Gt[:, 0:NC - 1, hf * P:(hf + 1) * P],
                                         k.psf[:, o:o + 5 * P].rearrange("p (c e) -> p c e", e=P), ACT.Copy)
                    nc.scalar.activation(Gt[0:LAST, NC - 1, hf * P:(hf + 1) * P],
                                         k.psf[0:LAST, o + 5 * P:o + 6 * P], ACT.Copy).then_inc(gt_ready, 1)
                act.wait_ge(gt_ready, 2)

            @block.tensor
            def _(pe):
                with pe.Fori(0, PAIRS) as i:
                    nt.tensor(pe, i)
                    pe.wait_ge(nt.moved, i * 4 + 4)
                    for m in range(12):
                        par, c = m // NC, m % NC
                        last = nc.tensor.matmul(k.ps[:, 4, m * E0:(m + 1) * E0], nt.xT[:, par, c * P:(c + 1) * P],
                                                k.gate0[:, :], start=True, stop=True)
                    last.then_inc(lg_ps, 1)
                pe.wait_ge(chain, PAIRS * PER)
                for hf in range(2):
                    for c in range(NC):
                        n = rows(c)
                        last = nc.tensor.transpose(k.psf[:, hf * 1024 + c * P:hf * 1024 + c * P + n],
                                                   aff[0:n, c, hf * P:(hf + 1) * P], k.ident[0:n, 0:n])
                    last.then_inc(af_ps, 1)
                for hf in range(2):
                    pe.wait_ge(g_ready, hf + 1)
                    for c in range(NC):
                        n = rows(c)
                        last = nc.tensor.transpose(k.psf[0:n, 2048 + hf * 1024 + c * P:2048 + hf * 1024 + (c + 1) * P],
                                                   G[:, hf, c * P:c * P + n], k.ident[:, :])
                    last.then_inc(gt_ps, 1)

        nt.base = 4 * PAIRS
        expert_block(nc, k, "e0_", sem, nt, gb, E0, 1, ACT.Gelu_apprx_tanh, k.w1_0, k.b1_0, k.w2_0,
                     lambda i, c, par, e, n: Gt[0:n, c, bass.ds(i * (2 * E0) + par * E0 + e, 1)])

        b2_ps, b2_added = sem("b2_ps"), sem("b2_added")
        with nc.Block() as block:
            @block.tensor
            def _(pe):
                for q in range(2 * NC):
                    hf, c = q // NC, q % NC
                    n = rows(c)
                    if q >= 4:
                        pe.wait_ge(b2_added, q - 3)
                    for s in range(2):
                        last = nc.tensor.matmul(k.ps[0:n, (q % 4) * 2 + s, :], G[:, hf, c * P:c * P + n],
                                                k.b2_0[:, s * 4:(s + 1) * 4, :].rearrange("p b d -> p (b d)"),
                                                start=True, stop=True)
                    last.then_inc(b2_ps, 1)

            @block.vector
            def _(dve):
                for q in range(2 * NC):
                    hf, c = q // NC, q % NC
                    n = rows(c)
                    dve.wait_ge(b2_ps, q + 1)
                    o = (q % 4) * 1024
                    hh = k.h[0:n, hf * 8:(hf + 1) * 8, c, :]
                    nc.vector.tensor_tensor(hh, hh, k.psf[0:n, o:o + 1024].rearrange("p (b d) -> p b d", d=C),
                                            ALU.add).then_inc(b2_added, 1)
                dve.wait_ge(b2_added, 2 * NC)


def expert_block(nc, k, tag, sem, nt, gb, experts, fh, func, w1, b1, w2, gate):
    h_ps, g_ready, o_ps, added = sem(tag + "h_ps"), sem(tag + "g_ready"), sem(tag + "o_ps"), sem(tag + "added")
    U = 2 * experts
    HP = 2 * fh
    nb = 4 // HP

    def piece(u, x):
        f, s = x // 2, x % 2
        return f, s * 384, NFREE[s], (u % nb) * HP + x

    with nc.Block() as block:
        @block.vector
        def _(dve):
            dve.sem_inc(added, 2)
            with dve.Fori(0, PAIRS) as i:
                nt.vector(dve, i, k.h)
                for u in range(U):
                    par, e = u // experts, u % experts
                    b = i * 2 + par
                    dve.wait_ge(o_ps, i * U + (u + 3))
                    if u % experts:
                        dve.wait_ge(added, i * U + (u + 2))
                    if u == 0:
                        dve.wait_ge(nt.normed, i * 4 + (nt.base + 4))
                    for c in range(NC):
                        n = rows(c)
                        last = nc.vector.scalar_tensor_tensor(
                            out=k.h[0:n, b, c, :], in0=k.psf[0:n, 2048 + (u % 2) * 1024 + c * P:2048 + (u % 2) * 1024 + (c + 1) * P],
                            scalar=gate(i, c, par, e, n), in1=k.h[0:n, b, c, :], op0=ALU.mult, op1=ALU.add)
                    last.then_inc(added, 1)

        @block.scalar
        def _(act):
            act.sem_inc(g_ready, 4)
            with act.Fori(0, PAIRS) as i:
                nt.scalar(act, i)
                for u in range(U):
                    e = u % experts
                    act.wait_ge(o_ps, i * U + (u + 1))
                    for x in range(HP):
                        f, c0, n, bank = piece(u, x)
                        act.wait_ge(h_ps, i * (U * HP) + (u * HP + x + 1))
                        out = gb[:, (u % 2) * fh + f, c0:c0 + n]
                        nc.scalar.activation(out, k.ps[:, bank, 0:n], func,
                                             bias=b1[:, e * fh + f:e * fh + f + 1]).then_inc(g_ready, 1)

        @block.tensor
        def _(pe):
            def hidden(i, u):
                par, e = u // experts, u % experts
                for x in range(HP):
                    f, c0, n, bank = piece(u, x)
                    pe.wait_ge(g_ready, i * (U * HP) + (u * HP + x + 1))
                    nc.tensor.matmul(k.ps[:, bank, 0:n], w1[:, e * fh + f, :], nt.xT[:, par, c0:c0 + n],
                                     start=True, stop=True).then_inc(h_ps, 1)

            def output(i, u):
                e = u % experts
                pe.wait_ge(g_ready, i * (U * HP) + ((u + 1) * HP + 4))
                pe.wait_ge(added, i * U + (u + 1))
                for c in range(NC):
                    n = rows(c)
                    o = 2048 + (u % 2) * 1024 + c * P
                    for f in range(fh):
                        last = nc.tensor.matmul(k.psf[0:n, o:o + P], gb[:, (u % 2) * fh + f, c * P:c * P + n],
                                                w2[:, e * fh + f, :], start=(f == 0), stop=(f == fh - 1))
                last.then_inc(o_ps, 1)

            pe.sem_inc(o_ps, 2)
            with pe.Fori(0, PAIRS) as i:
                nt.tensor(pe, i)
                pe.wait_ge(nt.moved, i * 4 + (nt.base + 4))
                for u in range(U):
                    hidden(i, u)
                    if u:
                        output(i, u - 1)
                output(i, U - 1)


def video_phase(nc, k):
    stack, sb, sem = phase_scope(nc)
    with stack:
        st = sb("vst", [P, NC, 6])
        mv = sb("vmv", [P, NC, 2])
        r1 = sb("vr1", [P, NC])
        r2 = sb("vr2", [P, NC])
        vx = sb("vx", [P, NC, C])
        vT = sb("vT", [P, NC * P])
        vD = sb("vD", [P, FR, 2, NV])
        stats, rooted, chain, normed = sem("v_stats"), sem("v_root"), sem("v_chain"), sem("v_normed")
        vt_ps, vt_ready, k_ps, v_ps, zero, laid, vd_ready = (
            sem(x) for x in ("vt_ps", "vt_ready", "vk_ps", "vv_ps", "v_zero", "v_laid", "vd_ready"))
        with nc.Block() as block:
            @block.gpsimd
            def _(pool):
                nc.gpsimd.memset(k.Kbd, 0.0).then_inc(zero, 1)
                nc.gpsimd.memset(k.Vbd, 0.0).then_inc(zero, 1)
                pool.wait_ge(vt_ready, 1)
                src = vT[:].rearrange("p (v a) -> p v a", a=NV)
                nc.gpsimd.tensor_copy(vD[:, :, 0, :], src)
                nc.gpsimd.tensor_copy(vD[:, :, 1, :], src).then_inc(vd_ready, 1)

            @block.vector
            def _(dve):
                for c in range(NC):
                    nc.vector.bn_stats(st[:, c, :], k.video[:, c, :]).then_inc(stats, 1)
                dve.wait_ge(stats, NC)
                for c in range(NC):
                    nc.vector.bn_aggr(mv[:, c, :], st[:, c, :]).then_inc(stats, 1)
                dve.wait_ge(rooted, 1)
                nc.vector.reciprocal(r2[:, :], r1[:, :]).then_inc(chain, 1)
                dve.wait_ge(chain, 1)
                for c in range(NC):
                    nc.vector.tensor_scalar(vx[:, c, :], k.video[:, c, :], mv[:, c, 0:1], r2[:, c:c + 1],
                                            ALU.subtract, ALU.mult).then_inc(normed, 1)
                dve.wait_ge(zero, 2)
                for s in range(2):
                    dve.wait_ge(k_ps, s + 1)
                    ps = k.ps[:, 2 + s, 0:GW].rearrange("p (v a) -> p v a", a=NV)
                    for hd in range(2):
                        q = slice(hd * 64, hd * 64 + 64)
                        nc.vector.tensor_scalar(k.Kbd[q, s * 6:(s + 1) * 6, q], ps[q, :, :], k.bk[q, 0:1], None, ALU.add)
                for s in range(3):
                    dve.wait_ge(v_ps, s + 1)
                    ps = k.ps[:, 4 + s, :].rearrange("p (v d) -> p v d", d=C)
                    for hd in range(2):
                        q = slice(hd * 64, hd * 64 + 64)
                        nc.vector.tensor_tensor(k.Vbd[q, s * 4:(s + 1) * 4, q], ps[q, :, q],
                                                k.bv[q, None, q].to_broadcast([64, 4, 64]), ALU.add).then_inc(laid, 1)
                dve.wait_ge(laid, 6)
                nc.vector.tensor_scalar(k.Vbd, k.Vbd, 1.0 / NV, None, ALU.mult).then_inc(laid, 1)
                dve.wait_ge(laid, 7)

            @block.scalar
            def _(act):
                act.wait_ge(stats, 2 * NC)
                nc.scalar.activation(r1[:, :], mv[:, :, 1], ACT.Sqrt, bias=k.eps[:, 0:1]).then_inc(rooted, 1)
                act.wait_ge(vt_ps, 1)
                nc.scalar.activation(vT[:, :], k.psf[:, 0:NC * P], ACT.Identity, scale=k.g1[:, 0:1],
                                     bias=k.b1n[:, 0:1]).then_inc(vt_ready, 1)

            @block.tensor
            def _(pe):
                for c in range(NC):
                    pe.wait_ge(normed, c + 1)
                    last = nc.tensor.transpose(k.psf[:, c * P:(c + 1) * P], vx[:, c, :], k.ident[:, :])
                last.then_inc(vt_ps, 1)
                pe.wait_ge(vt_ready, 1)
                for s in range(2):
                    nc.tensor.matmul(k.ps[:, 2 + s, 0:GW], k.wk[:, :], vT[:, s * GW:(s + 1) * GW],
                                     start=True, stop=True).then_inc(k_ps, 1)
                pe.wait_ge(vd_ready, 1)
                for v in range(FR):
                    last = nc.tensor.matmul(k.ps[:, 4 + v // 4, (v % 4) * C:(v % 4 + 1) * C],
                                            vD[:, v].rearrange("p h a -> p (h a)"), k.wv[:, :], start=True, stop=True)
                    if v % 4 == 3:
                        last.then_inc(v_ps, 1)


def attention_phase(nc, k):
    stack, sb, sem = phase_scope(nc)
    with stack:
        nt = NormTranspose(nc, k, "a_", sb, sem)
        qT = sb("qT", [P, 2, TP])
        nm = sb("nm", [P, 2, P], BF16)
        eb = sb("eb", [P, 3, FR, P])
        t1 = sb("t1", [P, 6, P])
        t2 = sb("t2", [P, 3, P])
        t3 = sb("t3", [P, P])
        den = sb("den", [P, 2, P])
        rd = sb("rd", [P, 2, P])
        aT = sb("aT", [P, 2, P])
        q_ps, q_ready, l_ps, m_ready, shifted, e_ready = (
            sem(x) for x in ("q_ps", "q_ready", "l_ps", "nm_ready", "shifted", "e_ready"))
        tree, summed, rd_ready, w_ready, a_ps, a_ready, o_ps, o_ready = (
            sem(x) for x in ("tree", "summed", "rd_ready", "aw_ready", "a_ps", "a_ready", "ao_ps", "ao_ready"))
        ST = 2 * NC

        def lbanks(j):
            o = 3 * (j % 2) * 512
            return k.psf[:, o:o + FR * P].rearrange("p (v t) -> p v t", t=P)

        with nc.Block() as block:
            @block.vector
            def _(dve):
                with dve.Fori(0, PAIRS) as i:
                    nt.vector(dve, i, k.h)
                    for g in range(4):
                        dve.wait_ge(q_ps, i * 4 + (g + 1))
                        nc.vector.tensor_scalar(qT[:, g // 2, (g % 2) * GW:(g % 2 + 1) * GW], k.ps[:, 4 + g, 0:GW],
                                                k.bq[:, 0:1], 0.125, ALU.add, ALU.mult).then_inc(q_ready, 1)
                    for j in range(ST + 3):
                        if j < ST:
                            dve.wait_ge(l_ps, i * ST + (j + 1))
                            nc.vector.tensor_reduce(nm[:, j % 2, :], lbanks(j).rearrange("p v t -> p t v"), AX_X,
                                                    ALU.max, negate=True).then_inc(m_ready, 1)
                        if 1 <= j <= ST:
                            w = j - 1
                            dve.wait_ge(summed, i * ST + (w + 1))
                            nc.vector.reciprocal(rd[:, w % 2, :], den[:, w % 2, :]).then_inc(rd_ready, 1)
                            dve.wait_ge(rd_ready, i * ST + (w + 1))
                            nc.vector.tensor_tensor(eb[:, w % 3], eb[:, w % 3],
                                                    rd[:, w % 2, None, :].to_broadcast([P, FR, P]),
                                                    ALU.mult).then_inc(w_ready, 1)
                        if j >= 3:
                            o = j - 3
                            dve.wait_ge(o_ps, i * ST + (o + 1))
                            nc.vector.tensor_tensor(k.big[:, i * 2 + o // NC, o % NC, :],
                                                    k.ps[:, 7, (o % 2) * P:(o % 2 + 1) * P], k.bo1[:, :],
                                                    ALU.add).then_inc(o_ready, 1)

            @block.scalar
            def _(act):
                with act.Fori(0, PAIRS) as i:
                    nt.scalar(act, i, k.g1[:, 0:1], k.b1n[:, 0:1])
                    for j in range(ST + 2):
                        if j >= 2:
                            a = j - 2
                            act.wait_ge(a_ps, i * ST + (a + 1))
                            nc.scalar.activation(aT[:, a % 2, :], k.ps[:, 6, (a % 2) * P:(a % 2 + 1) * P],
                                                 ACT.Copy).then_inc(a_ready, 1)
                        if j < ST:
                            act.wait_ge(shifted, i * ST + (j + 1))
                            nc.scalar.activation(eb[:, j % 3], lbanks(j), ACT.Exp).then_inc(e_ready, 1)

            @block.gpsimd
            def _(pool):
                with pool.Fori(0, PAIRS) as i:
                    for j in range(ST):
                        e = eb[:, j % 3]
                        pool.wait_ge(e_ready, i * ST + (j + 1))
                        nc.gpsimd.tensor_tensor(t1[:], e[:, 0:6], e[:, 6:12], ALU.add).then_inc(tree, 1)
                        pool.wait_ge(tree, i * (3 * ST) + (3 * j + 1))
                        nc.gpsimd.tensor_tensor(t2[:], t1[:, 0:3], t1[:, 3:6], ALU.add).then_inc(tree, 1)
                        pool.wait_ge(tree, i * (3 * ST) + (3 * j + 2))
                        nc.gpsimd.tensor_tensor(t3[:], t2[:, 0], t2[:, 1], ALU.add).then_inc(tree, 1)
                        pool.wait_ge(tree, i * (3 * ST) + (3 * j + 3))
                        nc.gpsimd.tensor_tensor(den[:, j % 2, :], t3[:], t2[:, 2], ALU.add).then_inc(summed, 1)

            @block.tensor
            def _(pe):
                with pe.Fori(0, PAIRS) as i:
                    nt.tensor(pe, i)
                    for g in range(4):
                        pe.wait_ge(nt.moved, i * 4 + (g + 1))
                        nc.tensor.matmul(k.ps[:, 4 + g, 0:GW], k.wq[:, :], nt.xT[:, g // 2, (g % 2) * GW:(g % 2 + 1) * GW],
                                         start=True, stop=True).then_inc(q_ps, 1)
                    pe.wait_ge(q_ready, i * 4 + 4)
                    for j in range(ST + 3):
                        if j < ST:
                            if j >= 2:
                                pe.wait_ge(e_ready, i * ST + (j - 1))
                            for v in range(FR):
                                last = nc.tensor.matmul(lbanks(j)[:, v, :], k.Kbd[:, v, :],
                                                        qT[:, j // NC, (j % NC) * P:(j % NC + 1) * P],
                                                        start=(v % 4 == 0), stop=True, skip_group_check=True)
                            last.then_inc(l_ps, 1)
                        if 2 <= j < ST + 2:
                            a = j - 2
                            pe.wait_ge(w_ready, i * ST + (a + 1))
                            if a:
                                pe.wait_ge(a_ready, i * ST + a)
                            for v in range(FR):
                                last = nc.tensor.matmul(k.ps[:, 6, (a % 2) * P:(a % 2 + 1) * P], k.Vbd[:, v, :],
                                                        eb[:, a % 3, v, :], start=(v == 0), stop=(v == FR - 1))
                            last.then_inc(a_ps, 1)
                        if j >= 3:
                            o = j - 3
                            pe.wait_ge(a_ready, i * ST + (o + 1))
                            if o:
                                pe.wait_ge(o_ready, i * ST + o)
                            nc.tensor.matmul(k.ps[:, 7, (o % 2) * P:(o % 2 + 1) * P], aT[:, o % 2, :], k.wo1[:, :],
                                             start=True, stop=True).then_inc(o_ps, 1)
                        if j < ST:
                            pe.wait_ge(m_ready, i * ST + (j + 1))
                            for s in range(3):
                                last = nc.tensor.matmul(
                                    lbanks(j)[:, s * 4:(s + 1) * 4, :], k.identb[:, :],
                                    nm[:, j % 2, None, :].to_broadcast([P, 4, P]), start=False, stop=True,
                                    skip_group_check=True)
                            last.then_inc(shifted, 1)


def attention_out_phase(nc, k):
    stack, sb, sem = phase_scope(nc)
    with stack:
        ol = sb("ol", [P, 4, GC, P])
        oT = sb("oT", [P, 4, GC, P])
        normed, scaled, ready, ot_ps, ot_ready, l_ps, z1, done = (
            sem(x) for x in ("on_normed", "on_scaled", "on_ready", "ot_ps", "ot_ready", "lin_ps", "z1", "z_done"))

        def bc(row):
            return row[:, None, :].to_broadcast([P, GC, P])

        with nc.Block() as block:
            @block.vector
            def _(dve):
                with dve.Fori(0, PAIRS) as i:
                    for g in range(4):
                        for j in range(GC):
                            at = i * (2 * NC) + g * GC + j
                            last = nc.vector.tensor_scalar(
                                ol[:, g, j, :], k.big[:, i * 2 + g // 2, (g % 2) * GC + j, :],
                                k.mean[:, bass.ds(at, 1)], k.rstd[:, bass.ds(at, 1)], ALU.subtract, ALU.mult)
                        last.then_inc(normed, 1)
                    for g in range(4):
                        b, c0 = i * 2 + g // 2, (g % 2) * GC
                        dve.wait_ge(l_ps, i * 4 + (g + 1))
                        dst = k.big[:, b, c0:c0 + GC, :]
                        nc.vector.tensor_tensor(dst, k.ps[:, 4 + g, 0:GW].rearrange("p (c t) -> p c t", t=P),
                                                ol[:, g], ALU.add).then_inc(z1, 1)
                        dve.wait_ge(z1, i * 4 + (g + 1))
                        nc.vector.tensor_tensor(dst, dst, bc(k.bl), ALU.add).then_inc(done, 1)

            @block.gpsimd
            def _(pool):
                with pool.Fori(0, PAIRS) as i:
                    for g in range(4):
                        pool.wait_ge(normed, i * 4 + (g + 1))
                        nc.gpsimd.tensor_tensor(ol[:, g], ol[:, g], bc(k.g2), ALU.mult).then_inc(scaled, 1)
                        pool.wait_ge(scaled, i * 4 + (g + 1))
                        nc.gpsimd.tensor_tensor(ol[:, g], ol[:, g], bc(k.b2n), ALU.add).then_inc(ready, 1)

            @block.tensor
            def _(pe):
                with pe.Fori(0, PAIRS) as i:
                    for g in range(4):
                        pe.wait_ge(ready, i * 4 + (g + 1))
                        for j in range(GC):
                            last = nc.tensor.transpose(k.ps[:, g, j * P:(j + 1) * P], ol[:, g, j, :], k.ident[:, :])
                        last.then_inc(ot_ps, 1)
                    for g in range(4):
                        pe.wait_ge(ot_ready, i * 4 + (g + 1))
                        for j in range(GC):
                            last = nc.tensor.matmul(k.ps[:, 4 + g, j * P:(j + 1) * P], oT[:, g, j, :], k.wl[:, :],
                                                    start=True, stop=True)
                        last.then_inc(l_ps, 1)

            @block.scalar
            def _(act):
                with act.Fori(0, PAIRS) as i:
                    for g in range(4):
                        act.wait_ge(ot_ps, i * 4 + (g + 1))
                        nc.scalar.activation(oT[:, g].rearrange("p c t -> p (c t)"), k.ps[:, g, 0:GW],
                                             ACT.Copy).then_inc(ot_ready, 1)


def attention_add_phase(nc, k):
    stack, sb, sem = phase_scope(nc)
    with stack:
        ol = sb("ol3", [P, 4, GC, P])
        normed, scaled, ready, added = (sem(x) for x in ("an_normed", "an_scaled", "an_ready", "an_added"))

        def bc(row):
            return row[:, None, :].to_broadcast([P, GC, P])

        with nc.Block() as block:
            @block.vector
            def _(dve):
                dve.sem_inc(added, 4)
                with dve.Fori(0, PAIRS) as i:
                    for g in range(4):
                        dve.wait_ge(added, i * 4 + (g + 1))
                        for j in range(GC):
                            at = i * (2 * NC) + g * GC + j
                            last = nc.vector.tensor_scalar(
                                ol[:, g, j, :], k.big[:, i * 2 + g // 2, (g % 2) * GC + j, :],
                                k.mean[:, bass.ds(at, 1)], k.rstd[:, bass.ds(at, 1)], ALU.subtract, ALU.mult)
                        last.then_inc(normed, 1)
                    for g in range(4):
                        b, c0 = i * 2 + g // 2, (g % 2) * GC
                        hh = k.h[:, b, c0:c0 + GC, :]
                        dve.wait_ge(ready, i * 4 + (g + 1))
                        nc.vector.tensor_tensor(hh, hh, ol[:, g], ALU.add).then_inc(added, 1)

            @block.gpsimd
            def _(pool):
                with pool.Fori(0, PAIRS) as i:
                    for g in range(4):
                        pool.wait_ge(normed, i * 4 + (g + 1))
                        nc.gpsimd.tensor_tensor(ol[:, g], ol[:, g], bc(k.g3), ALU.mult).then_inc(scaled, 1)
                        pool.wait_ge(scaled, i * 4 + (g + 1))
                        nc.gpsimd.tensor_tensor(ol[:, g], ol[:, g], bc(k.b3n), ALU.add).then_inc(ready, 1)


def token_choice_phase(nc, k):
    stack, sb, sem = phase_scope(nc)
    with stack:
        nt = NormTranspose(nc, k, "t_", sb, sem)
        lg = sb("lg", [P, NCH, E1])
        l2 = sb("l2", [P, NCH, E1])
        oh = sb("oh", [P, 2, NCH, E1])
        pr = sb("pr", [P, NCH, E1])
        mx = sb("mx", [P, 2, NCH])
        pm = sb("pm", [P, NCH])
        wt = sb("wt", [P, NC, B, E1])
        wT = sb("wT", [P, NC, P])
        rb = sb("rb", [P, 4, TP])
        lg_ps, biased, chain, expd, wt_ps, wt_ready = (
            sem(x) for x in ("tl_ps", "biased", "t_chain", "t_exp", "wt_ps", "wt_ready"))
        by_chunk = wt[:].rearrange("p c b e -> p b c e")
        WT_DONE = 17

        with nc.Block() as block:
            @block.vector
            def _(dve):
                with dve.Fori(0, PAIRS) as i:
                    nt.vector(dve, i, k.h)
                    dve.wait_ge(lg_ps, i + 1)
                    nc.vector.tensor_tensor(lg[:, bass.ds(i * 12, 12), :],
                                            k.ps[:, 4, 0:12 * E1].rearrange("p (m e) -> p m e", e=E1),
                                            k.gate_b[:, None, :].to_broadcast([P, 12, E1]), ALU.add).then_inc(biased, 1)
                dve.wait_ge(biased, PAIRS)
                n = [0]

                def link(ins):
                    n[0] += 1
                    ins.then_inc(chain, 1)
                    dve.wait_ge(chain, n[0])

                prio = k.prio[:, None, :].to_broadcast([P, NCH, E1])

                def wide(a):
                    return a[:, :, None].to_broadcast([P, NCH, E1])

                for q in range(2):
                    src = lg if q == 0 else l2
                    link(nc.vector.tensor_reduce(mx[:, q, :], src[:], AX_X, ALU.max))
                    link(nc.vector.tensor_tensor(pr[:], src[:], wide(mx[:, q, :]), ALU.is_equal))
                    link(nc.vector.tensor_tensor(pr[:], pr[:], prio, ALU.mult))
                    link(nc.vector.tensor_reduce(pm[:], pr[:], AX_X, ALU.max))
                    link(nc.vector.tensor_tensor(oh[:, q], prio, wide(pm[:, :]), ALU.is_equal))
                    if q == 0:
                        link(nc.vector.scalar_tensor_tensor(out=l2[:], in0=oh[:, 0], scalar=-3.0e38, in1=lg[:],
                                                            op0=ALU.mult, op1=ALU.add))
                link(nc.vector.tensor_tensor(pm[:], mx[:, 1, :], mx[:, 0, :], ALU.subtract))
                assert n[0] == 12
                dve.wait_ge(expd, 1)
                link(nc.vector.tensor_scalar(pm[:], mx[:, 0, :], 1.0, None, ALU.add))
                link(nc.vector.reciprocal(mx[:, 1, :], pm[:]))
                link(nc.vector.tensor_tensor(mx[:, 0, :], mx[:, 0, :], mx[:, 1, :], ALU.mult))
                link(nc.vector.tensor_tensor(l2[:], oh[:, 1], wide(mx[:, 0, :]), ALU.mult))
                link(nc.vector.tensor_tensor(pr[:], oh[:, 0], wide(mx[:, 1, :]), ALU.mult))
                nc.vector.tensor_tensor(by_chunk, l2[:].rearrange("p (b c) e -> p b c e", c=NC),
                                        pr[:].rearrange("p (b c) e -> p b c e", c=NC), ALU.add).then_inc(chain, 1)
                assert n[0] == WT_DONE

            @block.scalar
            def _(act):
                with act.Fori(0, PAIRS) as i:
                    nt.scalar(act, i)
                act.wait_ge(chain, 12)
                nc.scalar.activation(mx[:, 0, :], pm[:], ACT.Exp).then_inc(expd, 1)
                act.wait_ge(wt_ps, 1)
                nc.scalar.activation(wT[:].rearrange("p c t -> p (c t)"), k.psf[:, 0:NC * P], ACT.Copy).then_inc(wt_ready, 1)
                act.wait_ge(wt_ready, 1)

            @block.tensor
            def _(pe):
                with pe.Fori(0, PAIRS) as i:
                    nt.tensor(pe, i)
                    pe.wait_ge(nt.moved, i * 4 + 4)
                    for m in range(12):
                        last = nc.tensor.matmul(k.ps[:, 4, m * E1:(m + 1) * E1],
                                                nt.xT[:, m // NC, (m % NC) * P:(m % NC + 1) * P],
                                                k.gate1[:, :], start=True, stop=True)
                    last.then_inc(lg_ps, 1)
                pe.wait_ge(chain, WT_DONE + 1)
                for c in range(NC):
                    last = nc.tensor.transpose(k.psf[:, c * P:(c + 1) * P], wt[:, c].rearrange("p b e -> p (b e)"),
                                               k.ident[:, :])
                last.then_inc(wt_ps, 1)

        nt.base = 4 * PAIRS
        expert_block(nc, k, "e1_", sem, nt, rb, E1, 2, ACT.Relu, k.w1_1, k.b1_1, k.w2_1,
                     lambda i, c, par, e, n: by_chunk_flat(wt)[0:n, bass.ds(i * (2 * E1) + (c * B * E1 + par * E1 + e), 1)])

        b2_ps, b2_added, stored = sem("b2b_ps"), sem("b2b_added"), sem("stored")
        with nc.Block() as block:
            @block.tensor
            def _(pe):
                for c in range(NC):
                    n = rows(c)
                    for s in range(4):
                        q = c * 4 + s
                        if q >= 8:
                            pe.wait_ge(b2_added, q - 7)
                        nc.tensor.matmul(k.ps[0:n, q % 8, :], wT[:, c, 0:n],
                                         k.b2_1[:, s * 4:(s + 1) * 4, :].rearrange("p b d -> p (b d)"),
                                         start=True, stop=True).then_inc(b2_ps, 1)

            @block.vector
            def _(dve):
                for c in range(NC):
                    n = rows(c)
                    for s in range(4):
                        q = c * 4 + s
                        dve.wait_ge(b2_ps, q + 1)
                        hh = k.h[0:n, s * 4:(s + 1) * 4, c, :]
                        nc.vector.tensor_tensor(hh, hh, k.ps[0:n, q % 8, :].rearrange("p (b d) -> p b d", d=C),
                                                ALU.add).then_inc(b2_added, 1)

            @block.sync
            def _(sp):
                for c in range(NC):
                    sp.wait_ge(b2_added, 4 * (c + 1))
                    store_chunk(sp, k, c).then_inc(stored, 16)
                sp.wait_ge(stored, 16 * NC)


def by_chunk_flat(wt):
    return wt[:].rearrange("p c b e -> p (c b e)")


def store_chunk(sp, k, c):
    n = rows(c)
    return sp.dma_start(k.out[:, c * P:c * P + n, :].rearrange("b t d -> t b d"), k.h[0:n, :, c, :])


def audio_tower(nc, a, out):
    k = Ctx()
    with ExitStack() as ctx:
        def sb(name, shape, dt=F32):
            return ctx.enter_context(nc.sbuf_tensor(name, shape, dt))

        k.out = out
        k.xT = a["xT"]
        k.ps = ctx.enter_context(nc.psum_tensor("banks", [P, 8, 512], F32))[:]
        k.psf = k.ps.rearrange("p b n -> p (b n)")
        k.h = sb("h", [P, B, NC, C])
        k.mean = sb("mean", [P, NCH])
        k.rstd = sb("rstd", [P, NCH])
        k.eps = sb("eps", [P, 1])
        k.w_in = ctx.enter_context(nc.semaphore("w_in"))
        k.rest_in = ctx.enter_context(nc.semaphore("rest_in"))

        first, rest = [], []

        def load(name, shape, dram, group=rest, dt=F32):
            t = sb(name, shape, dt)
            group.append((t[:], dram))
            return t

        cw = a["L0_tok_WT"]
        k.wc01 = load("wc01", [P, C], cw[0:128, :], first)
        k.wc23 = load("wc23", [P, C], cw[128:256, :], first)
        k.wc4 = load("wc4", [64, C], cw[256:320, :], first)

        def col(name, src, group=rest):
            return load(name, [P, 1], a[src].rearrange("(p a) -> p a", a=1), group)

        def row(name, src, lo=0, n=C):
            return load(name, [P, n], a[src][lo:lo + n].partition_broadcast(P))

        k.conv_b = col("conv_b", "L0_tok_b", first)
        k.gamma = col("gamma", "L0_tok_gamma", first)
        k.beta = col("beta", "L0_tok_beta", first)
        k.ident = load("ident", [P, P], a["ident"], first)
        k.lmask = load("lmask", [P, NL + 1, P], a["lmask"])
        k.umask1 = load("umask1", [P, P], a["umask1"])
        k.upper = load("upper", [P, P], a["upper"])
        k.prio = load("prio", [P, E1], a["prio"].partition_broadcast(P))
        k.wkvl = sb("wkvl", [P, 2 * C + 1])
        rest.append((k.wkvl[:, 0:2 * C], a["L0_attn_WgT"][:, C:3 * C]))
        rest.append((k.wkvl[:, 2 * C:], a["L0_attn_WlrT"]))
        k.kvl_b = sb("kvl_b", [P, 2 * C + 1])
        rest.append((k.kvl_b[:, 0:2 * C], a["L0_attn_bg"][C:3 * C].partition_broadcast(P)))
        rest.append((k.kvl_b[:, 2 * C:], a["L0_attn_blr"].partition_broadcast(P)))
        k.wqb = sb("wqb", [P, C + 1])
        rest.append((k.wqb[:, 0:C], a["L0_attn_Wg"][0:C, :]))
        rest.append((k.wqb[:, C:], a["L0_attn_bg"][0:C].rearrange("(p a) -> p a", a=1)))
        k.wo0 = load("wo0", [P, C], a["L0_attn_WoT"])
        k.bo0 = row("bo0", "L0_attn_bo")
        k.gate0 = load("gate0", [P, E0], a["L0_ffn_gate_weight"])
        k.w1_0 = load("w1_0", [P, E0, P], a["L0_ffn_w1"].rearrange("e d f -> d e f"))
        k.w2_0 = load("w2_0", [P, E0, C], a["L0_ffn_w2"].rearrange("e f d -> f e d"))
        k.b1_0 = load("b1_0", [P, E0], a["L0_ffn_b1T"])
        k.b2_0 = sb("b2_0", [P, 8, C])
        k.b2_1 = sb("b2_1", [P, B, C])
        k.video = load("video", [P, NC, C], a["video"].rearrange("(c p) d -> p c d", p=P))
        k.wq = load("wq", [P, C], a["L1_attn_WqT"])
        k.wk = load("wk", [P, C], a["L1_attn_WkT"])
        k.wv = load("wv", [P, C], a["L1_attn_WvT"])
        k.wo1 = load("wo1", [P, C], a["L1_attn_WoT"])
        k.wl = load("wl", [P, C], a["L1_attn_WlT"])
        k.g1 = col("g1", "L1_attn_ln1_g")
        k.b1n = col("b1n", "L1_attn_ln1_b")
        k.bq = col("bq", "L1_attn_bq")
        k.bk = col("bk", "L1_attn_bk")
        k.bv = row("bv", "L1_attn_bv")
        k.bo1 = row("bo1", "L1_attn_bo")
        k.g2 = row("g2", "L1_attn_ln2_g")
        k.b2n = row("b2n", "L1_attn_ln2_b")
        k.bl = row("bl", "L1_attn_bl")
        k.g3 = row("g3", "L1_attn_ln3_g")
        k.b3n = row("b3n", "L1_attn_ln3_b")
        k.gate1 = load("gate1", [P, E1], a["L1_ffn_gate_w"])
        k.gate_b = row("gate_b", "L1_ffn_gate_b", 0, E1)
        k.w1_1 = load("w1_1", [P, 2 * E1, P], a["L1_ffn_w1T"])
        k.w2_1 = load("w2_1", [P, 2 * E1, C], a["L1_ffn_w2"].rearrange("e (f p) d -> p (e f) d", p=P))
        k.b1_1 = load("b1_1", [P, 2 * E1], a["L1_ffn_b1T"])
        k.first_loads, k.rest_loads = first, rest

        conv_phase(nc, k)
        k.identb = sb("identb", [P, P], BF16)
        setup_phase(nc, k, a, ctx)
        if DEBUG_STOP >= 1:
            norm_phase(nc, k, "n0", k.h)
            delta_phase(nc, k)
        if DEBUG_STOP >= 2:
            norm_phase(nc, k, "n1", k.h)
            expert_choice_phase(nc, k)
        if DEBUG_STOP >= 3:
            norm_phase(nc, k, "n2", k.h, twice=True)
            with ExitStack() as att:
                k.big = att.enter_context(nc.sbuf_tensor("o_all", [P, B, NC, C], F32))
                k.Kbd, k.Vbd = k.w1_0[:, 0:FR, :], k.w2_0[:, 0:FR, :]
                video_phase(nc, k)
                attention_phase(nc, k)
                norm_phase(nc, k, "n3", k.big)
                attention_out_phase(nc, k)
                norm_phase(nc, k, "n4", k.big)
                attention_add_phase(nc, k)
        if DEBUG_STOP >= 4:
            norm_phase(nc, k, "n5", k.h)
            token_choice_phase(nc, k)
        else:
            stored = ctx.enter_context(nc.semaphore("stored_dbg"))
            with nc.Block() as block:
                @block.sync
                def _(sp):
                    for c in range(NC):
                        store_chunk(sp, k, c).then_inc(stored, 16)
                    sp.wait_ge(stored, 16 * NC)


def setup_phase(nc, k, a, ctx):
    zeroed, b2_in = ctx.enter_context(nc.semaphore("b2_zeroed")), ctx.enter_context(nc.semaphore("b2_in"))
    with nc.Block() as block:
        @block.gpsimd
        def _(pool):
            nc.gpsimd.tensor_copy(k.identb[:, :], k.ident[:, :])
            nc.gpsimd.memset(k.b2_0[:], 0.0).then_inc(zeroed, 1)
            nc.gpsimd.memset(k.b2_1[:], 0.0).then_inc(zeroed, 1)

        @block.sync
        def _(sp):
            sp.wait_ge(zeroed, 2)
            for b in range(8):
                sp.dma_start(k.b2_0[b * E0:(b + 1) * E0, b, :], a["L0_ffn_b2"]).then_inc(b2_in, 16)
            for b in range(B):
                sp.dma_start(k.b2_1[b * E1:(b + 1) * E1, b, :], a["L1_ffn_b2"]).then_inc(b2_in, 16)
            sp.wait_ge(b2_in, 16 * (8 + B))


def shape_constants():
    t = np.arange(P)
    masks = []
    for s in (1,) + LEVELS:
        same = (t[:, None] // (2 * s)) == (t[None, :] // (2 * s))
        masks.append((same & (t[:, None] % (2 * s) >= s) & (t[None, :] % (2 * s) < s)).astype(np.float32))
    lmask = np.ascontiguousarray(np.stack(masks, axis=1))
    return {
        "ident": np.eye(P, dtype=np.float32),
        "lmask": lmask,
        "umask1": np.ascontiguousarray(masks[0].T),
        "upper": np.triu(np.ones((P, P), np.float32), 1),
        "prio": np.arange(E1, 0, -1).astype(np.float32),
    }


def kernel(**inputs):
    import concourse.bacc as bacc
    from concourse.bass_utils import run_bass_kernel_spmd

    x = {n: np.asarray(v) for n, v in inputs.items()}
    lay = {
        "xT": x["x"].transpose(2, 0, 1),
        "L0_tok_WT": x["L0_tok_W"].T,
        "L0_attn_WgT": x["L0_attn_Wg"].T,
        "L0_attn_WlrT": x["L0_attn_Wlr"].T,
        "L0_attn_WoT": x["L0_attn_Wo"].T,
        "L0_ffn_b1T": x["L0_ffn_b1"].T,
        "video": x["L1_attn_video_embeds"].transpose(1, 0, 2).reshape(FR * NV, C),
        "L1_attn_WqT": x["L1_attn_Wq"].T,
        "L1_attn_WkT": x["L1_attn_Wk"].T,
        "L1_attn_WvT": x["L1_attn_Wv"].T,
        "L1_attn_WoT": x["L1_attn_Wo"].T,
        "L1_attn_WlT": x["L1_attn_Wl"].T,
        "L1_ffn_w1T": x["L1_ffn_w1"].transpose(1, 0, 2).reshape(C, 2 * E1, P),
        "L1_ffn_b1T": x["L1_ffn_b1"].reshape(2 * E1, P).T,
    }
    for name in ("L0_tok_b", "L0_tok_gamma", "L0_tok_beta", "L0_attn_bg", "L0_attn_blr", "L0_attn_Wg", "L0_attn_bo",
                 "L0_ffn_gate_weight", "L0_ffn_w1", "L0_ffn_w2", "L0_ffn_b2", "L1_attn_ln1_g", "L1_attn_ln1_b",
                 "L1_attn_bq", "L1_attn_bk", "L1_attn_bv", "L1_attn_bo", "L1_attn_bl", "L1_attn_ln2_g",
                 "L1_attn_ln2_b", "L1_attn_ln3_g", "L1_attn_ln3_b", "L1_ffn_gate_w", "L1_ffn_gate_b", "L1_ffn_w2",
                 "L1_ffn_b2"):
        lay[name] = x[name]
    lay.update(shape_constants())
    lay = {n: np.ascontiguousarray(v) for n, v in lay.items()}

    nc = bacc.Bacc("TRN2", target_bir_lowering=False, num_devices=1)
    aps = {n: nc.dram_tensor(f"in_{n}", v.shape, mybir.dt.from_np(v.dtype), kind="ExternalInput").ap()
           for n, v in lay.items()}
    out = nc.dram_tensor("out", (B, T, C), F32, kind="ExternalOutput").ap()
    audio_tower(nc, aps, out)
    r = run_bass_kernel_spmd(nc, [{f"in_{n}": v for n, v in lay.items()}], core_ids=[0])
    return r.results[0]["out"]
```

```python
from contextlib import ExitStack

import numpy as np

import concourse.bass as bass
from concourse import mybir

ALU = mybir.AluOpType
ACT = mybir.ActivationFunctionType
F32 = mybir.dt.float32
BF16 = mybir.dt.bfloat16
AX_X = mybir.AxisListType.X

P = 128
B = 16
T_IN = 750
CTX = 5
T = T_IN - CTX + 1
C = 128
NC = 6
LAST = T - (NC - 1) * P
TP = NC * P
NCH = B * NC
PAIRS = B // 2
HALF_T = T // 2
GC = 3
GW = GC * P
LEVELS = (2, 4, 8, 16, 32, 64)
NL = len(LEVELS)
E0 = 16
CAP = T // E0 * 2
E1 = 8
NV = 64
FR = 12
NFREE = (384, T - 384)
EPS = 1e-5
DEBUG_STOP = 99


def rows(c):
    return P if c < NC - 1 else LAST


class Ctx:
    pass


def phase_scope(nc):
    stack = ExitStack()

    def sb(name, shape, dt=F32):
        return stack.enter_context(nc.sbuf_tensor(name, shape, dt))

    def sem(name):
        return stack.enter_context(nc.semaphore(name))

    return stack, sb, sem


def conv_phase(nc, k):
    stack, sb, sem = phase_scope(nc)
    with stack:
        yT = sb("yT", [P, B, T])
        yn = sb("yn", [P, 2, TP])
        bst = sb("bst", [P, 2 * B, 6])
        bmv = sb("bmv", [P, 2])
        bsc = sb("bsc", [P, 4])
        xw = k.h[:].rearrange("p b c d -> p (b c d)")[:, 0:B * T_IN].rearrange("p (b t) -> p b t", t=T_IN)
        x_in = [sem(f"x_in{q}") for q in range(4)]
        w_in, rest_in = k.w_in, k.rest_in
        conv_ps, conv_relu, stats = sem("conv_ps"), sem("conv_relu"), sem("conv_stats")
        bn_chain, bn_sqrt = sem("bn_chain"), sem("bn_sqrt")
        yn_ready, tr_ps, h_stored, pads = sem("yn_ready"), sem("tr_ps"), sem("h_stored"), sem("pads")
        qb = B // 4

        with nc.Block() as block:
            @block.sync
            def _(sp):
                for ap, dram in k.first_loads:
                    sp.dma_start(ap, dram).then_inc(w_in, 16)
                for q in range(4):
                    s = slice(q * qb, (q + 1) * qb)
                    sp.dma_start(xw[0:64, s, :], k.xT[:, s, :]).then_inc(x_in[q], 16)
                    sp.dma_start(xw[64:128, s, 0:T_IN - 1], k.xT[:, s, 1:T_IN]).then_inc(x_in[q], 16)
                for ap, dram in k.rest_loads:
                    sp.dma_start(ap, dram).then_inc(rest_in, 16)

            @block.tensor
            def _(pe):
                pe.wait_ge(w_in, 16 * len(k.first_loads))
                for q in range(4):
                    pe.wait_ge(x_in[q], 32)
                    with pe.Fori(q * qb // 2, (q + 1) * qb // 2) as i:
                        for par in range(2):
                            b = i * 2 + par
                            for half in range(2):
                                pe.wait_ge(conv_relu, i * 4 + (par * 2 + half + 1))
                                ps = k.ps[:, par * 2 + half, 0:HALF_T]
                                t0 = half * HALF_T
                                nc.tensor.matmul(ps, k.wc01[:, :], xw[:, b, t0:t0 + HALF_T], start=True, stop=False)
                                nc.tensor.matmul(ps, k.wc23[:, :], xw[:, b, t0 + 2:t0 + 2 + HALF_T],
                                                 start=False, stop=False)
                                nc.tensor.matmul(ps, k.wc4[:, :], xw[0:64, b, t0 + 4:t0 + 4 + HALF_T],
                                                 start=False, stop=True).then_inc(conv_ps, 1)

            @block.scalar
            def _(act):
                act.wait_ge(w_in, 16 * len(k.first_loads))
                act.sem_inc(conv_relu, 4)
                with act.Fori(0, PAIRS) as i:
                    for par in range(2):
                        b = i * 2 + par
                        for half in range(2):
                            act.wait_ge(conv_ps, i * 4 + (par * 2 + half + 1))
                            nc.scalar.activation(yT[:, b, half * HALF_T:(half + 1) * HALF_T],
                                                 k.ps[:, par * 2 + half, 0:HALF_T], ACT.Relu,
                                                 bias=k.conv_b[:, 0:1]).then_inc(conv_relu, 1)
                act.wait_ge(bn_chain, 1)
                nc.scalar.activation(bsc[:, 0:1], bmv[:, 1:2], ACT.Sqrt, bias=k.eps[:, 0:1]).then_inc(bn_sqrt, 1)

            @block.vector
            def _(dve):
                nc.vector.memset(k.eps[:], EPS)
                with dve.Fori(0, PAIRS) as i:
                    for par in range(2):
                        b = i * 2 + par
                        for half in range(2):
                            dve.wait_ge(conv_relu, i * 4 + (par * 2 + half + 5))
                            nc.vector.bn_stats(bst[:, i * 4 + (par * 2 + half), :],
                                               yT[:, b, half * HALF_T:(half + 1) * HALF_T]).then_inc(stats, 1)
                dve.wait_ge(stats, 2 * B)
                nc.vector.bn_aggr(bmv[:, :], bst[:].rearrange("p a s -> p (a s)")).then_inc(bn_chain, 1)
                dve.wait_ge(bn_sqrt, 1)
                nc.vector.reciprocal(bsc[:, 1:2], bsc[:, 0:1]).then_inc(bn_chain, 1)
                dve.wait_ge(bn_chain, 2)
                nc.vector.tensor_tensor(bsc[:, 2:3], bsc[:, 1:2], k.gamma[:, 0:1], ALU.mult).then_inc(bn_chain, 1)
                dve.wait_ge(bn_chain, 3)
                nc.vector.tensor_tensor(bsc[:, 0:1], bmv[:, 0:1], bsc[:, 2:3], ALU.mult).then_inc(bn_chain, 1)
                dve.wait_ge(bn_chain, 4)
                nc.vector.tensor_tensor(bsc[:, 3:4], k.beta[:, 0:1], bsc[:, 0:1], ALU.subtract).then_inc(bn_chain, 1)
                dve.wait_ge(bn_chain, 5)

        with nc.Block() as block:
            @block.sync
            def _(sp):
                sp.wait_ge(rest_in, 16 * len(k.rest_loads))

            @block.gpsimd
            def _(pool):
                nc.gpsimd.memset(k.h[96:128, :, NC - 1, :], 0.0).then_inc(pads, 1)

            @block.vector
            def _(dve):
                with dve.Fori(0, PAIRS) as i:
                    for par in range(2):
                        b = i * 2 + par
                        dve.wait_ge(tr_ps, i * 2 + (par + 1))
                        nc.vector.tensor_scalar(yn[:, par, 0:T], yT[:, b, :], bsc[:, 2:3], bsc[:, 3:4],
                                                ALU.mult, ALU.add).then_inc(yn_ready, 1)

            @block.tensor
            def _(pe):
                pe.sem_inc(tr_ps, 2)
                with pe.Fori(0, PAIRS) as i:
                    for par in range(2):
                        pe.wait_ge(yn_ready, i * 2 + (par + 1))
                        pe.wait_ge(h_stored, i * 2 + (par + 1))
                        for c in range(NC):
                            n = rows(c)
                            last = nc.tensor.transpose(k.psf[0:n, par * 1024 + c * P:par * 1024 + (c + 1) * P],
                                                       yn[:, par, c * P:c * P + n], k.ident[:, :])
                        last.then_inc(tr_ps, 1)

            @block.scalar
            def _(act):
                act.sem_inc(h_stored, 2)
                act.wait_ge(pads, 1)
                with act.Fori(0, PAIRS) as i:
                    for par in range(2):
                        b = i * 2 + par
                        act.wait_ge(tr_ps, i * 2 + (par + 3))
                        o = par * 1024
                        nc.scalar.activation(k.h[:, b, 0:NC - 1, :],
                                             k.psf[:, o:o + 5 * P].rearrange("p (c d) -> p c d", d=P), ACT.Copy)
                        nc.scalar.activation(k.h[0:LAST, b, NC - 1, :],
                                             k.psf[0:LAST, o + 5 * P:o + 6 * P], ACT.Copy).then_inc(h_stored, 1)


def norm_phase(nc, k, tag, src, twice=False, counted=False):
    stack, sb, sem = phase_scope(nc)
    with stack:
        st = k.st
        tmp = sb(tag + "tmp", [P, 4, NCH])
        seen, chain, rooted = k.norm_seen, k.norm_chain, k.norm_rooted
        seen0, chain0, rooted0 = k.norm_past
        k.norm_past = (seen0 + (0 if counted else B), chain0 + (12 if twice else 8), rooted0 + (2 if twice else 1))
        with nc.Block() as block:
            @block.vector
            def _(dve):
                if not counted:
                    with dve.Fori(0, B) as b:
                        for c in range(NC):
                            last = nc.vector.bn_stats(st[:, b * NC + c, :], src[:, b, c, :])
                        last.then_inc(seen, 1)
                    dve.wait_ge(seen, seen0 + B)
                n = [0]

                def link(ins):
                    n[0] += 1
                    ins.then_inc(chain, 1)
                    dve.wait_ge(chain, chain0 + n[0])

                me, ve, mo, vo = (st[:, :, q] for q in (1, 2, 4, 5))
                link(nc.vector.tensor_tensor(tmp[:, 0, :], me, mo, ALU.add))
                link(nc.vector.tensor_tensor(tmp[:, 1, :], me, mo, ALU.subtract))
                link(nc.vector.tensor_tensor(tmp[:, 2, :], ve, vo, ALU.add))
                link(nc.vector.tensor_scalar(k.mean[:, :], tmp[:, 0, :], 0.5, None, ALU.mult))
                link(nc.vector.tensor_tensor(tmp[:, 3, :], tmp[:, 1, :], tmp[:, 1, :], ALU.mult))
                link(nc.vector.tensor_scalar(tmp[:, 0, :], tmp[:, 2, :], 1.0 / C, None, ALU.mult))
                link(nc.vector.scalar_tensor_tensor(out=tmp[:, 1, :], in0=tmp[:, 3, :], scalar=0.25,
                                                    in1=tmp[:, 0, :], op0=ALU.mult, op1=ALU.add))
                var_at = n[0]
                dve.wait_ge(rooted, rooted0 + 1)
                link(nc.vector.reciprocal(k.rstd[:, :], tmp[:, 2, :]))
                if twice:
                    link(nc.vector.tensor_tensor(tmp[:, 0, :], k.rstd[:, :], k.rstd[:, :], ALU.mult))
                    link(nc.vector.tensor_tensor(tmp[:, 3, :], tmp[:, 0, :], tmp[:, 1, :], ALU.mult))
                    dve.wait_ge(rooted, rooted0 + 2)
                    link(nc.vector.reciprocal(tmp[:, 0, :], tmp[:, 2, :]))
                    link(nc.vector.tensor_tensor(k.rstd[:, :], k.rstd[:, :], tmp[:, 0, :], ALU.mult))
                assert var_at == 7 and chain0 + n[0] == k.norm_past[1]

            @block.scalar
            def _(act):
                act.wait_ge(chain, chain0 + 7)
                nc.scalar.activation(tmp[:, 2, :], tmp[:, 1, :], ACT.Sqrt, bias=k.eps[:, 0:1]).then_inc(rooted, 1)
                if twice:
                    act.wait_ge(chain, chain0 + 10)
                    nc.scalar.activation(tmp[:, 2, :], tmp[:, 3, :], ACT.Sqrt, bias=k.eps[:, 0:1]).then_inc(rooted, 1)


def over_pairs(eng, body):
    with eng.Fori(0, PAIRS - 1) as i:
        body(i, False)
    body(PAIRS - 1, True)


class NormTranspose:

    def __init__(self, nc, k, tag, sb, sem):
        self.nc, self.k = nc, k
        self.xl = sb(tag + "xl", [P, 4, GC, P])
        self.xT = sb(tag + "xT", [P, 2, TP])
        self.normed, self.turned, self.moved = sem(tag + "normed"), sem(tag + "turned"), sem(tag + "moved")

    def norm(self, i, g, src):
        for j in range(GC):
            c = (g % 2) * GC + j
            at = i * (2 * NC) + ((g // 2) * NC + c)
            last = self.nc.vector.tensor_scalar(
                self.xl[:, g, j, :], src[:, i * 2 + g // 2, c, :], self.k.mean[:, bass.ds(at, 1)],
                self.k.rstd[:, bass.ds(at, 1)], ALU.subtract, ALU.mult)
        last.then_inc(self.normed, 1)

    def vector(self, dve, i, src):
        for g in range(4):
            self.norm(i, g, src)

    def next_pair(self, dve, i, src):
        for g in range(4):
            dve.wait_ge(self.turned, i * 4 + (g + 1))
            self.norm(i + 1, g, src)

    def turn(self, pe, i, g, bank):
        pe.wait_ge(self.normed, i * 4 + (g + 1))
        for j in range(GC):
            last = self.nc.tensor.transpose(self.k.ps[:, bank, j * P:(j + 1) * P], self.xl[:, g, j, :],
                                            self.k.ident[:, :])
        last.then_inc(self.turned, 1)

    def tensor(self, pe, i):
        for g in range(4):
            self.turn(pe, i, g, g)

    def move(self, act, i, g, bank, scale=None, bias=None):
        act.wait_ge(self.turned, i * 4 + (g + 1))
        out = self.xT[:, g // 2, (g % 2) * GW:(g % 2 + 1) * GW]
        if scale is None:
            ins = self.nc.scalar.activation(out, self.k.ps[:, bank, 0:GW], ACT.Copy)
        else:
            ins = self.nc.scalar.activation(out, self.k.ps[:, bank, 0:GW], ACT.Identity, scale=scale, bias=bias)
        ins.then_inc(self.moved, 1)

    def scalar(self, act, i):
        for g in range(4):
            self.move(act, i, g, g)


def delta_phase(nc, k):
    stack, sb, sem = phase_scope(nc)
    with stack:
        nt = NormTranspose(nc, k, "d_", sb, sem)
        kvl = sb("kvl", [P, 12, 2 * C + 1])
        junk = sb("junk", [P, 12, C])
        nk = sb("nk", [P, 12])
        nks = sb("nks", [P, 12])
        rk = sb("rk", [P, 12])
        kh = sb("kh", [P, 12, P])
        kT = sb("kT", [P, 12, P])
        NT = sb("NT", [P, 4, GC, P])
        D = sb("D", [P, 4, GC, P])
        DT = sb("DT", [P, 4, GC, P])
        W = sb("W", [P, 4, GC, P])
        R = sb("R", [P, 2, P])
        UU = sb("UU", [P, 2, 2 * P])
        S = sb("S", [P, 2, P])
        kvs = sb("kvs", [P, 2, P])
        PT = sb("PT", [P, 2, P + 1])
        M = sb("M", [P, 2, P])
        bb = sb("bb", [P, 2, P])
        kv_ps, kv_ready, squared, rooted, rk_ready = (sem(x) for x in ("kv_ps", "kv_ready", "k_sq", "k_root", "rk_ready"))
        kh_ready, kT_ps, kT_ready, gram_ps, nt_ready = (sem(x) for x in ("kh_ready", "kT_ps", "kT_ready", "gram_ps", "nt_ready"))
        m0, dt0, d0_ps, d0 = (sem(x) for x in ("m0", "dt0", "d0_ps", "d0"))
        w_ps, w_ready, x_ps, d_ready, t_ps, dt_ready = (sem(x) for x in ("w_ps", "w_ready", "x_ps", "d_ready", "t_ps", "dt_ready"))
        r_ps, r_ready, u_ps, u_ready, sk_ps, s_ready = (
            sem(x) for x in ("r_ps", "r_ready", "u_ps", "u_ready", "sk_ps", "s_ready"))
        kvs_ready, pt_ps, pt_ready, m_ps, m_ready, bb_ready, y_ps, hb_ready, h_ready = (
            sem(x) for x in ("kvs_ready", "pt_ps", "pt_ready", "m_ps", "m_ready", "bb_ready", "y_ps", "hb_ready", "dh_ready"))
        zeroed = sem("rk_zeroed")

        def kv_bank(m):
            return (4 + m) % 8

        def y_bank(g):
            return (2, 3, 6, 7)[g]

        def bc(row, n):
            return row[:, None, :].to_broadcast([P, n, P])

        with nc.Block() as block:
            @block.vector
            def _(dve):
                nc.vector.memset(rk[:], 0.0).then_inc(zeroed, 1)
                dve.wait_ge(zeroed, 1)
                with dve.Fori(0, PAIRS) as i:
                    nt.vector(dve, i, k.h)
                    for m in range(12):
                        dve.wait_ge(kv_ps, i * 12 + (m + 1))
                        nc.vector.tensor_tensor(kvl[:, m, :], k.ps[:, kv_bank(m), 0:2 * C + 1], k.kvl_b[:, :],
                                                ALU.add).then_inc(kv_ready, 1)
                    dve.wait_ge(rooted, i + 1)
                    rk2 = rk[:].rearrange("p (s c) -> p s c", c=NC)
                    nks2 = nks[:].rearrange("p (s c) -> p s c", c=NC)
                    nc.vector.reciprocal(rk2[:, :, 0:NC - 1], nks2[:, :, 0:NC - 1])
                    nc.vector.reciprocal(rk2[0:LAST, :, NC - 1], nks2[0:LAST, :, NC - 1]).then_inc(rk_ready, 1)
                    for g in range(4):
                        dve.wait_ge(gram_ps, i * 4 + (g + 1))
                        nc.vector.tensor_tensor(NT[:, g], k.ps[:, 4 + g, 0:GW].rearrange("p (c t) -> p c t", t=P),
                                                bc(k.upper, GC), ALU.mult).then_inc(nt_ready, 1)
                    for lv in range(NL):
                        for g in range(4):
                            dve.wait_ge(w_ps, i * (4 * NL) + (lv * 4 + g + 1))
                            nc.vector.tensor_tensor(W[:, g], k.ps[:, 4 + g, 0:GW].rearrange("p (c t) -> p c t", t=P),
                                                    bc(k.lmask[:, lv + 1, :], GC), ALU.mult).then_inc(w_ready, 1)
                        for g in range(4):
                            dve.wait_ge(x_ps, i * (4 * NL) + (lv * 4 + g + 1))
                            nc.vector.tensor_tensor(D[:, g], D[:, g],
                                                    k.ps[:, g, 0:GW].rearrange("p (c t) -> p c t", t=P),
                                                    ALU.subtract).then_inc(d_ready, 1)
                    for c in range(NC):
                        for par in range(2):
                            m = par * NC + c
                            if c:
                                dve.wait_ge(r_ps, i * 10 + ((c - 1) * 2 + par + 1))
                                nc.vector.tensor_tensor(R[:, par, :], kvl[:, m, C:2 * C], k.ps[:, par, 0:P],
                                                        ALU.subtract).then_inc(r_ready, 1)
                        for par in range(2):
                            m = par * NC + c
                            dve.wait_ge(u_ps, i * 12 + (c * 2 + par + 1))
                            nc.vector.tensor_scalar(UU[:, par, P:2 * P], k.ps[:, 2 + par, 0:P],
                                                    kvl[:, m, 2 * C:2 * C + 1], None, ALU.mult)
                            nc.vector.tensor_copy(UU[:, par, 0:P], k.ps[:, 2 + par, 0:P]).then_inc(u_ready, 1)
                    for par in range(2):
                        dve.wait_ge(m_ps, i * 2 + (par + 1))
                        nc.vector.tensor_tensor(bb[:, par, :], k.ps[:, 4 + par, 0:P], k.bo0[:, :],
                                                ALU.add).then_inc(bb_ready, 1)
                    for g in range(4):
                        b, c0 = i * 2 + g // 2, (g % 2) * GC
                        dve.wait_ge(y_ps, i * 4 + (g + 1))
                        dve.wait_ge(hb_ready, i * 4 + (g + 1))
                        nc.vector.tensor_tensor(k.h[:, b, c0:c0 + GC, :], k.h[:, b, c0:c0 + GC, :],
                                                k.ps[:, y_bank(g), 0:GW].rearrange("p (c t) -> p c t", t=P),
                                                ALU.add).then_inc(h_ready, 1)

            @block.gpsimd
            def _(pool):
                with pool.Fori(0, PAIRS) as i:
                    for g in range(4):
                        m0_ = (g // 2) * NC + (g % 2) * GC
                        if g == 0:
                            pool.wait_ge(rk_ready, i + 1)
                        nc.gpsimd.tensor_tensor(kh[:, m0_:m0_ + GC, :], kvl[:, m0_:m0_ + GC, 0:C],
                                                rk[:, m0_:m0_ + GC, None].to_broadcast([P, GC, P]),
                                                ALU.mult).then_inc(kh_ready, 1)
                    for g in range(4):
                        pool.wait_ge(nt_ready, i * 4 + (g + 1))
                        nc.gpsimd.tensor_tensor(W[:, g], NT[:, g], bc(k.umask1, GC), ALU.mult).then_inc(m0, 1)
                        pool.wait_ge(m0, i * 4 + (g + 1))
                        nc.gpsimd.tensor_tensor(DT[:, g], bc(k.ident, GC), W[:, g], ALU.subtract).then_inc(dt0, 1)
                    for g in range(4):
                        b, c0 = i * 2 + g // 2, (g % 2) * GC
                        pool.wait_ge(bb_ready, i * 2 + (g // 2 + 1))
                        nc.gpsimd.tensor_tensor(k.h[:, b, c0:c0 + GC, :], k.h[:, b, c0:c0 + GC, :],
                                                bb[:, g // 2, None, :].to_broadcast([P, GC, P]),
                                                ALU.add).then_inc(hb_ready, 1)

            @block.scalar
            def _(act):
                with act.Fori(0, PAIRS) as i:
                    nt.scalar(act, i)
                    for m in range(12):
                        act.wait_ge(kv_ready, i * 12 + (m + 1))
                        nc.scalar.activation(junk[:, m, :], kvl[:, m, 0:C], ACT.Square,
                                             accum_out=nk[:, m:m + 1]).then_inc(squared, 1)
                    act.wait_ge(squared, i * 12 + 12)
                    nc.scalar.activation(nks[:, :], nk[:, :], ACT.Sqrt).then_inc(rooted, 1)
                    for g in range(4):
                        act.wait_ge(kT_ps, i * 4 + (g + 1))
                        m = (g // 2) * NC + (g % 2) * GC
                        nc.scalar.activation(kT[:, m:m + GC, :].rearrange("p c t -> p (c t)"), k.ps[:, g, 0:GW],
                                             ACT.Copy).then_inc(kT_ready, 1)
                    for g in range(4):
                        act.wait_ge(d0_ps, i * 4 + (g + 1))
                        nc.scalar.activation(D[:, g].rearrange("p c t -> p (c t)"), k.ps[:, g, 0:GW],
                                             ACT.Copy).then_inc(d0, 1)
                    for lv in range(NL):
                        for g in range(4):
                            act.wait_ge(t_ps, i * (4 * NL) + (lv * 4 + g + 1))
                            nc.scalar.activation(DT[:, g].rearrange("p c t -> p (c t)"), k.ps[:, 4 + g, 0:GW],
                                                 ACT.Copy).then_inc(dt_ready, 1)
                    for c in range(NC):
                        for par in range(2):
                            act.wait_ge(sk_ps, i * 12 + (c * 2 + par + 1))
                            if c < NC - 1:
                                nc.scalar.activation(S[:, par, :], k.ps[:, 4 + par, 0:P], ACT.Copy).then_inc(s_ready, 1)
                            else:
                                nc.scalar.activation(kvs[:, par, :], k.ps[:, 4 + par, P:2 * P],
                                                     ACT.Copy).then_inc(kvs_ready, 1)
                    for par in range(2):
                        act.wait_ge(pt_ps, i * 2 + (par + 1))
                        nc.scalar.activation(PT[:, par, :], k.ps[:, 6 + par, 0:P + 1], ACT.Copy).then_inc(pt_ready, 1)
                    for par in range(2):
                        act.wait_ge(m_ps, i * 2 + (par + 1))
                        nc.scalar.activation(M[:, par, :], k.ps[:, par, 0:P], ACT.Copy).then_inc(m_ready, 1)

            @block.tensor
            def _(pe):
                with pe.Fori(0, PAIRS) as i:
                    nt.tensor(pe, i)
                    for m in range(12):
                        pe.wait_ge(nt.moved, i * 4 + (min(m // GC, 3) + 1 if m < 4 else 4))
                        if m >= 8:
                            pe.wait_ge(kv_ready, i * 12 + (m - 7))
                        par, c = m // NC, m % NC
                        nc.tensor.matmul(k.ps[:, kv_bank(m), 0:2 * C + 1], nt.xT[:, par, c * P:(c + 1) * P],
                                         k.wkvl[:, :], start=True, stop=True).then_inc(kv_ps, 1)
                    for g in range(4):
                        pe.wait_ge(kh_ready, i * 4 + (g + 1))
                        for j in range(GC):
                            m = (g // 2) * NC + (g % 2) * GC + j
                            last = nc.tensor.transpose(k.ps[:, g, j * P:(j + 1) * P], kh[:, m, :], k.ident[:, :])
                        last.then_inc(kT_ps, 1)
                    for g in range(4):
                        pe.wait_ge(kT_ready, i * 4 + (g + 1))
                        for j in range(GC):
                            m = (g // 2) * NC + (g % 2) * GC + j
                            last = nc.tensor.matmul(k.ps[:, 4 + g, j * P:(j + 1) * P], kT[:, m, :], kT[:, m, :],
                                                    start=True, stop=True)
                        last.then_inc(gram_ps, 1)
                    for g in range(4):
                        pe.wait_ge(dt0, i * 4 + (g + 1))
                        for j in range(GC):
                            last = nc.tensor.transpose(k.ps[:, g, j * P:(j + 1) * P], DT[:, g, j, :], k.ident[:, :])
                        last.then_inc(d0_ps, 1)
                    for lv in range(NL):
                        for g in range(4):
                            if lv == 0:
                                pe.wait_ge(d0, i * 4 + (g + 1))
                            else:
                                pe.wait_ge(dt_ready, i * (4 * NL) + ((lv - 1) * 4 + g + 1))
                            for j in range(GC):
                                last = nc.tensor.matmul(k.ps[:, 4 + g, j * P:(j + 1) * P], NT[:, g, j, :],
                                                        D[:, g, j, :], start=True, stop=True)
                            last.then_inc(w_ps, 1)
                        for g in range(4):
                            pe.wait_ge(w_ready, i * (4 * NL) + (lv * 4 + g + 1))
                            for j in range(GC):
                                last = nc.tensor.matmul(k.ps[:, g, j * P:(j + 1) * P], DT[:, g, j, :],
                                                        W[:, g, j, :], start=True, stop=True)
                            last.then_inc(x_ps, 1)
                        for g in range(4):
                            pe.wait_ge(d_ready, i * (4 * NL) + (lv * 4 + g + 1))
                            for j in range(GC):
                                last = nc.tensor.transpose(k.ps[:, 4 + g, j * P:(j + 1) * P], D[:, g, j, :],
                                                           k.ident[:, :])
                            last.then_inc(t_ps, 1)
                    for c in range(NC):
                        n = rows(c)
                        if c:
                            for par in range(2):
                                pe.wait_ge(s_ready, i * 10 + ((c - 1) * 2 + par + 1))
                                nc.tensor.matmul(k.ps[:, par, 0:P], kT[:, par * NC + c, :], S[:, par, :],
                                                 start=True, stop=True).then_inc(r_ps, 1)
                        for par in range(2):
                            g = par * 2 + c // GC
                            if c == 0:
                                pe.wait_ge(dt_ready, i * (4 * NL) + 4 * NL)
                                rhs = kvl[:, par * NC, C:2 * C]
                            else:
                                pe.wait_ge(r_ready, i * 10 + ((c - 1) * 2 + par + 1))
                                rhs = R[:, par, :]
                            nc.tensor.matmul(k.ps[:, 2 + par, 0:P], DT[:, g, c % GC, :], rhs,
                                             start=True, stop=True).then_inc(u_ps, 1)
                        for par in range(2):
                            pe.wait_ge(u_ready, i * 12 + (c * 2 + par + 1))
                            nc.tensor.matmul(k.ps[:, 4 + par, 0:2 * P], kh[0:n, par * NC + c, :], UU[0:n, par, :],
                                             start=(c == 0), stop=True, skip_group_check=True).then_inc(sk_ps, 1)
                    for par in range(2):
                        pe.wait_ge(kvs_ready, i * 2 + (par + 1))
                        nc.tensor.matmul(k.ps[:, 6 + par, 0:P + 1], kvs[:, par, :], k.wqb[:, :],
                                         start=True, stop=True).then_inc(pt_ps, 1)
                    for par in range(2):
                        pe.wait_ge(pt_ready, i * 2 + (par + 1))
                        nc.tensor.matmul(k.ps[:, par, 0:P], PT[:, par, 0:P], k.wo0[:, :], start=True, stop=True)
                        nc.tensor.matmul(k.ps[:, 4 + par, 0:P], PT[:, par, P:P + 1].to_broadcast([P, P]), k.wo0[:, :],
                                         start=True, stop=True).then_inc(m_ps, 1)
                    for g in range(4):
                        pe.wait_ge(m_ready, i * 2 + (g // 2 + 1))
                        for j in range(GC):
                            c = (g % 2) * GC + j
                            last = nc.tensor.matmul(k.ps[:, y_bank(g), j * P:(j + 1) * P],
                                                    nt.xT[:, g // 2, c * P:(c + 1) * P], M[:, g // 2, :],
                                                    start=True, stop=True)
                        last.then_inc(y_ps, 1)


def expert_choice_phase(nc, k):
    stack, sb, sem = phase_scope(nc)
    with stack:
        nt = NormTranspose(nc, k, "r_", sb, sem)
        aff = sb("aff", [P, NC, B * E0])
        z = sb("z", [P, 12, E0])
        ez = sb("ez", [P, 12, E0])
        zs = sb("zs", [P, 3, 12])
        AF = sb("AF", [P, 2, T])
        work = sb("work", [P, 2, T])
        top = sb("top", [P, 2, 8])
        G = sb("G", [P, 2, T])
        Gt = sb("Gt", [P, NC, B * E0])
        gb = sb("gb", [P, 2, TP])
        lg_ps, lg_free, chain, expd = (sem(x) for x in ("lg_ps", "lg_free", "sm_chain", "sm_exp"))
        tk = [sem("topk0"), sem("topk1")]
        af_ps, af_ready, g_ready, gt_ps, gt_ready = (
            sem(x) for x in ("af_ps", "af_ready", "g_ready", "gt_ps", "gt_ready"))
        PER = 5

        with nc.Block() as block:
            @block.vector
            def _(dve):
                def body(i, last_pair):
                    if not last_pair:
                        nt.next_pair(dve, i, k.h)
                    ps = k.ps[:, 4, 0:12 * E0].rearrange("p (m e) -> p m e", e=E0)
                    dve.wait_ge(lg_ps, i + 1)
                    nc.vector.tensor_reduce(zs[:, 0, :], ps, AX_X, ALU.max).then_inc(chain, 1)
                    dve.wait_ge(chain, i * PER + 1)
                    nc.vector.tensor_tensor(z[:], ps, zs[:, 0, :, None].to_broadcast([P, 12, E0]),
                                            ALU.subtract).then_inc(chain, 1)
                    dve.wait_ge(expd, i + 1)
                    nc.vector.tensor_reduce(zs[:, 1, :], ez[:], AX_X, ALU.add).then_inc(chain, 1)
                    dve.wait_ge(chain, i * PER + 3)
                    dve.sem_inc(lg_free, 1)
                    nc.vector.reciprocal(zs[:, 2, :], zs[:, 1, :]).then_inc(chain, 1)
                    dve.wait_ge(chain, i * PER + 4)
                    for par in range(2):
                        last = nc.vector.tensor_tensor(
                            aff[:, :, bass.ds(i * (2 * E0) + par * E0, E0)], ez[:, par * NC:(par + 1) * NC, :],
                            zs[:, 2, par * NC:(par + 1) * NC, None].to_broadcast([P, NC, E0]), ALU.mult)
                    last.then_inc(chain, 1)

                dve.sem_inc(lg_free, 1)
                nt.vector(dve, 0, k.h)
                over_pairs(dve, body)
                n = [0, 0]

                def chained(hf, ins):
                    n[hf] += 1
                    ins.then_inc(tk[hf], 1)

                rounds = (CAP + 7) // 8
                for r in range(rounds):
                    src = AF if r == 0 else work
                    for hf in range(2):
                        if r == 0:
                            dve.wait_ge(af_ready, hf + 1)
                        else:
                            dve.wait_ge(tk[hf], n[hf])
                        chained(hf, nc.vector.max(top[:, hf, :], src[:, hf, :]))
                    if r == rounds - 1 and CAP % 8:
                        for hf in range(2):
                            dve.wait_ge(tk[hf], n[hf])
                            chained(hf, nc.vector.memset(top[:, hf, CAP % 8:8], -1.0))
                    for hf in range(2):
                        dve.wait_ge(tk[hf], n[hf])
                        chained(hf, nc.vector.match_replace(work[:, hf, :], top[:, hf, :], src[:, hf, :], -1.0))
                for hf in range(2):
                    dve.wait_ge(tk[hf], n[hf])
                    nc.vector.scalar_tensor_tensor(out=G[:, hf, :], in0=work[:, hf, :], scalar=0.0,
                                                   in1=AF[:, hf, :], op0=ALU.is_lt, op1=ALU.mult).then_inc(g_ready, 1)

            @block.scalar
            def _(act):
                with act.Fori(0, PAIRS) as i:
                    nt.scalar(act, i)
                    act.wait_ge(chain, i * PER + 2)
                    nc.scalar.activation(ez[:], z[:], ACT.Exp).then_inc(expd, 1)
                for hf in range(2):
                    act.wait_ge(af_ps, hf + 1)
                    nc.scalar.activation(AF[:, hf, :], k.psf[:, hf * 1024:hf * 1024 + T], ACT.Copy).then_inc(af_ready, 1)
                for hf in range(2):
                    act.wait_ge(gt_ps, hf + 1)
                    o = 2048 + hf * 1024
                    nc.scalar.activation(Gt[:, 0:NC - 1, hf * P:(hf + 1) * P],
                                         k.psf[:, o:o + 5 * P].rearrange("p (c e) -> p c e", e=P), ACT.Copy)
                    nc.scalar.activation(Gt[0:LAST, NC - 1, hf * P:(hf + 1) * P],
                                         k.psf[0:LAST, o + 5 * P:o + 6 * P], ACT.Copy).then_inc(gt_ready, 1)
                act.wait_ge(gt_ready, 2)

            @block.tensor
            def _(pe):
                with pe.Fori(0, PAIRS) as i:
                    nt.tensor(pe, i)
                    pe.wait_ge(nt.moved, i * 4 + 4)
                    pe.wait_ge(lg_free, i + 1)
                    for m in range(12):
                        par, c = m // NC, m % NC
                        last = nc.tensor.matmul(k.ps[:, 4, m * E0:(m + 1) * E0], nt.xT[:, par, c * P:(c + 1) * P],
                                                k.gate0[:, :], start=True, stop=True)
                    last.then_inc(lg_ps, 1)
                pe.wait_ge(chain, PAIRS * PER)
                for hf in range(2):
                    for c in range(NC):
                        n = rows(c)
                        last = nc.tensor.transpose(k.psf[:, hf * 1024 + c * P:hf * 1024 + c * P + n],
                                                   aff[0:n, c, hf * P:(hf + 1) * P], k.ident[0:n, 0:n])
                    last.then_inc(af_ps, 1)
                for hf in range(2):
                    pe.wait_ge(g_ready, hf + 1)
                    for c in range(NC):
                        n = rows(c)
                        last = nc.tensor.transpose(k.psf[0:n, 2048 + hf * 1024 + c * P:2048 + hf * 1024 + (c + 1) * P],
                                                   G[:, hf, c * P:c * P + n], k.ident[:, :])
                    last.then_inc(gt_ps, 1)

        expert_block(nc, k, "e0_", sb, sem, nt, gb, E0, 1, ACT.Gelu_apprx_tanh, k.w1_0, k.b1_0, k.w2_0,
                     lambda i, c, par, e, n: Gt[0:n, c, bass.ds(i * (2 * E0) + par * E0 + e, 1)])

        b2_ps, b2_added = sem("b2_ps"), sem("b2_added")
        with nc.Block() as block:
            @block.tensor
            def _(pe):
                for q in range(2 * NC):
                    hf, c = q // NC, q % NC
                    n = rows(c)
                    if q >= 4:
                        pe.wait_ge(b2_added, q - 3)
                    for s in range(2):
                        last = nc.tensor.matmul(k.ps[0:n, (q % 4) * 2 + s, :], G[:, hf, c * P:c * P + n],
                                                k.b2_0[:, s * 4:(s + 1) * 4, :].rearrange("p b d -> p (b d)"),
                                                start=True, stop=True)
                    last.then_inc(b2_ps, 1)

            @block.vector
            def _(dve):
                for q in range(2 * NC):
                    hf, c = q // NC, q % NC
                    n = rows(c)
                    dve.wait_ge(b2_ps, q + 1)
                    o = (q % 4) * 1024
                    hh = k.h[0:n, hf * 8:(hf + 1) * 8, c, :]
                    nc.vector.tensor_tensor(hh, hh, k.psf[0:n, o:o + 1024].rearrange("p (b d) -> p b d", d=C),
                                            ALU.add).then_inc(b2_added, 1)
                dve.wait_ge(b2_added, 2 * NC)


def expert_block(nc, k, tag, sb, sem, nt, gb, experts, fh, func, w1, b1, w2, gate):
    F32R = mybir.dt.float32r
    w1h = sb(tag + "w1h", [P, experts * fh, P], F32R)
    w1l = sb(tag + "w1l", [P, experts * fh, P], F32R)
    xh = sb(tag + "xh", [P, 4, GW], F32R)
    xlo = sb(tag + "xlo", [P, 4, GW], F32R)
    w_split, normed, full, free = sem(tag + "w_split"), sem(tag + "normed"), sem(tag + "full"), sem(tag + "free")
    split, o_ps, added = sem(tag + "split"), sem(tag + "o_ps"), sem(tag + "added")
    U = 2 * experts
    HP = 2 * fh
    PIECES = U * HP + 4
    slots = {2: 2, 3: 3, experts + 2: 0, experts + 3: 1}

    def pieces(last):
        out, n = [], 2
        for u in range(U):
            if u in slots and not (last and slots[u] < 2):
                out.append((n, "turn", slots[u], u))
                n += 1
            for x in range(HP):
                out.append((n, "hidden", u, x))
                n += 1
        assert last or n == PIECES + 2
        return out

    def at(i, n):
        return i * PIECES + n

    with nc.Block() as block:
        @block.vector
        def _(dve):
            dve.sem_inc(added, 2)

            def norm(i, g):
                for j in range(GC):
                    c = (g % 2) * GC + j
                    col = i * (2 * NC) + ((g // 2) * NC + c)
                    last = nc.vector.tensor_scalar(
                        nt.xl[:, g, j, :], k.h[:, i * 2 + g // 2, c, :], k.mean[:, bass.ds(col, 1)],
                        k.rstd[:, bass.ds(col, 1)], ALU.subtract, ALU.mult)
                last.then_inc(normed, 1)

            def body(i, last_pair):
                for g in (2, 3):
                    norm(i, g)
                for u in range(U):
                    par, e = u // experts, u % experts
                    b = i * 2 + par
                    if u == experts and not last_pair:
                        for g in (0, 1):
                            norm(i + 1, g)
                    dve.wait_ge(o_ps, i * U + (u + 3))
                    if u % experts:
                        dve.wait_ge(added, i * U + (u + 2))
                    else:
                        dve.wait_ge(normed, i * 4 + (par * 2 + 2))
                    for c in range(NC):
                        n = rows(c)
                        o = 2048 + (u % 2) * 1024 + c * P
                        last = nc.vector.scalar_tensor_tensor(
                            out=k.h[0:n, b, c, :], in0=k.psf[0:n, o:o + P],
                            scalar=gate(i, c, par, e, n), in1=k.h[0:n, b, c, :], op0=ALU.mult, op1=ALU.add)
                    last.then_inc(added, 1)

            norm(0, 0)
            norm(0, 1)
            over_pairs(dve, body)
            dve.wait_ge(added, PAIRS * U + 2)

        @block.gpsimd
        def _(pool):
            nc.gpsimd.tensor_copy(w1h[:], w1[:]).then_inc(w_split, 1)
            pool.wait_ge(w_split, 1)
            nc.gpsimd.tensor_tensor(w1l[:], w1[:], w1h[:].bitcast(F32), ALU.subtract).then_inc(w_split, 1)

            def halve(i, g, count):
                x = nt.xT[:, g // 2, (g % 2) * GW:(g % 2 + 1) * GW]
                pool.wait_ge(free, count)
                nc.gpsimd.tensor_tensor(xlo[:, g], x, xh[:, g].bitcast(F32), ALU.subtract).then_inc(split, 1)

            halve(0, 0, 1 + 4)
            halve(0, 1, 2 + 4)

            def body(i, last_pair):
                for n, kind, g, _ in pieces(last_pair):
                    if kind == "turn":
                        halve(i if g >= 2 else i + 1, g, at(i, n + 1 + 4))

            over_pairs(pool, body)

        @block.scalar
        def _(act):
            act.sem_inc(free, 4)

            def move(g, bank):
                nc.scalar.activation(nt.xT[:, g // 2, (g % 2) * GW:(g % 2 + 1) * GW], k.ps[:, bank, 0:GW], ACT.Copy)
                nc.scalar.activation(xh[:, g], k.ps[:, bank, 0:GW], ACT.Copy).then_inc(free, 1)

            for g in range(2):
                act.wait_ge(full, g + 1)
                move(g, g)

            def body(i, last_pair):
                for n, kind, q, x in pieces(last_pair):
                    act.wait_ge(full, at(i, n + 1))
                    if kind == "turn":
                        move(q, n % 4)
                        continue
                    u, e = q, q % experts
                    if x == 0:
                        act.wait_ge(o_ps, i * U + (u + 1))
                    f, s = x // 2, x % 2
                    nc.scalar.activation(gb[:, (u % 2) * fh + f, s * 384:s * 384 + NFREE[s]],
                                         k.ps[:, n % 4, 0:NFREE[s]], func,
                                         bias=b1[:, e * fh + f:e * fh + f + 1]).then_inc(free, 1)

            over_pairs(act, body)

        @block.tensor
        def _(pe):
            def turn(i, g, bank):
                pe.wait_ge(normed, i * 4 + (g + 1))
                for j in range(GC):
                    last = nc.tensor.transpose(k.ps[:, bank, j * P:(j + 1) * P], nt.xl[:, g, j, :], k.ident[:, :])
                last.then_inc(full, 1)

            def output(i, u, count):
                e = u % experts
                pe.wait_ge(free, count)
                pe.wait_ge(added, i * U + (u + 1))
                for c in range(NC):
                    n = rows(c)
                    o = 2048 + (u % 2) * 1024 + c * P
                    for f in range(fh):
                        last = nc.tensor.matmul(k.psf[0:n, o:o + P], gb[:, (u % 2) * fh + f, c * P:c * P + n],
                                                w2[:, e * fh + f, :], start=(f == 0), stop=(f == fh - 1))
                last.then_inc(o_ps, 1)

            def body(i, last_pair):
                done = {}
                for n, kind, q, x in pieces(last_pair):
                    pe.wait_ge(free, at(i, n + 1))
                    if kind == "turn":
                        turn(i if q >= 2 else i + 1, q, n % 4)
                        continue
                    u, e, par = q, q % experts, q // experts
                    f, s = x // 2, x % 2
                    g, w = par * 2 + s, NFREE[s]
                    if e == 0 and f == 0:
                        pe.wait_ge(split, i * 4 + (g + 1))
                    ps = k.ps[:, n % 4, 0:w]
                    nc.tensor.matmul(ps, w1h[:, e * fh + f, :], xh[:, g, 0:w], start=True, stop=False)
                    nc.tensor.matmul(ps, w1h[:, e * fh + f, :], xlo[:, g, 0:w], start=False, stop=False)
                    nc.tensor.matmul(ps, w1l[:, e * fh + f, :], xh[:, g, 0:w],
                                     start=False, stop=True).then_inc(full, 1)
                    done[u] = n + 1 + 4
                    if x == HP - 1 and u:
                        output(i, u - 1, at(i, done[u - 1]))
                output(i, U - 1, at(i, done[U - 1]))

            pe.sem_inc(o_ps, 2)
            turn(0, 0, 0)
            turn(0, 1, 1)
            pe.wait_ge(w_split, 2)
            over_pairs(pe, body)


def video_phase(nc, k):
    stack, sb, sem = phase_scope(nc)
    with stack:
        st = sb("vst", [P, NC, 6])
        mv = sb("vmv", [P, NC, 2])
        r1 = sb("vr1", [P, NC])
        r2 = sb("vr2", [P, NC])
        vx = sb("vx", [P, NC, C])
        vT = sb("vT", [P, NC * P])
        vD = sb("vD", [P, FR, 2, NV])
        stats, rooted, chain, normed = sem("v_stats"), sem("v_root"), sem("v_chain"), sem("v_normed")
        vt_ps, vt_ready, k_ps, v_ps, zero, laid, vd_ready = (
            sem(x) for x in ("vt_ps", "vt_ready", "vk_ps", "vv_ps", "v_zero", "v_laid", "vd_ready"))
        with nc.Block() as block:
            @block.gpsimd
            def _(pool):
                nc.gpsimd.memset(k.Kbd, 0.0).then_inc(zero, 1)
                nc.gpsimd.memset(k.Vbd, 0.0).then_inc(zero, 1)
                pool.wait_ge(vt_ready, 1)
                src = vT[:].rearrange("p (v a) -> p v a", a=NV)
                nc.gpsimd.tensor_copy(vD[:, :, 0, :], src)
                nc.gpsimd.tensor_copy(vD[:, :, 1, :], src).then_inc(vd_ready, 1)

            @block.vector
            def _(dve):
                for c in range(NC):
                    nc.vector.bn_stats(st[:, c, :], k.video[:, c, :]).then_inc(stats, 1)
                dve.wait_ge(stats, NC)
                for c in range(NC):
                    nc.vector.bn_aggr(mv[:, c, :], st[:, c, :]).then_inc(stats, 1)
                dve.wait_ge(rooted, 1)
                nc.vector.reciprocal(r2[:, :], r1[:, :]).then_inc(chain, 1)
                dve.wait_ge(chain, 1)
                for c in range(NC):
                    nc.vector.tensor_scalar(vx[:, c, :], k.video[:, c, :], mv[:, c, 0:1], r2[:, c:c + 1],
                                            ALU.subtract, ALU.mult).then_inc(normed, 1)
                dve.wait_ge(zero, 2)
                for s in range(2):
                    dve.wait_ge(k_ps, s + 1)
                    ps = k.ps[:, 2 + s, 0:GW].rearrange("p (v a) -> p v a", a=NV)
                    for hd in range(2):
                        q = slice(hd * 64, hd * 64 + 64)
                        nc.vector.tensor_scalar(k.Kbd[q, s * 6:(s + 1) * 6, q], ps[q, :, :], k.bk[q, 0:1], None, ALU.add)
                for s in range(3):
                    dve.wait_ge(v_ps, s + 1)
                    ps = k.ps[:, 4 + s, :].rearrange("p (v d) -> p v d", d=C)
                    for hd in range(2):
                        q = slice(hd * 64, hd * 64 + 64)
                        nc.vector.tensor_tensor(k.Vbd[q, s * 4:(s + 1) * 4, q], ps[q, :, q],
                                                k.bv[q, None, q].to_broadcast([64, 4, 64]), ALU.add).then_inc(laid, 1)
                dve.wait_ge(laid, 6)
                nc.vector.tensor_scalar(k.Vbd, k.Vbd, 1.0 / NV, None, ALU.mult).then_inc(laid, 1)
                dve.wait_ge(laid, 7)

            @block.scalar
            def _(act):
                act.wait_ge(stats, 2 * NC)
                nc.scalar.activation(r1[:, :], mv[:, :, 1], ACT.Sqrt, bias=k.eps[:, 0:1]).then_inc(rooted, 1)
                act.wait_ge(vt_ps, 1)
                nc.scalar.activation(vT[:, :], k.psf[:, 0:NC * P], ACT.Identity, scale=k.g1[:, 0:1],
                                     bias=k.b1n[:, 0:1]).then_inc(vt_ready, 1)

            @block.tensor
            def _(pe):
                for c in range(NC):
                    pe.wait_ge(normed, c + 1)
                    last = nc.tensor.transpose(k.psf[:, c * P:(c + 1) * P], vx[:, c, :], k.ident[:, :])
                last.then_inc(vt_ps, 1)
                pe.wait_ge(vt_ready, 1)
                for s in range(2):
                    nc.tensor.matmul(k.ps[:, 2 + s, 0:GW], k.wk[:, :], vT[:, s * GW:(s + 1) * GW],
                                     start=True, stop=True).then_inc(k_ps, 1)
                pe.wait_ge(vd_ready, 1)
                for v in range(FR):
                    last = nc.tensor.matmul(k.ps[:, 4 + v // 4, (v % 4) * C:(v % 4 + 1) * C],
                                            vD[:, v].rearrange("p h a -> p (h a)"), k.wv[:, :], start=True, stop=True)
                    if v % 4 == 3:
                        last.then_inc(v_ps, 1)


def attention_phase(nc, k):
    stack, sb, sem = phase_scope(nc)
    with stack:
        nt = NormTranspose(nc, k, "a_", sb, sem)
        qT = sb("qT", [P, 2, TP])
        nm = sb("nm", [P, 2, P], BF16)
        eb = sb("eb", [P, 3, FR, P])
        t1 = sb("t1", [P, 6, P])
        t2 = sb("t2", [P, 3, P])
        t3 = sb("t3", [P, P])
        den = sb("den", [P, 2, P])
        rd = sb("rd", [P, 2, P])
        aT = sb("aT", [P, 2, P])
        q_ps, q_ready, l_ps, m_ready, shifted, e_ready = (
            sem(x) for x in ("q_ps", "q_ready", "l_ps", "nm_ready", "shifted", "e_ready"))
        tree, summed, rd_ready, w_ready, a_ps, a_ready, o_ps, o_ready = (
            sem(x) for x in ("tree", "summed", "rd_ready", "aw_ready", "a_ps", "a_ready", "ao_ps", "ao_ready"))
        counted = sem("ao_counted")
        ST = 2 * NC
        slots = {1: 2, 3: 3, NC + 1: 0, NC + 3: 1}
        big = k.big[:].rearrange("p b c d -> p (b c) d")

        def lbanks(j):
            o = 3 * (j % 2) * 512
            return k.psf[:, o:o + FR * P].rearrange("p (v t) -> p v t", t=P)

        def slot(i, j, last_pair):
            g = slots.get(j)
            if g is None or (g < 2 and last_pair):
                return None
            return (i, g) if g >= 2 else (i + 1, g)

        def over_steps(eng, step):
            for j in range(ST):
                step(0, j, j, False)
            with eng.Fori(1, PAIRS - 1) as i:
                for j in range(ST):
                    step(i, j, ST, False)
            for j in range(ST + 3):
                step(PAIRS - 1, j, ST, True)

        with nc.Block() as block:
            @block.vector
            def _(dve):
                def query(i, g, bank):
                    dve.wait_ge(q_ps, i * 4 + (g + 1))
                    nc.vector.tensor_scalar(qT[:, g // 2, (g % 2) * GW:(g % 2 + 1) * GW], k.ps[:, bank, 0:GW],
                                            k.bq[:, 0:1], 0.125, ALU.add, ALU.mult).then_inc(q_ready, 1)

                def step(i, j, past, last_pair):
                    if j < ST:
                        dve.wait_ge(l_ps, i * ST + (j + 1))
                        nc.vector.tensor_reduce(nm[:, j % 2, :], lbanks(j).rearrange("p v t -> p t v"), AX_X,
                                                ALU.max, negate=True).then_inc(m_ready, 1)
                    before = slot(i, j - 1, last_pair)
                    if before:
                        query(before[0], before[1], 7)
                    nxt = slot(i, j + 1, last_pair)
                    if nxt:
                        nt.norm(nxt[0], nxt[1], k.h)
                    if past >= 1 and j <= ST:
                        w = j - 1
                        dve.wait_ge(summed, i * ST + (w + 1))
                        nc.vector.reciprocal(rd[:, w % 2, :], den[:, w % 2, :]).then_inc(rd_ready, 1)
                        dve.wait_ge(rd_ready, i * ST + (w + 1))
                        nc.vector.tensor_tensor(eb[:, w % 3], eb[:, w % 3],
                                                rd[:, w % 2, None, :].to_broadcast([P, FR, P]),
                                                ALU.mult).then_inc(w_ready, 1)
                    if past >= 3:
                        dve.wait_ge(o_ps, i * ST + (j - 3 + 1))
                        nc.vector.tensor_tensor(big[:, i * ST + (j - 3), :], k.ps[:, 7, 0:P], k.bo1[:, :],
                                                ALU.add).then_inc(o_ready, 1)
                    if past >= 4:
                        dve.wait_ge(o_ready, i * ST + (j - 4 + 1))
                        nc.vector.bn_stats(k.st[:, i * ST + (j - 4), :], big[:, i * ST + (j - 4), :]).then_inc(counted, 1)

                for g in range(2):
                    nt.norm(0, g, k.h)
                for g in range(2):
                    query(0, g, 4 + g)
                over_steps(dve, step)
                dve.wait_ge(o_ready, NCH)
                nc.vector.bn_stats(k.st[:, NCH - 1, :], big[:, NCH - 1, :]).then_inc(counted, 1)
                dve.wait_ge(counted, NCH)

            @block.scalar
            def _(act):
                def step(i, j, past, last_pair):
                    now = slot(i, j, last_pair)
                    if now:
                        nt.move(act, now[0], now[1], 7, k.g1[:, 0:1], k.b1n[:, 0:1])
                    if past >= 2 and j < ST + 2:
                        act.wait_ge(a_ps, i * ST + (j - 2 + 1))
                        nc.scalar.activation(aT[:, j % 2, :], k.ps[:, 6, 0:P], ACT.Copy).then_inc(a_ready, 1)
                    if j < ST:
                        act.wait_ge(shifted, i * ST + (j + 1))
                        nc.scalar.activation(eb[:, j % 3], lbanks(j), ACT.Exp).then_inc(e_ready, 1)

                for g in range(2):
                    nt.move(act, 0, g, 6 + g, k.g1[:, 0:1], k.b1n[:, 0:1])
                over_steps(act, step)

            @block.gpsimd
            def _(pool):
                with pool.Fori(0, PAIRS) as i:
                    for j in range(ST):
                        e = eb[:, j % 3]
                        pool.wait_ge(e_ready, i * ST + (j + 1))
                        nc.gpsimd.tensor_tensor(t1[:], e[:, 0:6], e[:, 6:12], ALU.add).then_inc(tree, 1)
                        pool.wait_ge(tree, i * (3 * ST) + (3 * j + 1))
                        nc.gpsimd.tensor_tensor(t2[:], t1[:, 0:3], t1[:, 3:6], ALU.add).then_inc(tree, 1)
                        pool.wait_ge(tree, i * (3 * ST) + (3 * j + 2))
                        nc.gpsimd.tensor_tensor(t3[:], t2[:, 0], t2[:, 1], ALU.add).then_inc(tree, 1)
                        pool.wait_ge(tree, i * (3 * ST) + (3 * j + 3))
                        nc.gpsimd.tensor_tensor(den[:, j % 2, :], t3[:], t2[:, 2], ALU.add).then_inc(summed, 1)

            @block.tensor
            def _(pe):
                def query(i, g, bank):
                    pe.wait_ge(nt.moved, i * 4 + (g + 1))
                    nc.tensor.matmul(k.ps[:, bank, 0:GW], k.wq[:, :], nt.xT[:, g // 2, (g % 2) * GW:(g % 2 + 1) * GW],
                                     start=True, stop=True).then_inc(q_ps, 1)

                def step(i, j, past, last_pair):
                    now, before = slot(i, j, last_pair), slot(i, j - 1, last_pair)
                    if j < ST:
                        if j % NC == 0:
                            pe.wait_ge(q_ready, i * 4 + (2 + 2 * (j // NC)))
                        if past >= 2:
                            pe.wait_ge(e_ready, i * ST + (j - 1))
                        for v in range(FR):
                            last = nc.tensor.matmul(lbanks(j)[:, v, :], k.Kbd[:, v, :],
                                                    qT[:, j // NC, (j % NC) * P:(j % NC + 1) * P],
                                                    start=(v % 4 == 0), stop=True, skip_group_check=True)
                        last.then_inc(l_ps, 1)
                    if now or before:
                        if past >= 4:
                            pe.wait_ge(o_ready, i * ST + (j - 3))
                    if now:
                        if past < 4 and j > 1:
                            pe.wait_ge(q_ready, now[0] * 4 + now[1])
                        nt.turn(pe, now[0], now[1], 7)
                    if before:
                        query(before[0], before[1], 7)
                    if past >= 2 and j < ST + 2:
                        a = j - 2
                        pe.wait_ge(w_ready, i * ST + (a + 1))
                        if past >= 3:
                            pe.wait_ge(a_ready, i * ST + a)
                        for v in range(FR):
                            last = nc.tensor.matmul(k.ps[:, 6, 0:P], k.Vbd[:, v, :],
                                                    eb[:, a % 3, v, :], start=(v == 0), stop=(v == FR - 1))
                        last.then_inc(a_ps, 1)
                    if past >= 3:
                        o = j - 3
                        pe.wait_ge(a_ready, i * ST + (o + 1))
                        if past >= 4:
                            pe.wait_ge(o_ready, i * ST + o)
                        else:
                            pe.wait_ge(q_ready, 3)
                        if now:
                            pe.wait_ge(nt.moved, now[0] * 4 + (now[1] + 1))
                        if before:
                            pe.wait_ge(q_ready, before[0] * 4 + (before[1] + 1))
                        nc.tensor.matmul(k.ps[:, 7, 0:P], aT[:, o % 2, :], k.wo1[:, :],
                                         start=True, stop=True).then_inc(o_ps, 1)
                    if j < ST:
                        pe.wait_ge(m_ready, i * ST + (j + 1))
                        for s in range(3):
                            last = nc.tensor.matmul(
                                lbanks(j)[:, s * 4:(s + 1) * 4, :], k.identb[:, :],
                                nm[:, j % 2, None, :].to_broadcast([P, 4, P]), start=False, stop=True,
                                skip_group_check=True)
                        last.then_inc(shifted, 1)

                for g in range(2):
                    nt.turn(pe, 0, g, 6 + g)
                for g in range(2):
                    query(0, g, 4 + g)
                over_steps(pe, step)


def attention_out_phase(nc, k):
    stack, sb, sem = phase_scope(nc)
    with stack:
        ol = sb("ol", [P, 4, GC, P])
        og = sb("og", [P, 4, GC, P])
        oT = sb("oT", [P, 4, GC, P])
        bsum = sb("bsum", [P, C])
        normed, scaled, ot_ps, ot_ready, l_ps, z1, done, counted = (
            sem(x) for x in ("on_normed", "on_scaled", "ot_ps", "ot_ready", "lin_ps", "z1", "z_done", "z_counted"))

        def bc(row):
            return row[:, None, :].to_broadcast([P, GC, P])

        with nc.Block() as block:
            @block.vector
            def _(dve):
                def norm(i, g):
                    for j in range(GC):
                        at = i * (2 * NC) + (g * GC + j)
                        last = nc.vector.tensor_scalar(
                            ol[:, g, j, :], k.big[:, i * 2 + g // 2, (g % 2) * GC + j, :],
                            k.mean[:, bass.ds(at, 1)], k.rstd[:, bass.ds(at, 1)], ALU.subtract, ALU.mult)
                    last.then_inc(normed, 1)

                def body(i, last_pair):
                    for g in range(4):
                        b, c0 = i * 2 + g // 2, (g % 2) * GC
                        dve.wait_ge(l_ps, i * 4 + (g + 1))
                        dst = k.big[:, b, c0:c0 + GC, :]
                        nc.vector.tensor_tensor(dst, k.ps[:, 4 + g, 0:GW].rearrange("p (c t) -> p c t", t=P),
                                                og[:, g], ALU.add).then_inc(z1, 1)
                        if not last_pair:
                            norm(i + 1, g)
                        dve.wait_ge(z1, i * 4 + (g + 1))
                        nc.vector.tensor_tensor(dst, dst, bc(bsum), ALU.add).then_inc(done, 1)
                    for g in range(4):
                        dve.wait_ge(done, i * 4 + (g + 1))
                        for j in range(GC):
                            last = nc.vector.bn_stats(k.st[:, i * (2 * NC) + (g * GC + j), :],
                                                      k.big[:, i * 2 + g // 2, (g % 2) * GC + j, :])
                        last.then_inc(counted, 1)

                nc.vector.tensor_tensor(bsum[:], k.b2n[:], k.bl[:], ALU.add).then_inc(counted, 1)
                for g in range(4):
                    norm(0, g)
                dve.wait_ge(counted, 1)
                over_pairs(dve, body)
                dve.wait_ge(counted, 4 * PAIRS + 1)

            @block.gpsimd
            def _(pool):
                with pool.Fori(0, PAIRS) as i:
                    for g in range(4):
                        pool.wait_ge(normed, i * 4 + (g + 1))
                        nc.gpsimd.tensor_tensor(og[:, g], ol[:, g], bc(k.g2), ALU.mult).then_inc(scaled, 1)

            @block.tensor
            def _(pe):
                with pe.Fori(0, PAIRS) as i:
                    for g in range(5):
                        if g < 4:
                            pe.wait_ge(normed, i * 4 + (g + 1))
                            for j in range(GC):
                                last = nc.tensor.transpose(k.ps[:, g, j * P:(j + 1) * P], ol[:, g, j, :],
                                                           k.ident[:, :])
                            last.then_inc(ot_ps, 1)
                        if g:
                            q = g - 1
                            pe.wait_ge(ot_ready, i * 4 + (q + 1))
                            pe.wait_ge(scaled, i * 4 + (q + 1))
                            for j in range(GC):
                                last = nc.tensor.matmul(k.ps[:, 4 + q, j * P:(j + 1) * P], oT[:, q, j, :],
                                                        k.wl[:, :], start=True, stop=True)
                            last.then_inc(l_ps, 1)

            @block.scalar
            def _(act):
                with act.Fori(0, PAIRS) as i:
                    for g in range(4):
                        act.wait_ge(ot_ps, i * 4 + (g + 1))
                        nc.scalar.activation(oT[:, g].rearrange("p c t -> p (c t)"), k.ps[:, g, 0:GW],
                                             ACT.Identity, scale=k.g2c[:, 0:1], bias=k.b2c[:, 0:1]).then_inc(ot_ready, 1)


def attention_add_phase(nc, k):
    stack, sb, sem = phase_scope(nc)
    with stack:
        ol = sb("ol3", [P, 4, GC, P])
        normed, scaled, biased, added, counted = (
            sem(x) for x in ("an_normed", "an_scaled", "an_biased", "an_added", "an_counted"))

        def bc(row):
            return row[:, None, :].to_broadcast([P, GC, P])

        with nc.Block() as block:
            @block.vector
            def _(dve):
                def norm(i, g):
                    for j in range(GC):
                        at = i * (2 * NC) + (g * GC + j)
                        last = nc.vector.tensor_scalar(
                            ol[:, g, j, :], k.big[:, i * 2 + g // 2, (g % 2) * GC + j, :],
                            k.mean[:, bass.ds(at, 1)], k.rstd[:, bass.ds(at, 1)], ALU.subtract, ALU.mult)
                    last.then_inc(normed, 1)

                def body(i, last_pair):
                    for g in range(4):
                        b, c0 = i * 2 + g // 2, (g % 2) * GC
                        hh = k.h[:, b, c0:c0 + GC, :]
                        dve.wait_ge(scaled, i * 4 + (g + 1))
                        nc.vector.tensor_tensor(ol[:, g], ol[:, g], bc(k.b3n), ALU.add).then_inc(biased, 1)
                        dve.wait_ge(biased, i * 4 + (g + 1))
                        nc.vector.tensor_tensor(hh, hh, ol[:, g], ALU.add).then_inc(added, 1)
                        dve.wait_ge(added, i * 4 + (g + 1))
                        if not last_pair:
                            norm(i + 1, g)
                        for j in range(GC):
                            last = nc.vector.bn_stats(k.st[:, i * (2 * NC) + (g * GC + j), :], k.h[:, b, c0 + j, :])
                        last.then_inc(counted, 1)

                for g in range(4):
                    norm(0, g)
                over_pairs(dve, body)
                dve.wait_ge(counted, 4 * PAIRS)

            @block.gpsimd
            def _(pool):
                with pool.Fori(0, PAIRS) as i:
                    for g in range(4):
                        pool.wait_ge(normed, i * 4 + (g + 1))
                        nc.gpsimd.tensor_tensor(ol[:, g], ol[:, g], bc(k.g3), ALU.mult).then_inc(scaled, 1)


def token_choice_phase(nc, k):
    stack, sb, sem = phase_scope(nc)
    with stack:
        nt = NormTranspose(nc, k, "t_", sb, sem)
        lg = sb("lg", [P, NCH, E1])
        l2 = sb("l2", [P, NCH, E1])
        oh = sb("oh", [P, 2, NCH, E1])
        pr = sb("pr", [P, NCH, E1])
        mx = sb("mx", [P, 2, NCH])
        pm = sb("pm", [P, NCH])
        wt = sb("wt", [P, NC, B, E1])
        wT = sb("wT", [P, NC, P])
        rb = sb("rb", [P, 4, TP])
        lg_ps, biased, chain, expd, wt_ps, wt_ready = (
            sem(x) for x in ("tl_ps", "biased", "t_chain", "t_exp", "wt_ps", "wt_ready"))
        by_chunk = wt[:].rearrange("p c b e -> p b c e")
        WT_DONE = 17

        with nc.Block() as block:
            @block.vector
            def _(dve):
                def body(i, last_pair):
                    if not last_pair:
                        nt.next_pair(dve, i, k.h)
                    dve.wait_ge(lg_ps, i + 1)
                    nc.vector.tensor_tensor(lg[:, bass.ds(i * 12, 12), :],
                                            k.ps[:, 4, 0:12 * E1].rearrange("p (m e) -> p m e", e=E1),
                                            k.gate_b[:, None, :].to_broadcast([P, 12, E1]), ALU.add).then_inc(biased, 1)

                dve.sem_inc(biased, 1)
                nt.vector(dve, 0, k.h)
                over_pairs(dve, body)
                dve.wait_ge(biased, PAIRS + 1)
                n = [0]

                def link(ins):
                    n[0] += 1
                    ins.then_inc(chain, 1)
                    dve.wait_ge(chain, n[0])

                prio = k.prio[:, None, :].to_broadcast([P, NCH, E1])

                def wide(a):
                    return a[:, :, None].to_broadcast([P, NCH, E1])

                for q in range(2):
                    src = lg if q == 0 else l2
                    link(nc.vector.tensor_reduce(mx[:, q, :], src[:], AX_X, ALU.max))
                    link(nc.vector.tensor_tensor(pr[:], src[:], wide(mx[:, q, :]), ALU.is_equal))
                    link(nc.vector.tensor_tensor(pr[:], pr[:], prio, ALU.mult))
                    link(nc.vector.tensor_reduce(pm[:], pr[:], AX_X, ALU.max))
                    link(nc.vector.tensor_tensor(oh[:, q], prio, wide(pm[:, :]), ALU.is_equal))
                    if q == 0:
                        link(nc.vector.scalar_tensor_tensor(out=l2[:], in0=oh[:, 0], scalar=-3.0e38, in1=lg[:],
                                                            op0=ALU.mult, op1=ALU.add))
                link(nc.vector.tensor_tensor(pm[:], mx[:, 1, :], mx[:, 0, :], ALU.subtract))
                assert n[0] == 12
                dve.wait_ge(expd, 1)
                link(nc.vector.tensor_scalar(pm[:], mx[:, 0, :], 1.0, None, ALU.add))
                link(nc.vector.reciprocal(mx[:, 1, :], pm[:]))
                link(nc.vector.tensor_tensor(mx[:, 0, :], mx[:, 0, :], mx[:, 1, :], ALU.mult))
                link(nc.vector.tensor_tensor(l2[:], oh[:, 1], wide(mx[:, 0, :]), ALU.mult))
                link(nc.vector.tensor_tensor(pr[:], oh[:, 0], wide(mx[:, 1, :]), ALU.mult))
                nc.vector.tensor_tensor(by_chunk, l2[:].rearrange("p (b c) e -> p b c e", c=NC),
                                        pr[:].rearrange("p (b c) e -> p b c e", c=NC), ALU.add).then_inc(chain, 1)
                assert n[0] == WT_DONE

            @block.scalar
            def _(act):
                with act.Fori(0, PAIRS) as i:
                    nt.scalar(act, i)
                act.wait_ge(chain, 12)
                nc.scalar.activation(mx[:, 0, :], pm[:], ACT.Exp).then_inc(expd, 1)
                act.wait_ge(wt_ps, 1)
                nc.scalar.activation(wT[:].rearrange("p c t -> p (c t)"), k.psf[:, 0:NC * P], ACT.Copy).then_inc(wt_ready, 1)
                act.wait_ge(wt_ready, 1)

            @block.tensor
            def _(pe):
                with pe.Fori(0, PAIRS) as i:
                    nt.tensor(pe, i)
                    pe.wait_ge(nt.moved, i * 4 + 4)
                    pe.wait_ge(biased, i + 1)
                    for m in range(12):
                        last = nc.tensor.matmul(k.ps[:, 4, m * E1:(m + 1) * E1],
                                                nt.xT[:, m // NC, (m % NC) * P:(m % NC + 1) * P],
                                                k.gate1[:, :], start=True, stop=True)
                    last.then_inc(lg_ps, 1)
                pe.wait_ge(chain, WT_DONE + 1)
                for c in range(NC):
                    last = nc.tensor.transpose(k.psf[:, c * P:(c + 1) * P], wt[:, c].rearrange("p b e -> p (b e)"),
                                               k.ident[:, :])
                last.then_inc(wt_ps, 1)

        expert_block(nc, k, "e1_", sb, sem, nt, rb, E1, 2, ACT.Relu, k.w1_1, k.b1_1, k.w2_1,
                     lambda i, c, par, e, n: by_chunk_flat(wt)[0:n, bass.ds(i * (2 * E1) + (c * B * E1 + par * E1 + e), 1)])

        b2_ps, b2_added, stored = sem("b2b_ps"), sem("b2b_added"), k.stored
        with nc.Block() as block:
            @block.tensor
            def _(pe):
                for c in range(NC):
                    n = rows(c)
                    for s in range(4):
                        q = c * 4 + s
                        if q >= 8:
                            pe.wait_ge(b2_added, q - 7)
                        nc.tensor.matmul(k.ps[0:n, q % 8, :], wT[:, c, 0:n],
                                         k.b2_1[:, s * 4:(s + 1) * 4, :].rearrange("p b d -> p (b d)"),
                                         start=True, stop=True).then_inc(b2_ps, 1)

            @block.vector
            def _(dve):
                for c in range(NC):
                    n = rows(c)
                    for s in range(4):
                        q = c * 4 + s
                        dve.wait_ge(b2_ps, q + 1)
                        hh = k.h[0:n, s * 4:(s + 1) * 4, c, :]
                        nc.vector.tensor_tensor(hh, hh, k.ps[0:n, q % 8, :].rearrange("p (b d) -> p b d", d=C),
                                                ALU.add).then_inc(b2_added, 1)

            @block.sync
            def _(sp):
                for c in range(NC):
                    sp.wait_ge(b2_added, 4 * (c + 1))
                    store_chunk(sp, k, c).then_inc(stored, 16)
                sp.wait_ge(stored, 16 * NC)


def by_chunk_flat(wt):
    return wt[:].rearrange("p c b e -> p (c b e)")


def store_chunk(sp, k, c):
    n = rows(c)
    return sp.dma_start(k.out[:, c * P:c * P + n, :].rearrange("b t d -> t b d"), k.h[0:n, :, c, :])


def audio_tower(nc, a, out):
    k = Ctx()
    with ExitStack() as ctx:
        def sb(name, shape, dt=F32):
            return ctx.enter_context(nc.sbuf_tensor(name, shape, dt))

        k.out = out
        k.xT = a["xT"]
        k.ps = ctx.enter_context(nc.psum_tensor("banks", [P, 8, 512], F32))[:]
        k.psf = k.ps.rearrange("p b n -> p (b n)")
        k.h = sb("h", [P, B, NC, C])
        k.mean = sb("mean", [P, NCH])
        k.rstd = sb("rstd", [P, NCH])
        k.st = sb("st", [P, NCH, 6])
        k.eps = sb("eps", [P, 1])
        k.w_in = ctx.enter_context(nc.semaphore("w_in"))
        k.rest_in = ctx.enter_context(nc.semaphore("rest_in"))
        k.stored = ctx.enter_context(nc.semaphore("stored"))
        k.norm_seen, k.norm_chain, k.norm_rooted = (
            ctx.enter_context(nc.semaphore(x)) for x in ("norm_seen", "norm_chain", "norm_rooted"))
        k.norm_past = (0, 0, 0)

        first, rest = [], []

        def load(name, shape, dram, group=rest, dt=F32):
            t = sb(name, shape, dt)
            group.append((t[:], dram))
            return t

        cw = a["L0_tok_WT"]
        k.wc01 = load("wc01", [P, C], cw[0:128, :], first)
        k.wc23 = load("wc23", [P, C], cw[128:256, :], first)
        k.wc4 = load("wc4", [64, C], cw[256:320, :], first)

        def col(name, src, group=rest):
            return load(name, [P, 1], a[src].rearrange("(p a) -> p a", a=1), group)

        def row(name, src, lo=0, n=C):
            return load(name, [P, n], a[src][lo:lo + n].partition_broadcast(P))

        k.conv_b = col("conv_b", "L0_tok_b", first)
        k.gamma = col("gamma", "L0_tok_gamma", first)
        k.beta = col("beta", "L0_tok_beta", first)
        k.ident = load("ident", [P, P], a["ident"], first)
        k.lmask = load("lmask", [P, NL + 1, P], a["lmask"])
        k.umask1 = load("umask1", [P, P], a["umask1"])
        k.upper = load("upper", [P, P], a["upper"])
        k.prio = load("prio", [P, E1], a["prio"].partition_broadcast(P))
        k.wkvl = sb("wkvl", [P, 2 * C + 1])
        rest.append((k.wkvl[:, 0:2 * C], a["L0_attn_WgT"][:, C:3 * C]))
        rest.append((k.wkvl[:, 2 * C:], a["L0_attn_WlrT"]))
        k.kvl_b = sb("kvl_b", [P, 2 * C + 1])
        rest.append((k.kvl_b[:, 0:2 * C], a["L0_attn_bg"][C:3 * C].partition_broadcast(P)))
        rest.append((k.kvl_b[:, 2 * C:], a["L0_attn_blr"].partition_broadcast(P)))
        k.wqb = sb("wqb", [P, C + 1])
        rest.append((k.wqb[:, 0:C], a["L0_attn_Wg"][0:C, :]))
        rest.append((k.wqb[:, C:], a["L0_attn_bg"][0:C].rearrange("(p a) -> p a", a=1)))
        k.wo0 = load("wo0", [P, C], a["L0_attn_WoT"])
        k.bo0 = row("bo0", "L0_attn_bo")
        k.gate0 = load("gate0", [P, E0], a["L0_ffn_gate_weight"])
        k.w1_0 = load("w1_0", [P, E0, P], a["L0_ffn_w1"].rearrange("e d f -> d e f"))
        k.w2_0 = load("w2_0", [P, E0, C], a["L0_ffn_w2"].rearrange("e f d -> f e d"))
        k.b1_0 = load("b1_0", [P, E0], a["L0_ffn_b1T"])
        k.b2_0 = sb("b2_0", [P, 8, C])
        k.b2_1 = sb("b2_1", [P, B, C])
        k.video = load("video", [P, NC, C], a["video"].rearrange("(c p) d -> p c d", p=P))
        k.wq = load("wq", [P, C], a["L1_attn_WqT"])
        k.wk = load("wk", [P, C], a["L1_attn_WkT"])
        k.wv = load("wv", [P, C], a["L1_attn_WvT"])
        k.wo1 = load("wo1", [P, C], a["L1_attn_WoT"])
        k.wl = load("wl", [P, C], a["L1_attn_WlT"])
        k.g1 = col("g1", "L1_attn_ln1_g")
        k.b1n = col("b1n", "L1_attn_ln1_b")
        k.bq = col("bq", "L1_attn_bq")
        k.bk = col("bk", "L1_attn_bk")
        k.bv = row("bv", "L1_attn_bv")
        k.bo1 = row("bo1", "L1_attn_bo")
        k.g2 = row("g2", "L1_attn_ln2_g")
        k.b2n = row("b2n", "L1_attn_ln2_b")
        k.g2c = col("g2c", "L1_attn_ln2_g")
        k.b2c = col("b2c", "L1_attn_ln2_b")
        k.bl = row("bl", "L1_attn_bl")
        k.g3 = row("g3", "L1_attn_ln3_g")
        k.b3n = row("b3n", "L1_attn_ln3_b")
        k.gate1 = load("gate1", [P, E1], a["L1_ffn_gate_w"])
        k.gate_b = row("gate_b", "L1_ffn_gate_b", 0, E1)
        k.w1_1 = load("w1_1", [P, 2 * E1, P], a["L1_ffn_w1T"])
        k.w2_1 = load("w2_1", [P, 2 * E1, C], a["L1_ffn_w2"].rearrange("e (f p) d -> p (e f) d", p=P))
        k.b1_1 = load("b1_1", [P, 2 * E1], a["L1_ffn_b1T"])
        k.first_loads, k.rest_loads = first, rest

        conv_phase(nc, k)
        k.identb = sb("identb", [P, P], BF16)
        setup_phase(nc, k, a, ctx)
        if DEBUG_STOP >= 1:
            norm_phase(nc, k, "n0", k.h)
            delta_phase(nc, k)
        if DEBUG_STOP >= 2:
            norm_phase(nc, k, "n1", k.h)
            expert_choice_phase(nc, k)
        if DEBUG_STOP >= 3:
            norm_phase(nc, k, "n2", k.h, twice=True)
            with ExitStack() as att:
                k.big = att.enter_context(nc.sbuf_tensor("o_all", [P, B, NC, C], F32))
                k.Kbd, k.Vbd = k.w1_0[:, 0:FR, :], k.w2_0[:, 0:FR, :]
                video_phase(nc, k)
                attention_phase(nc, k)
                norm_phase(nc, k, "n3", k.big, counted=True)
                attention_out_phase(nc, k)
                norm_phase(nc, k, "n4", k.big, counted=True)
                attention_add_phase(nc, k)
        if DEBUG_STOP >= 4:
            norm_phase(nc, k, "n5", k.h, counted=True)
            token_choice_phase(nc, k)
        else:
            stored = k.stored
            with nc.Block() as block:
                @block.sync
                def _(sp):
                    for c in range(NC):
                        store_chunk(sp, k, c).then_inc(stored, 16)
                    sp.wait_ge(stored, 16 * NC)


def setup_phase(nc, k, a, ctx):
    zeroed, b2_in = ctx.enter_context(nc.semaphore("b2_zeroed")), ctx.enter_context(nc.semaphore("b2_in"))
    with nc.Block() as block:
        @block.gpsimd
        def _(pool):
            nc.gpsimd.tensor_copy(k.identb[:, :], k.ident[:, :])
            nc.gpsimd.memset(k.b2_0[:], 0.0).then_inc(zeroed, 1)
            nc.gpsimd.memset(k.b2_1[:], 0.0).then_inc(zeroed, 1)

        @block.sync
        def _(sp):
            sp.wait_ge(zeroed, 2)
            for b in range(8):
                sp.dma_start(k.b2_0[b * E0:(b + 1) * E0, b, :], a["L0_ffn_b2"]).then_inc(b2_in, 16)
            for b in range(B):
                sp.dma_start(k.b2_1[b * E1:(b + 1) * E1, b, :], a["L1_ffn_b2"]).then_inc(b2_in, 16)
            sp.wait_ge(b2_in, 16 * (8 + B))


def shape_constants():
    t = np.arange(P)
    masks = []
    for s in (1,) + LEVELS:
        same = (t[:, None] // (2 * s)) == (t[None, :] // (2 * s))
        masks.append((same & (t[:, None] % (2 * s) >= s) & (t[None, :] % (2 * s) < s)).astype(np.float32))
    lmask = np.ascontiguousarray(np.stack(masks, axis=1))
    return {
        "ident": np.eye(P, dtype=np.float32),
        "lmask": lmask,
        "umask1": np.ascontiguousarray(masks[0].T),
        "upper": np.triu(np.ones((P, P), np.float32), 1),
        "prio": np.arange(E1, 0, -1).astype(np.float32),
    }


def kernel(**inputs):
    import concourse.bacc as bacc
    from concourse.bass_utils import run_bass_kernel_spmd

    x = {n: np.asarray(v) for n, v in inputs.items()}
    lay = {
        "xT": x["x"].transpose(2, 0, 1),
        "L0_tok_WT": x["L0_tok_W"].T,
        "L0_attn_WgT": x["L0_attn_Wg"].T,
        "L0_attn_WlrT": x["L0_attn_Wlr"].T,
        "L0_attn_WoT": x["L0_attn_Wo"].T,
        "L0_ffn_b1T": x["L0_ffn_b1"].T,
        "video": x["L1_attn_video_embeds"].transpose(1, 0, 2).reshape(FR * NV, C),
        "L1_attn_WqT": x["L1_attn_Wq"].T,
        "L1_attn_WkT": x["L1_attn_Wk"].T,
        "L1_attn_WvT": x["L1_attn_Wv"].T,
        "L1_attn_WoT": x["L1_attn_Wo"].T,
        "L1_attn_WlT": x["L1_attn_Wl"].T,
        "L1_ffn_w1T": x["L1_ffn_w1"].transpose(1, 0, 2).reshape(C, 2 * E1, P),
        "L1_ffn_b1T": x["L1_ffn_b1"].reshape(2 * E1, P).T,
    }
    for name in ("L0_tok_b", "L0_tok_gamma", "L0_tok_beta", "L0_attn_bg", "L0_attn_blr", "L0_attn_Wg", "L0_attn_bo",
                 "L0_ffn_gate_weight", "L0_ffn_w1", "L0_ffn_w2", "L0_ffn_b2", "L1_attn_ln1_g", "L1_attn_ln1_b",
                 "L1_attn_bq", "L1_attn_bk", "L1_attn_bv", "L1_attn_bo", "L1_attn_bl", "L1_attn_ln2_g",
                 "L1_attn_ln2_b", "L1_attn_ln3_g", "L1_attn_ln3_b", "L1_ffn_gate_w", "L1_ffn_gate_b", "L1_ffn_w2",
                 "L1_ffn_b2"):
        lay[name] = x[name]
    lay.update(shape_constants())
    lay = {n: np.ascontiguousarray(v) for n, v in lay.items()}

    nc = bacc.Bacc("TRN2", target_bir_lowering=False, num_devices=1)
    aps = {n: nc.dram_tensor(f"in_{n}", v.shape, mybir.dt.from_np(v.dtype), kind="ExternalInput").ap()
           for n, v in lay.items()}
    out = nc.dram_tensor("out", (B, T, C), F32, kind="ExternalOutput").ap()
    audio_tower(nc, aps, out)
    r = run_bass_kernel_spmd(nc, [{f"in_{n}": v for n, v in lay.items()}], core_ids=[0])
    return r.results[0]["out"]
```

```python
from contextlib import ExitStack

import numpy as np

import concourse.bass as bass
from concourse import mybir

ALU = mybir.AluOpType
ACT = mybir.ActivationFunctionType
F32 = mybir.dt.float32
BF16 = mybir.dt.bfloat16
AX_X = mybir.AxisListType.X

P = 128
B = 16
T_IN = 750
CTX = 5
T = T_IN - CTX + 1
C = 128
NC = 6
LAST = T - (NC - 1) * P
TP = NC * P
NCH = B * NC
PAIRS = B // 2
HALF_T = T // 2
GC = 3
GW = GC * P
HALF = P // 2
LEVELS = (2, 4, 8, 16, 32, 64)
NL = len(LEVELS)
E0 = 16
CAP = T // E0 * 2
E1 = 8
NV = 64
FR = 12
NFREE = (384, T - 384)
EPS = 1e-5


def rows(c):
    return P if c < NC - 1 else LAST


class Ctx:
    pass


def phase_scope(nc):
    stack = ExitStack()

    def sb(name, shape, dt=F32):
        return stack.enter_context(nc.sbuf_tensor(name, shape, dt))

    def sem(name):
        return stack.enter_context(nc.semaphore(name))

    return stack, sb, sem


def conv_phase(nc, k):
    stack, sb, sem = phase_scope(nc)
    with stack:
        yT = sb("yT", [P, B, T])
        yn = sb("yn", [P, 2, TP])
        bst = sb("bst", [P, 2 * B, 6])
        bmv = sb("bmv", [P, 2])
        bsc = sb("bsc", [P, 4])
        xw = k.h[:].rearrange("p b c d -> p (b c d)")[:, 0:B * T_IN].rearrange("p (b t) -> p b t", t=T_IN)
        x_in = [sem(f"x_in{q}") for q in range(4)]
        w_in, rest_in = k.w_in, k.rest_in
        conv_ps, conv_relu, stats = sem("conv_ps"), sem("conv_relu"), sem("conv_stats")
        bn_chain, bn_sqrt = sem("bn_chain"), sem("bn_sqrt")
        yn_ready, tr_ps, h_stored, pads = sem("yn_ready"), sem("tr_ps"), sem("h_stored"), sem("pads")
        counted, zeroed = sem("c_counted"), sem("b2_zeroed")
        qb = B // 4

        with nc.Block() as block:
            @block.sync
            def _(sp):
                for ap, dram in k.first_loads:
                    sp.dma_start(ap, dram).then_inc(w_in, 16)
                for q in range(4):
                    s = slice(q * qb, (q + 1) * qb)
                    sp.dma_start(xw[0:64, s, :], k.xT[:, s, :]).then_inc(x_in[q], 16)
                    sp.dma_start(xw[64:128, s, 0:T_IN - 1], k.xT[:, s, 1:T_IN]).then_inc(x_in[q], 16)
                for ap, dram in k.rest_loads:
                    sp.dma_start(ap, dram).then_inc(rest_in, 16)
                sp.wait_ge(zeroed, 2)
                for ap, dram in k.zeroed_loads:
                    sp.dma_start(ap, dram).then_inc(rest_in, 16)

            @block.gpsimd
            def _(pool):
                pool.wait_ge(w_in, 16 * len(k.first_loads))
                nc.gpsimd.tensor_copy(k.identb[:, :], k.ident[:, :])
                nc.gpsimd.memset(k.b2_0[:], 0.0).then_inc(zeroed, 1)
                nc.gpsimd.memset(k.b2_1[:], 0.0).then_inc(zeroed, 1)

            @block.tensor
            def _(pe):
                pe.wait_ge(w_in, 16 * len(k.first_loads))
                for q in range(4):
                    pe.wait_ge(x_in[q], 32)
                    with pe.Fori(q * qb // 2, (q + 1) * qb // 2) as i:
                        for par in range(2):
                            b = i * 2 + par
                            for half in range(2):
                                pe.wait_ge(conv_relu, i * 4 + (par * 2 + half + 1))
                                ps = k.ps[:, par * 2 + half, 0:HALF_T]
                                t0 = half * HALF_T
                                nc.tensor.matmul(ps, k.wc01[:, :], xw[:, b, t0:t0 + HALF_T], start=True, stop=False)
                                nc.tensor.matmul(ps, k.wc23[:, :], xw[:, b, t0 + 2:t0 + 2 + HALF_T],
                                                 start=False, stop=False)
                                nc.tensor.matmul(ps, k.wc4[:, :], xw[0:64, b, t0 + 4:t0 + 4 + HALF_T],
                                                 start=False, stop=True).then_inc(conv_ps, 1)

            @block.scalar
            def _(act):
                act.wait_ge(w_in, 16 * len(k.first_loads))
                act.sem_inc(conv_relu, 4)
                with act.Fori(0, PAIRS) as i:
                    for par in range(2):
                        b = i * 2 + par
                        for half in range(2):
                            act.wait_ge(conv_ps, i * 4 + (par * 2 + half + 1))
                            nc.scalar.activation(yT[:, b, half * HALF_T:(half + 1) * HALF_T],
                                                 k.ps[:, par * 2 + half, 0:HALF_T], ACT.Relu,
                                                 bias=k.conv_b[:, 0:1]).then_inc(conv_relu, 1)
                act.wait_ge(bn_chain, 1)
                nc.scalar.activation(bsc[:, 0:1], bmv[:, 1:2], ACT.Sqrt, bias=k.eps[:, 0:1]).then_inc(bn_sqrt, 1)

            @block.vector
            def _(dve):
                nc.vector.memset(k.eps[:], EPS)
                with dve.Fori(0, PAIRS) as i:
                    for par in range(2):
                        b = i * 2 + par
                        for half in range(2):
                            dve.wait_ge(conv_relu, i * 4 + (par * 2 + half + 5))
                            nc.vector.bn_stats(bst[:, i * 4 + (par * 2 + half), :],
                                               yT[:, b, half * HALF_T:(half + 1) * HALF_T]).then_inc(stats, 1)
                dve.wait_ge(stats, 2 * B)
                nc.vector.bn_aggr(bmv[:, :], bst[:].rearrange("p a s -> p (a s)")).then_inc(bn_chain, 1)
                dve.wait_ge(bn_sqrt, 1)
                nc.vector.reciprocal(bsc[:, 1:2], bsc[:, 0:1]).then_inc(bn_chain, 1)
                dve.wait_ge(bn_chain, 2)
                nc.vector.tensor_tensor(bsc[:, 2:3], bsc[:, 1:2], k.gamma[:, 0:1], ALU.mult).then_inc(bn_chain, 1)
                dve.wait_ge(bn_chain, 3)
                nc.vector.tensor_tensor(bsc[:, 0:1], bmv[:, 0:1], bsc[:, 2:3], ALU.mult).then_inc(bn_chain, 1)
                dve.wait_ge(bn_chain, 4)
                nc.vector.tensor_tensor(bsc[:, 3:4], k.beta[:, 0:1], bsc[:, 0:1], ALU.subtract).then_inc(bn_chain, 1)
                dve.wait_ge(bn_chain, 5)

        with nc.Block() as block:
            @block.sync
            def _(sp):
                sp.wait_ge(rest_in, 16 * (len(k.rest_loads) + len(k.zeroed_loads)))

            @block.gpsimd
            def _(pool):
                nc.gpsimd.memset(k.h[96:128, :, NC - 1, :], 0.0).then_inc(pads, 1)

            @block.vector
            def _(dve):
                def stats(b):
                    dve.wait_ge(h_stored, b + 3)
                    for c in range(NC):
                        last = nc.vector.bn_stats(k.st[:, b * NC + c, :], k.h[:, b, c, :])
                    last.then_inc(counted, 1)

                for b in range(B):
                    dve.wait_ge(tr_ps, b + 1)
                    nc.vector.tensor_scalar(yn[:, b % 2, 0:T], yT[:, b, :], bsc[:, 2:3], bsc[:, 3:4],
                                            ALU.mult, ALU.add).then_inc(yn_ready, 1)
                    if b >= 2:
                        stats(b - 2)
                for b in range(B - 2, B):
                    stats(b)
                dve.wait_ge(counted, B)

            @block.tensor
            def _(pe):
                pe.sem_inc(tr_ps, 2)
                with pe.Fori(0, PAIRS) as i:
                    for par in range(2):
                        pe.wait_ge(yn_ready, i * 2 + (par + 1))
                        pe.wait_ge(h_stored, i * 2 + (par + 1))
                        for c in range(NC):
                            n = rows(c)
                            last = nc.tensor.transpose(k.psf[0:n, par * 1024 + c * P:par * 1024 + (c + 1) * P],
                                                       yn[:, par, c * P:c * P + n], k.ident[:, :])
                        last.then_inc(tr_ps, 1)

            @block.scalar
            def _(act):
                act.sem_inc(h_stored, 2)
                act.wait_ge(pads, 1)
                with act.Fori(0, PAIRS) as i:
                    for par in range(2):
                        b = i * 2 + par
                        act.wait_ge(tr_ps, i * 2 + (par + 3))
                        o = par * 1024
                        nc.scalar.activation(k.h[:, b, 0:NC - 1, :],
                                             k.psf[:, o:o + 5 * P].rearrange("p (c d) -> p c d", d=P), ACT.Copy)
                        nc.scalar.activation(k.h[0:LAST, b, NC - 1, :],
                                             k.psf[0:LAST, o + 5 * P:o + 6 * P], ACT.Copy).then_inc(h_stored, 1)


def norm_phase(nc, k, tag, twice=False, shift=False):
    stack, sb, sem = phase_scope(nc)
    with stack:
        st = k.st
        tmp = sb(tag + "tmp", [P, 4, NCH])
        chain, rooted = k.norm_chain, k.norm_rooted
        chain0, rooted0 = k.norm_past
        k.norm_past = (chain0 + (12 if twice else 9 if shift else 8), rooted0 + (2 if twice else 1))
        with nc.Block() as block:
            @block.vector
            def _(dve):
                n = [0]

                def link(ins):
                    n[0] += 1
                    ins.then_inc(chain, 1)
                    dve.wait_ge(chain, chain0 + n[0])

                me, ve, mo, vo = (st[:, :, q] for q in (1, 2, 4, 5))
                link(nc.vector.tensor_tensor(tmp[:, 0, :], me, mo, ALU.add))
                link(nc.vector.tensor_tensor(tmp[:, 1, :], me, mo, ALU.subtract))
                link(nc.vector.tensor_tensor(tmp[:, 2, :], ve, vo, ALU.add))
                link(nc.vector.tensor_scalar(k.mean[:, :], tmp[:, 0, :], 0.5, None, ALU.mult))
                link(nc.vector.tensor_tensor(tmp[:, 3, :], tmp[:, 1, :], tmp[:, 1, :], ALU.mult))
                link(nc.vector.tensor_scalar(tmp[:, 0, :], tmp[:, 2, :], 1.0 / C, None, ALU.mult))
                link(nc.vector.scalar_tensor_tensor(out=tmp[:, 1, :], in0=tmp[:, 3, :], scalar=0.25,
                                                    in1=tmp[:, 0, :], op0=ALU.mult, op1=ALU.add))
                var_at = n[0]
                dve.wait_ge(rooted, rooted0 + 1)
                link(nc.vector.reciprocal(k.rstd[:, :], tmp[:, 2, :]))
                if twice:
                    link(nc.vector.tensor_tensor(tmp[:, 0, :], k.rstd[:, :], k.rstd[:, :], ALU.mult))
                    link(nc.vector.tensor_tensor(tmp[:, 3, :], tmp[:, 0, :], tmp[:, 1, :], ALU.mult))
                    dve.wait_ge(rooted, rooted0 + 2)
                    link(nc.vector.reciprocal(tmp[:, 0, :], tmp[:, 2, :]))
                    link(nc.vector.tensor_tensor(k.rstd[:, :], k.rstd[:, :], tmp[:, 0, :], ALU.mult))
                if shift:
                    link(nc.vector.scalar_tensor_tensor(out=k.mean[:, :], in0=k.mean[:, :], scalar=-1.0,
                                                        in1=k.rstd[:, :], op0=ALU.mult, op1=ALU.mult))
                assert var_at == 7 and chain0 + n[0] == k.norm_past[0]

            @block.scalar
            def _(act):
                act.wait_ge(chain, chain0 + 7)
                nc.scalar.activation(tmp[:, 2, :], tmp[:, 1, :], ACT.Sqrt, bias=k.eps[:, 0:1]).then_inc(rooted, 1)
                if twice:
                    act.wait_ge(chain, chain0 + 10)
                    nc.scalar.activation(tmp[:, 2, :], tmp[:, 3, :], ACT.Sqrt, bias=k.eps[:, 0:1]).then_inc(rooted, 1)


def over_pairs(eng, body):
    with eng.Fori(0, PAIRS - 1) as i:
        body(i, False)
    body(PAIRS - 1, True)


class NormTranspose:

    def __init__(self, nc, k, tag, sb, sem):
        self.nc, self.k = nc, k
        self.xl = sb(tag + "xl", [P, 4, GC, P])
        self.xT = sb(tag + "xT", [P, 2, TP])
        self.normed, self.turned, self.moved = sem(tag + "normed"), sem(tag + "turned"), sem(tag + "moved")

    def norm(self, i, g, src):
        for j in range(GC):
            c = (g % 2) * GC + j
            at = i * (2 * NC) + ((g // 2) * NC + c)
            last = self.nc.vector.tensor_scalar(
                self.xl[:, g, j, :], src[:, i * 2 + g // 2, c, :], self.k.mean[:, bass.ds(at, 1)],
                self.k.rstd[:, bass.ds(at, 1)], ALU.subtract, ALU.mult)
        last.then_inc(self.normed, 1)

    def vector(self, dve, i, src):
        for g in range(4):
            self.norm(i, g, src)

    def next_pair(self, dve, i, src):
        for g in range(4):
            dve.wait_ge(self.turned, i * 4 + (g + 1))
            self.norm(i + 1, g, src)

    def turn(self, pe, i, g, bank):
        pe.wait_ge(self.normed, i * 4 + (g + 1))
        for j in range(GC):
            last = self.nc.tensor.transpose(self.k.ps[:, bank, j * P:(j + 1) * P], self.xl[:, g, j, :],
                                            self.k.ident[:, :])
        last.then_inc(self.turned, 1)

    def tensor(self, pe, i):
        for g in range(4):
            self.turn(pe, i, g, g)

    def move(self, act, i, g, bank, scale=None, bias=None):
        act.wait_ge(self.turned, i * 4 + (g + 1))
        out = self.xT[:, g // 2, (g % 2) * GW:(g % 2 + 1) * GW]
        if scale is None:
            ins = self.nc.scalar.activation(out, self.k.ps[:, bank, 0:GW], ACT.Copy)
        else:
            ins = self.nc.scalar.activation(out, self.k.ps[:, bank, 0:GW], ACT.Identity, scale=scale, bias=bias)
        ins.then_inc(self.moved, 1)

    def scalar(self, act, i):
        for g in range(4):
            self.move(act, i, g, g)


def delta_phase(nc, k):
    stack, sb, sem = phase_scope(nc)
    with stack:
        xl = sb("d_xl", [P, 4, GC, P])
        yb = xl
        xT = sb("d_xT", [P, 2, 2, TP])
        kvl = sb("kvl", [P, 2, 12, 2 * C + 1])
        nk = sb("nk", [P, 12])
        nks = sb("nks", [P, 12])
        rk = sb("rk", [P, 12])
        kh = sb("kh", [P, 2, 12, P])
        kT = sb("kT", [P, 2, 12, P])
        NT = sb("NT", [P, 12, P])
        D = sb("D", [P, 12, P])
        DT = sb("DT", [P, 12, P])
        W = sb("W", [P, 12, HALF])
        R = sb("R", [P, 2, P])
        bb = R
        UU = sb("UU", [P, 2, 2 * P])
        S = sb("S", [P, 2, P])
        kvs = sb("kvs", [P, 2, P])
        PT = sb("PT", [P, 2, P + 1])
        M = sb("M", [P, 2, P])
        normed, turned, moved = sem("d_normed"), sem("d_turned"), sem("d_moved")
        kv_ps, kv_ready, squared, rooted, rk_ready = (sem(x) for x in ("kv_ps", "kv_ready", "k_sq", "k_root", "rk_ready"))
        kh_ready, kT_ps, kT_ready, gram_ps, reset = (sem(x) for x in ("kh_ready", "kT_ps", "kT_ready", "gram_ps", "d_reset"))
        near, w_ps, w_ready, x_ps, d_ready, t_ps, dt_ready = (
            sem(x) for x in ("near", "w_ps", "w_ready", "x_ps", "d_ready", "t_ps", "dt_ready"))
        r_ps, r_ready, u_ps, u_ready, sk_ps, s_ready = (
            sem(x) for x in ("r_ps", "r_ready", "u_ps", "u_ready", "sk_ps", "s_ready"))
        kvs_ready, pt_ps, pt_ready, m_ps, m_ready, bb_ready, y_ps, yb_ready, h_ready, counted = (
            sem(x) for x in ("kvs_ready", "pt_ps", "pt_ready", "m_ps", "m_ready", "bb_ready", "y_ps", "yb_ready",
                             "dh_ready", "d_counted"))
        PLACES = (((0, 1), (2,), (3,)), ((0, 1, 2), (3, 4), (5,)), ((0, 1, 2), (3, 4), (5,)), ((), (), ()),
                  ((0, 1), (2, 3), ()), ((0, 1, 2, 3), (), ()))
        LV = NL + 1
        UP = 2 * (NC - 1)

        def front_bank(x):
            return (2, 3, 6, 7)[x]

        def bc(row, n, w=P):
            return row[:, None, :].to_broadcast([P, n, w])

        def seq(t, par):
            return t[:, par * NC:(par + 1) * NC]

        def left(t, s):
            return t.rearrange("p (q t) -> p q t", t=2 * s)[:, :, 0:s]

        def flat(t):
            return t.rearrange("p c t -> p (c t)")

        def two_banks(par):
            return k.ps[:, par * 4 + 2:par * 4 + 4, 0:GW]

        def by_bank(t, par):
            return seq(t, par).rearrange("p (a c) t -> p a (c t)", a=2)

        def all_pairs(eng, body):
            with eng.Fori(0, PAIRS // 2 - 1) as i:
                for p in range(2):
                    with eng.Fori(i * 2 + p, i * 2 + (p + 1)) as pair:
                        body(pair, p, False, False)
            body(PAIRS - 2, 0, True, False)
            body(PAIRS - 1, 1, False, True)

        with nc.Block() as block:
            @block.vector
            def _(dve):
                def norm(i, g):
                    for j in range(GC):
                        c = (g % 2) * GC + j
                        at = i * (2 * NC) + ((g // 2) * NC + c)
                        last = nc.vector.tensor_scalar(
                            xl[:, g, j, :], k.h[:, i * 2 + g // 2, c, :], k.mean[:, bass.ds(at, 1)],
                            k.rstd[:, bass.ds(at, 1)], ALU.subtract, ALU.mult)
                    last.then_inc(normed, 1)

                def keys_values(i, q, m):
                    dve.wait_ge(kv_ps, i * 12 + (m + 1))
                    nc.vector.tensor_tensor(kvl[:, q, m, :], k.ps[:, front_bank(m % 4), 0:2 * C + 1],
                                            k.kvl_b[:, :], ALU.add).then_inc(kv_ready, 1)

                def unit_keys(i, q):
                    dve.wait_ge(rooted, i + 1)
                    rk2 = rk[:].rearrange("p (s c) -> p s c", c=NC)
                    nks2 = nks[:].rearrange("p (s c) -> p s c", c=NC)
                    nc.vector.reciprocal(rk2[:, :, 0:NC - 1], nks2[:, :, 0:NC - 1])
                    nc.vector.reciprocal(rk2[0:LAST, :, NC - 1], nks2[0:LAST, :, NC - 1]).then_inc(rk_ready, 1)
                    dve.wait_ge(rk_ready, i + 2)
                    for g in range(4):
                        m = g * GC
                        nc.vector.tensor_tensor(kh[:, q, m:m + GC, :], kvl[:, q, m:m + GC, 0:C],
                                                rk[:, m:m + GC, None].to_broadcast([P, GC, P]),
                                                ALU.mult).then_inc(kh_ready, 1)

                def gram(i, par):
                    dve.wait_ge(gram_ps, i * 4 + (par * 2 + 2))
                    nc.vector.tensor_tensor(by_bank(NT, par).rearrange("p a (c t) -> p a c t", t=P),
                                            two_banks(par).rearrange("p a (c t) -> p a c t", t=P),
                                            k.upper[:, None, None, :].to_broadcast([P, 2, GC, P]), ALU.mult)
                    evens = two_banks(par).rearrange("p a (n t) -> p a n t", t=2)[:, :, :, 0]
                    nc.vector.tensor_tensor(seq(W, par).rearrange("p (a c) t -> p a c t", a=2),
                                            evens.rearrange("p a (c t) -> p a c t", t=HALF),
                                            k.cmask[:, 0, None, None, :].to_broadcast([P, 2, GC, HALF]),
                                            ALU.mult).then_inc(near, 1)
                    dve.wait_ge(near, i * 2 + (par + 1))
                    dve.wait_ge(reset, i * 2 + (par + 1))
                    nc.vector.tensor_tensor(left(flat(seq(D, par)), 1)[:, :, 0].rearrange("p (c t) -> p c t", t=HALF),
                                            bc(left(k.ident[:, :], 1)[:, :, 0], NC, HALF), seq(W, par),
                                            ALU.subtract).then_inc(d_ready, 1)

                def masked(i, lv, par):
                    dve.wait_ge(w_ps, i * (2 * NL) + ((lv - 1) * 2 + par + 1))
                    nc.vector.tensor_tensor(seq(W, par), k.ps[:, par * 4, 0:GW].rearrange("p (c t) -> p c t", t=HALF),
                                            bc(k.cmask[:, lv, :], NC, HALF), ALU.mult).then_inc(w_ready, 1)

                def levels(i, first, last_pair):
                    for par in range(2):
                        masked(i, 1, par)
                    for lv in range(1, LV):
                        s = LEVELS[lv - 1]
                        for par in range(2):
                            dve.wait_ge(x_ps, i * (2 * NL) + ((lv - 1) * 2 + par + 1))
                            d = left(flat(seq(D, par)), s)
                            nc.vector.tensor_tensor(d, d, k.ps[:, par * 4 + 1, 0:GW].rearrange("p (q t) -> p q t", t=s),
                                                    ALU.subtract).then_inc(d_ready, 1)
                        if lv < LV - 1:
                            for par in range(2):
                                masked(i, lv + 1, par)
                        if lv in (1, 2) and not last_pair:
                            for g in (2 * lv - 2, 2 * lv - 1):
                                dve.wait_ge(turned, i * 4 + (g + 1))
                                dve.wait_ge(h_ready, i * 4 + (g + 1))
                                norm(i + 1, g)
                        if lv in (3, 4) and not first:
                            stats(i - 1, lv - 3)

                def stats(i, par):
                    dve.wait_ge(h_ready, i * 4 + (2 * par + 2 + 4))
                    for c in range(NC):
                        at = i * (2 * NC) + (par * NC + c)
                        last = nc.vector.bn_stats(k.st[:, at, :], k.h[:, i * 2 + par, c, :])
                    last.then_inc(counted, 1)

                def part(i, q, c, xs):
                    if c in (1, 2):
                        for x in xs:
                            keys_values(i, q, (c - 1) * 6 + x)

                def body(i, p, before_last, last_pair):
                    q = 1 - p
                    for c in range(NC):
                        for par in range(2):
                            if c:
                                dve.wait_ge(r_ps, i * UP + ((c - 1) * 2 + par + 1))
                                nc.vector.tensor_tensor(R[:, par, :], kvl[:, p, par * NC + c, C:2 * C],
                                                        k.ps[:, par * 4, 0:P], ALU.subtract).then_inc(r_ready, 1)
                        if not last_pair:
                            part(i + 1, q, c, (0, 1))
                        for par in range(2):
                            dve.wait_ge(u_ps, i * 12 + (c * 2 + par + 1))
                            nc.vector.tensor_scalar(UU[:, par, P:2 * P], k.ps[:, par * 4, 0:P],
                                                    kvl[:, p, par * NC + c, 2 * C:2 * C + 1], None, ALU.mult)
                            nc.vector.tensor_copy(UU[:, par, 0:P], k.ps[:, par * 4, 0:P]).then_inc(u_ready, 1)
                        if not last_pair:
                            part(i + 1, q, c, (2, 3, 4, 5))
                            if c == 3:
                                unit_keys(i + 1, q)
                    if not last_pair:
                        gram(i + 1, 0)
                    for par in range(2):
                        dve.wait_ge(m_ps, i * 2 + (par + 1))
                        nc.vector.tensor_tensor(bb[:, par, :], k.ps[:, par * 4, 0:P], k.bo0[:, :],
                                                ALU.add).then_inc(bb_ready, 1)
                    if not last_pair:
                        gram(i + 1, 1)
                    dve.wait_ge(bb_ready, i * 2 + 2)
                    for g in range(4):
                        par = g // 2
                        dve.wait_ge(y_ps, i * 4 + (g + 1))
                        nc.vector.tensor_tensor(yb[:, g], k.ps[:, par * 4 + g % 2, 0:GW].rearrange("p (c t) -> p c t", t=P),
                                                bc(bb[:, par, :], GC), ALU.add).then_inc(yb_ready, 1)
                    if not last_pair:
                        levels(i + 1, False, before_last)

                nc.vector.memset(rk[:], 0.0).then_inc(rk_ready, 1)
                dve.sem_inc(yb_ready, 4)
                for g in range(4):
                    norm(0, g)
                for c in (1, 2):
                    part(0, 0, c, range(6))
                unit_keys(0, 0)
                for par in range(2):
                    gram(0, par)
                levels(0, True, False)
                all_pairs(dve, body)
                for par in range(2):
                    stats(PAIRS - 1, par)
                dve.wait_ge(counted, B)

            @block.gpsimd
            def _(pool):
                pool.sem_inc(h_ready, 4)
                with pool.Fori(0, PAIRS) as i:
                    for g in range(4):
                        b, c0 = i * 2 + g // 2, (g % 2) * GC
                        pool.wait_ge(yb_ready, i * 4 + (g + 5))
                        nc.gpsimd.tensor_tensor(k.h[:, b, c0:c0 + GC, :], k.h[:, b, c0:c0 + GC, :], yb[:, g],
                                                ALU.add).then_inc(h_ready, 1)

            @block.scalar
            def _(act):
                def move(i, q, g):
                    act.wait_ge(turned, i * 4 + (g + 1))
                    nc.scalar.activation(xT[:, q, g // 2, (g % 2) * GW:(g % 2 + 1) * GW],
                                         k.ps[:, front_bank(g), 0:GW], ACT.Copy).then_inc(moved, 1)

                def squares(i, q, c):
                    for m in range((c - 1) * 6, c * 6):
                        act.wait_ge(kv_ready, i * 12 + (m + 1))
                        nc.scalar.activation(kh[:, q, m, :], kvl[:, q, m, 0:C], ACT.Square,
                                             accum_out=nk[:, m:m + 1]).then_inc(squared, 1)
                    if c == 2:
                        act.wait_ge(squared, i * 12 + 12)
                        nc.scalar.activation(nks[:, :], nk[:, :], ACT.Sqrt).then_inc(rooted, 1)

                def keys(i, q):
                    for g in range(4):
                        act.wait_ge(kT_ps, i * 4 + (g + 1))
                        nc.scalar.activation(flat(kT[:, q, g * GC:(g + 1) * GC, :]), k.ps[:, front_bank(g), 0:GW],
                                             ACT.Copy).then_inc(kT_ready, 1)

                def unit(par):
                    nc.scalar.activation(seq(D, par), bc(k.ident[:, :], NC), ACT.Copy).then_inc(reset, 1)

                def levels(i, last_pair):
                    for lv in range(LV):
                        for par in range(2):
                            act.wait_ge(t_ps, i * (2 * LV) + (lv * 2 + par + 1))
                            nc.scalar.activation(by_bank(DT, par), two_banks(par), ACT.Copy).then_inc(dt_ready, 1)
                    if not last_pair:
                        for par in range(2):
                            unit(par)

                def body(i, p, before_last, last_pair):
                    q = 1 - p
                    for c in range(NC):
                        if not last_pair:
                            if c == 0:
                                for g in range(3):
                                    move(i + 1, q, g)
                            if c == 4:
                                keys(i + 1, q)
                        for par in range(2):
                            act.wait_ge(sk_ps, i * 12 + (c * 2 + par + 1))
                            if c < NC - 1:
                                nc.scalar.activation(S[:, par, :], k.ps[:, par * 4 + 1, 0:P], ACT.Copy).then_inc(s_ready, 1)
                            else:
                                nc.scalar.activation(kvs[:, par, :], k.ps[:, par * 4 + 1, P:2 * P],
                                                     ACT.Copy).then_inc(kvs_ready, 1)
                        if not last_pair:
                            if c == 0:
                                move(i + 1, q, 3)
                            if c in (1, 2):
                                squares(i + 1, q, c)
                    for par in range(2):
                        act.wait_ge(pt_ps, i * 2 + (par + 1))
                        nc.scalar.activation(PT[:, par, :], k.ps[:, par * 4, 0:P + 1], ACT.Copy).then_inc(pt_ready, 1)
                    for par in range(2):
                        act.wait_ge(m_ps, i * 2 + (par + 1))
                        nc.scalar.activation(M[:, par, :], k.ps[:, par * 4 + 1, 0:P], ACT.Copy).then_inc(m_ready, 1)
                    if not last_pair:
                        levels(i + 1, before_last)

                for par in range(2):
                    unit(par)
                for g in range(4):
                    move(0, 0, g)
                for c in (1, 2):
                    squares(0, 0, c)
                keys(0, 0)
                levels(0, False)
                all_pairs(act, body)

            @block.tensor
            def _(pe):
                def front(i, q, c, x):
                    bank = front_bank(x % 4)
                    if c == 0:
                        pe.wait_ge(normed, i * 4 + (x + 1))
                        for j in range(GC):
                            last = nc.tensor.transpose(k.ps[:, bank, j * P:(j + 1) * P], xl[:, x, j, :], k.ident[:, :])
                        last.then_inc(turned, 1)
                    elif c < 3:
                        m = (c - 1) * 6 + x
                        bank = front_bank(m % 4)
                        if m < 4:
                            pe.wait_ge(moved, i * 4 + (m + 1))
                        else:
                            pe.wait_ge(kv_ready, i * 12 + (m - 3))
                        nc.tensor.matmul(k.ps[:, bank, 0:2 * C + 1], xT[:, q, m // NC, (m % NC) * P:(m % NC + 1) * P],
                                         k.wkvl[:, :], start=True, stop=True).then_inc(kv_ps, 1)
                    elif c == 4:
                        if x == 0:
                            pe.wait_ge(kv_ready, i * 12 + 12)
                        pe.wait_ge(kh_ready, i * 4 + (x + 1))
                        for j in range(GC):
                            last = nc.tensor.transpose(k.ps[:, bank, j * P:(j + 1) * P], kh[:, q, x * GC + j, :],
                                                       k.ident[:, :])
                        last.then_inc(kT_ps, 1)
                    else:
                        pe.wait_ge(kT_ready, i * 4 + (x + 1))
                        for j in range(GC):
                            kc = kT[:, q, x * GC + j, :]
                            last = nc.tensor.matmul(k.ps[:, bank, j * P:(j + 1) * P], kc, kc, start=True, stop=True)
                        last.then_inc(gram_ps, 1)

                def turn(i, lv, par):
                    pe.wait_ge(d_ready, i * (2 * LV) + (lv * 2 + par + 1))
                    for c in range(NC):
                        last = nc.tensor.transpose(k.ps[:, par * 4 + 2 + c // GC, (c % GC) * P:(c % GC + 1) * P],
                                                   D[:, par * NC + c, :], k.ident[:, :])
                    last.then_inc(t_ps, 1)

                def n_d(lv, par):
                    s = LEVELS[lv - 1]
                    for c in range(NC):
                        m = par * NC + c
                        last = nc.tensor.matmul(
                            k.ps[:, par * 4, c * HALF:(c + 1) * HALF].rearrange("p (q t) -> p q t", t=s),
                            NT[:, m, :], left(D[:, m, :], s), start=True, stop=True)
                    last.then_inc(w_ps, 1)

                def levels(i):
                    for par in range(2):
                        turn(i, 0, par)
                        pe.wait_ge(yb_ready, i * 4 + 2 * par + 2)
                        n_d(1, par)
                    for lv in range(1, LV):
                        for par in range(2):
                            pe.wait_ge(w_ready, i * (2 * NL) + ((lv - 1) * 2 + par + 1))
                            pe.wait_ge(dt_ready, i * (2 * LV) + ((lv - 1) * 2 + par + 1))
                            for c in range(NC):
                                m = par * NC + c
                                last = nc.tensor.matmul(k.ps[:, par * 4 + 1, c * HALF:(c + 1) * HALF],
                                                        DT[:, m, :], W[:, m, :], start=True, stop=True)
                            last.then_inc(x_ps, 1)
                        for par in range(2):
                            turn(i, lv, par)
                            if lv < LV - 1:
                                n_d(lv + 1, par)

                def body(i, p, before_last, last_pair):
                    q = 1 - p

                    def part(c, where):
                        if not last_pair:
                            for x in PLACES[c][where]:
                                front(i + 1, q, c, x)

                    for c in range(NC):
                        n = rows(c)
                        if c:
                            for par in range(2):
                                pe.wait_ge(s_ready, i * UP + ((c - 1) * 2 + par + 1))
                                nc.tensor.matmul(k.ps[:, par * 4, 0:P], kT[:, p, par * NC + c, :], S[:, par, :],
                                                 start=True, stop=True).then_inc(r_ps, 1)
                        if c == 0:
                            pe.wait_ge(dt_ready, i * (2 * LV) + 2 * LV)
                        part(c, 0)
                        for par in range(2):
                            if c == 0:
                                rhs = kvl[:, p, par * NC, C:2 * C]
                            else:
                                pe.wait_ge(r_ready, i * UP + ((c - 1) * 2 + par + 1))
                                rhs = R[:, par, :]
                            nc.tensor.matmul(k.ps[:, par * 4, 0:P], DT[:, par * NC + c, :], rhs,
                                             start=True, stop=True).then_inc(u_ps, 1)
                        part(c, 1)
                        for par in range(2):
                            pe.wait_ge(u_ready, i * 12 + (c * 2 + par + 1))
                            nc.tensor.matmul(k.ps[:, par * 4 + 1, 0:2 * P], kh[0:n, p, par * NC + c, :], UU[0:n, par, :],
                                             start=(c == 0), stop=True, skip_group_check=True).then_inc(sk_ps, 1)
                        part(c, 2)
                    for par in range(2):
                        pe.wait_ge(kvs_ready, i * 2 + (par + 1))
                        nc.tensor.matmul(k.ps[:, par * 4, 0:P + 1], kvs[:, par, :], k.wqb[:, :],
                                         start=True, stop=True).then_inc(pt_ps, 1)
                    for par in range(2):
                        pe.wait_ge(pt_ready, i * 2 + (par + 1))
                        nc.tensor.matmul(k.ps[:, par * 4 + 1, 0:P], PT[:, par, 0:P], k.wo0[:, :], start=True, stop=True)
                        nc.tensor.matmul(k.ps[:, par * 4, 0:P], PT[:, par, P:P + 1].to_broadcast([P, P]), k.wo0[:, :],
                                         start=True, stop=True).then_inc(m_ps, 1)
                    for g in range(4):
                        par = g // 2
                        pe.wait_ge(m_ready, i * 2 + (par + 1))
                        pe.wait_ge(bb_ready, i * 2 + (par + 1))
                        for j in range(GC):
                            c = (g % 2) * GC + j
                            last = nc.tensor.matmul(k.ps[:, par * 4 + g % 2, j * P:(j + 1) * P],
                                                    xT[:, p, par, c * P:(c + 1) * P], M[:, par, :],
                                                    start=True, stop=True)
                        last.then_inc(y_ps, 1)
                    if not last_pair:
                        levels(i + 1)

                for c in range(NC):
                    for where in range(3):
                        for x in PLACES[c][where]:
                            front(0, 0, c, x)
                levels(0)
                all_pairs(pe, body)


def expert_choice_phase(nc, k):
    stack, sb, sem = phase_scope(nc)
    with stack:
        nt = NormTranspose(nc, k, "r_", sb, sem)
        aff = sb("aff", [P, NC, B * E0])
        z = sb("z", [P, NCH, E0])
        zs = sb("zs", [P, 3, NCH])
        AF = sb("AF", [P, 2, T])
        work = sb("work", [P, 2, T])
        top = sb("top", [P, 2, 8])
        G = sb("G", [P, 2, T])
        Gt = sb("Gt", [P, NC, B * E0])
        gb = sb("gb", [P, 2, TP])
        lg_ps, lg_free, chain, expd = (sem(x) for x in ("lg_ps", "lg_free", "sm_chain", "sm_exp"))
        tk = [sem("topk0"), sem("topk1")]
        af_ps, af_ready, g_ready, gt_ps, gt_ready = (
            sem(x) for x in ("af_ps", "af_ready", "g_ready", "gt_ps", "gt_ready"))

        halves = split_room("e0_", sb, sem, E0)

        with nc.Block() as block:
            @block.gpsimd
            def _(pool):
                split_weights(nc, pool, k.w1_0, halves)

            @block.vector
            def _(dve):
                def body(i, last_pair):
                    if not last_pair:
                        nt.next_pair(dve, i, k.h)

                nt.vector(dve, 0, k.h)
                over_pairs(dve, body)
                dve.wait_ge(lg_free, PAIRS + 1)
                nc.vector.tensor_reduce(zs[:, 0, :], z[:], AX_X, ALU.max).then_inc(chain, 1)
                dve.wait_ge(chain, 1)
                nc.vector.tensor_tensor(z[:], z[:], zs[:, 0, :, None].to_broadcast([P, NCH, E0]),
                                        ALU.subtract).then_inc(chain, 1)
                dve.wait_ge(expd, 1)
                nc.vector.tensor_reduce(zs[:, 1, :], z[:], AX_X, ALU.add).then_inc(chain, 1)
                dve.wait_ge(chain, 3)
                nc.vector.reciprocal(zs[:, 2, :], zs[:, 1, :]).then_inc(chain, 1)
                dve.wait_ge(chain, 4)
                by_sequence = zs[:, 2, :].rearrange("p (b c) -> p b c", c=NC)[:, :, :, None]
                nc.vector.tensor_tensor(aff[:].rearrange("p c (b e) -> p b c e", e=E0),
                                        z[:].rearrange("p (b c) e -> p b c e", c=NC),
                                        by_sequence.to_broadcast([P, B, NC, E0]), ALU.mult).then_inc(chain, 1)
                n = [0, 0]

                def chained(hf, ins):
                    n[hf] += 1
                    ins.then_inc(tk[hf], 1)

                rounds = (CAP + 7) // 8
                for r in range(rounds):
                    src = AF if r == 0 else work
                    for hf in range(2):
                        if r == 0:
                            dve.wait_ge(af_ready, hf + 1)
                        else:
                            dve.wait_ge(tk[hf], n[hf])
                        chained(hf, nc.vector.max(top[:, hf, :], src[:, hf, :]))
                    if r == rounds - 1 and CAP % 8:
                        for hf in range(2):
                            dve.wait_ge(tk[hf], n[hf])
                            chained(hf, nc.vector.memset(top[:, hf, CAP % 8:8], -1.0))
                    for hf in range(2):
                        dve.wait_ge(tk[hf], n[hf])
                        chained(hf, nc.vector.match_replace(work[:, hf, :], top[:, hf, :], src[:, hf, :], -1.0))
                for hf in range(2):
                    dve.wait_ge(tk[hf], n[hf])
                    nc.vector.scalar_tensor_tensor(out=G[:, hf, :], in0=work[:, hf, :], scalar=0.0,
                                                   in1=AF[:, hf, :], op0=ALU.is_lt, op1=ALU.mult).then_inc(g_ready, 1)

            @block.scalar
            def _(act):
                act.sem_inc(lg_free, 1)
                with act.Fori(0, PAIRS) as i:
                    nt.scalar(act, i)
                    act.wait_ge(lg_ps, i + 1)
                    nc.scalar.activation(z[:, bass.ds(i * 12, 12), :],
                                         k.ps[:, 4, 0:12 * E0].rearrange("p (m e) -> p m e", e=E0),
                                         ACT.Copy).then_inc(lg_free, 1)
                act.wait_ge(chain, 2)
                nc.scalar.activation(z[:], z[:], ACT.Exp).then_inc(expd, 1)
                for hf in range(2):
                    act.wait_ge(af_ps, hf + 1)
                    nc.scalar.activation(AF[:, hf, :], k.psf[:, hf * 1024:hf * 1024 + T], ACT.Copy).then_inc(af_ready, 1)
                for hf in range(2):
                    act.wait_ge(gt_ps, hf + 1)
                    o = 2048 + hf * 1024
                    nc.scalar.activation(Gt[:, 0:NC - 1, hf * P:(hf + 1) * P],
                                         k.psf[:, o:o + 5 * P].rearrange("p (c e) -> p c e", e=P), ACT.Copy)
                    nc.scalar.activation(Gt[0:LAST, NC - 1, hf * P:(hf + 1) * P],
                                         k.psf[0:LAST, o + 5 * P:o + 6 * P], ACT.Copy).then_inc(gt_ready, 1)
                act.wait_ge(gt_ready, 2)

            @block.tensor
            def _(pe):
                with pe.Fori(0, PAIRS) as i:
                    nt.tensor(pe, i)
                    pe.wait_ge(lg_free, i + 1)
                    for m in range(12):
                        if m % GC == 0:
                            pe.wait_ge(nt.moved, i * 4 + (m // GC + 1))
                        par, c = m // NC, m % NC
                        last = nc.tensor.matmul(k.ps[:, 4, m * E0:(m + 1) * E0], nt.xT[:, par, c * P:(c + 1) * P],
                                                k.gate0[:, :], start=True, stop=True)
                    last.then_inc(lg_ps, 1)
                pe.wait_ge(chain, 5)
                for hf in range(2):
                    for c in range(NC):
                        n = rows(c)
                        last = nc.tensor.transpose(k.psf[:, hf * 1024 + c * P:hf * 1024 + c * P + n],
                                                   aff[0:n, c, hf * P:(hf + 1) * P], k.ident[0:n, 0:n])
                    last.then_inc(af_ps, 1)
                for hf in range(2):
                    pe.wait_ge(g_ready, hf + 1)
                    for c in range(NC):
                        n = rows(c)
                        last = nc.tensor.transpose(k.psf[0:n, 2048 + hf * 1024 + c * P:2048 + hf * 1024 + (c + 1) * P],
                                                   G[:, hf, c * P:c * P + n], k.ident[:, :])
                    last.then_inc(gt_ps, 1)

        expert_block(nc, k, "e0_", sb, sem, nt, gb, E0, 1, ACT.Gelu_apprx_tanh, halves, k.b1_0, k.w2_0,
                     lambda i, c, par, e, n: Gt[0:n, c, bass.ds(i * (2 * E0) + par * E0 + e, 1)])

        b2_ps, b2_added, b2_counted = sem("b2_ps"), sem("b2_added"), sem("b2_counted")
        with nc.Block() as block:
            @block.tensor
            def _(pe):
                for q in range(2 * NC):
                    hf, c = q // NC, q % NC
                    n = rows(c)
                    if q >= 4:
                        pe.wait_ge(b2_added, q - 3)
                    for s in range(2):
                        last = nc.tensor.matmul(k.ps[0:n, (q % 4) * 2 + s, :], G[:, hf, c * P:c * P + n],
                                                k.b2_0[:, s * 4:(s + 1) * 4, :].rearrange("p b d -> p (b d)"),
                                                start=True, stop=True)
                    last.then_inc(b2_ps, 1)

            @block.vector
            def _(dve):
                def stats(q):
                    hf, c = q // NC, q % NC
                    dve.wait_ge(b2_added, q + 1)
                    for b in range(hf * 8, hf * 8 + 8):
                        last = nc.vector.bn_stats(k.st[:, b * NC + c, :], k.h[:, b, c, :])
                    last.then_inc(b2_counted, 1)

                for q in range(2 * NC):
                    hf, c = q // NC, q % NC
                    n = rows(c)
                    dve.wait_ge(b2_ps, q + 1)
                    o = (q % 4) * 1024
                    hh = k.h[0:n, hf * 8:(hf + 1) * 8, c, :]
                    nc.vector.tensor_tensor(hh, hh, k.psf[0:n, o:o + 1024].rearrange("p (b d) -> p b d", d=C),
                                            ALU.add).then_inc(b2_added, 1)
                    if q:
                        stats(q - 1)
                stats(2 * NC - 1)
                dve.wait_ge(b2_counted, 2 * NC)


def split_room(tag, sb, sem, n):
    return (sb(tag + "w1h", [P, n, P], mybir.dt.float32r), sb(tag + "w1l", [P, n, P], mybir.dt.float32r),
            sem(tag + "w_split"))


def split_weights(nc, pool, w1, room):
    w1h, w1l, w_split = room
    nc.gpsimd.tensor_copy(w1h[:], w1[:]).then_inc(w_split, 1)
    pool.wait_ge(w_split, 1)
    nc.gpsimd.tensor_tensor(w1l[:], w1[:], w1h[:].bitcast(F32), ALU.subtract).then_inc(w_split, 1)


def expert_block(nc, k, tag, sb, sem, nt, gb, experts, fh, func, w1, b1, w2, gate):
    F32R = mybir.dt.float32r
    w1h, w1l, w_split = w1
    xh = sb(tag + "xh", [P, 4, GW], F32R)
    xlo = sb(tag + "xlo", [P, 4, GW], F32R)
    normed, full, free = sem(tag + "normed"), sem(tag + "full"), sem(tag + "free")
    split, o_ps, added = sem(tag + "split"), sem(tag + "o_ps"), sem(tag + "added")
    U = 2 * experts
    HP = 2 * fh
    PIECES = U * HP + 4
    slots = {2: 2, 3: 3, experts + 2: 0, experts + 3: 1}

    def pieces(last):
        out, n = [], 2
        for u in range(U):
            if u in slots and not (last and slots[u] < 2):
                out.append((n, "turn", slots[u], u))
                n += 1
            for x in range(HP):
                out.append((n, "hidden", u, x))
                n += 1
        assert last or n == PIECES + 2
        return out

    def at(i, n):
        return i * PIECES + n

    with nc.Block() as block:
        @block.vector
        def _(dve):
            dve.sem_inc(added, 2)

            def norm(i, g):
                for j in range(GC):
                    c = (g % 2) * GC + j
                    col = i * (2 * NC) + ((g // 2) * NC + c)
                    last = nc.vector.tensor_scalar(
                        nt.xl[:, g, j, :], k.h[:, i * 2 + g // 2, c, :], k.mean[:, bass.ds(col, 1)],
                        k.rstd[:, bass.ds(col, 1)], ALU.subtract, ALU.mult)
                last.then_inc(normed, 1)

            def body(i, last_pair):
                for g in (2, 3):
                    norm(i, g)
                for u in range(U):
                    par, e = u // experts, u % experts
                    b = i * 2 + par
                    if u == experts and not last_pair:
                        for g in (0, 1):
                            norm(i + 1, g)
                    dve.wait_ge(o_ps, i * U + (u + 3))
                    if u % experts:
                        dve.wait_ge(added, i * U + (u + 2))
                    else:
                        dve.wait_ge(normed, i * 4 + (par * 2 + 2))
                    for c in range(NC):
                        n = rows(c)
                        o = 2048 + (u % 2) * 1024 + c * P
                        last = nc.vector.scalar_tensor_tensor(
                            out=k.h[0:n, b, c, :], in0=k.psf[0:n, o:o + P],
                            scalar=gate(i, c, par, e, n), in1=k.h[0:n, b, c, :], op0=ALU.mult, op1=ALU.add)
                    last.then_inc(added, 1)

            norm(0, 0)
            norm(0, 1)
            over_pairs(dve, body)
            dve.wait_ge(added, PAIRS * U + 2)

        @block.gpsimd
        def _(pool):
            def halve(i, g, count):
                x = nt.xT[:, g // 2, (g % 2) * GW:(g % 2 + 1) * GW]
                pool.wait_ge(free, count)
                nc.gpsimd.tensor_tensor(xlo[:, g], x, xh[:, g].bitcast(F32), ALU.subtract).then_inc(split, 1)

            halve(0, 0, 1 + 4)
            halve(0, 1, 2 + 4)

            def body(i, last_pair):
                for n, kind, g, _ in pieces(last_pair):
                    if kind == "turn":
                        halve(i if g >= 2 else i + 1, g, at(i, n + 1 + 4))

            over_pairs(pool, body)

        @block.scalar
        def _(act):
            act.sem_inc(free, 4)

            def move(g, bank):
                nc.scalar.activation(nt.xT[:, g // 2, (g % 2) * GW:(g % 2 + 1) * GW], k.ps[:, bank, 0:GW], ACT.Copy)
                nc.scalar.activation(xh[:, g], k.ps[:, bank, 0:GW], ACT.Copy).then_inc(free, 1)

            for g in range(2):
                act.wait_ge(full, g + 1)
                move(g, g)

            def body(i, last_pair):
                for n, kind, q, x in pieces(last_pair):
                    act.wait_ge(full, at(i, n + 1))
                    if kind == "turn":
                        move(q, n % 4)
                        continue
                    u, e = q, q % experts
                    if x == 0:
                        act.wait_ge(o_ps, i * U + (u + 1))
                    f, s = x // 2, x % 2
                    nc.scalar.activation(gb[:, (u % 2) * fh + f, s * 384:s * 384 + NFREE[s]],
                                         k.ps[:, n % 4, 0:NFREE[s]], func,
                                         bias=b1[:, e * fh + f:e * fh + f + 1]).then_inc(free, 1)

            over_pairs(act, body)

        @block.tensor
        def _(pe):
            def turn(i, g, bank):
                pe.wait_ge(normed, i * 4 + (g + 1))
                for j in range(GC):
                    last = nc.tensor.transpose(k.ps[:, bank, j * P:(j + 1) * P], nt.xl[:, g, j, :], k.ident[:, :])
                last.then_inc(full, 1)

            def output(i, u, count):
                e = u % experts
                pe.wait_ge(free, count)
                pe.wait_ge(added, i * U + (u + 1))
                for c in range(NC):
                    n = rows(c)
                    o = 2048 + (u % 2) * 1024 + c * P
                    for f in range(fh):
                        last = nc.tensor.matmul(k.psf[0:n, o:o + P], gb[:, (u % 2) * fh + f, c * P:c * P + n],
                                                w2[:, e * fh + f, :], start=(f == 0), stop=(f == fh - 1))
                last.then_inc(o_ps, 1)

            def body(i, last_pair):
                done = {}
                for n, kind, q, x in pieces(last_pair):
                    pe.wait_ge(free, at(i, n + 1))
                    if kind == "turn":
                        turn(i if q >= 2 else i + 1, q, n % 4)
                        continue
                    u, e, par = q, q % experts, q // experts
                    f, s = x // 2, x % 2
                    g, w = par * 2 + s, NFREE[s]
                    if e == 0 and f == 0:
                        pe.wait_ge(split, i * 4 + (g + 1))
                    ps = k.ps[:, n % 4, 0:w]
                    nc.tensor.matmul(ps, w1h[:, e * fh + f, :], xh[:, g, 0:w], start=True, stop=False)
                    nc.tensor.matmul(ps, w1h[:, e * fh + f, :], xlo[:, g, 0:w], start=False, stop=False)
                    nc.tensor.matmul(ps, w1l[:, e * fh + f, :], xh[:, g, 0:w],
                                     start=False, stop=True).then_inc(full, 1)
                    done[u] = n + 1 + 4
                    if x == HP - 1 and u:
                        output(i, u - 1, at(i, done[u - 1]))
                output(i, U - 1, at(i, done[U - 1]))

            pe.sem_inc(o_ps, 2)
            turn(0, 0, 0)
            turn(0, 1, 1)
            pe.wait_ge(w_split, 2)
            over_pairs(pe, body)


def video_phase(nc, k):
    stack, sb, sem = phase_scope(nc)
    with stack:
        st = sb("vst", [P, NC, 6])
        mv = sb("vmv", [P, NC, 2])
        r1 = sb("vr1", [P, NC])
        r2 = sb("vr2", [P, NC])
        vx = sb("vx", [P, NC, C])
        vT = sb("vT", [P, NC * P])
        vD = sb("vD", [P, FR, 2, NV])
        stats, rooted, chain, normed = sem("v_stats"), sem("v_root"), sem("v_chain"), sem("v_normed")
        vt_ps, vt_ready, k_ps, v_ps, zero, laid, vd_ready = (
            sem(x) for x in ("vt_ps", "vt_ready", "vk_ps", "vv_ps", "v_zero", "v_laid", "vd_ready"))
        with nc.Block() as block:
            @block.gpsimd
            def _(pool):
                nc.gpsimd.memset(k.Kbd, 0.0).then_inc(zero, 1)
                nc.gpsimd.memset(k.Vbd, 0.0).then_inc(zero, 1)
                pool.wait_ge(vt_ready, 1)
                src = vT[:].rearrange("p (v a) -> p v a", a=NV)
                nc.gpsimd.tensor_copy(vD[:, :, 0, :], src)
                nc.gpsimd.tensor_copy(vD[:, :, 1, :], src).then_inc(vd_ready, 1)

            @block.vector
            def _(dve):
                for c in range(NC):
                    nc.vector.bn_stats(st[:, c, :], k.video[:, c, :]).then_inc(stats, 1)
                dve.wait_ge(stats, NC)
                for c in range(NC):
                    nc.vector.bn_aggr(mv[:, c, :], st[:, c, :]).then_inc(stats, 1)
                dve.wait_ge(rooted, 1)
                nc.vector.reciprocal(r2[:, :], r1[:, :]).then_inc(chain, 1)
                dve.wait_ge(chain, 1)
                for c in range(NC):
                    nc.vector.tensor_scalar(vx[:, c, :], k.video[:, c, :], mv[:, c, 0:1], r2[:, c:c + 1],
                                            ALU.subtract, ALU.mult).then_inc(normed, 1)
                dve.wait_ge(zero, 2)
                for s in range(2):
                    dve.wait_ge(k_ps, s + 1)
                    ps = k.ps[:, 2 + s, 0:GW].rearrange("p (v a) -> p v a", a=NV)
                    for hd in range(2):
                        q = slice(hd * 64, hd * 64 + 64)
                        nc.vector.tensor_scalar(k.Kbd[q, s * 6:(s + 1) * 6, q], ps[q, :, :], k.bk[q, 0:1], None, ALU.add)
                for s in range(3):
                    dve.wait_ge(v_ps, s + 1)
                    ps = k.ps[:, 4 + s, :].rearrange("p (v d) -> p v d", d=C)
                    for hd in range(2):
                        q = slice(hd * 64, hd * 64 + 64)
                        nc.vector.tensor_tensor(k.Vbd[q, s * 4:(s + 1) * 4, q], ps[q, :, q],
                                                k.bv[q, None, q].to_broadcast([64, 4, 64]), ALU.add).then_inc(laid, 1)
                dve.wait_ge(laid, 6)
                nc.vector.tensor_scalar(k.Vbd, k.Vbd, 1.0 / NV, None, ALU.mult).then_inc(laid, 1)
                dve.wait_ge(laid, 7)

            @block.scalar
            def _(act):
                act.wait_ge(stats, 2 * NC)
                nc.scalar.activation(r1[:, :], mv[:, :, 1], ACT.Sqrt, bias=k.eps[:, 0:1]).then_inc(rooted, 1)
                act.wait_ge(vt_ps, 1)
                nc.scalar.activation(vT[:, :], k.psf[:, 0:NC * P], ACT.Identity, scale=k.g1[:, 0:1],
                                     bias=k.b1n[:, 0:1]).then_inc(vt_ready, 1)

            @block.tensor
            def _(pe):
                for c in range(NC):
                    pe.wait_ge(normed, c + 1)
                    last = nc.tensor.transpose(k.psf[:, c * P:(c + 1) * P], vx[:, c, :], k.ident[:, :])
                last.then_inc(vt_ps, 1)
                pe.wait_ge(vt_ready, 1)
                for s in range(2):
                    nc.tensor.matmul(k.ps[:, 2 + s, 0:GW], k.wk[:, :], vT[:, s * GW:(s + 1) * GW],
                                     start=True, stop=True).then_inc(k_ps, 1)
                pe.wait_ge(vd_ready, 1)
                for v in range(FR):
                    last = nc.tensor.matmul(k.ps[:, 4 + v // 4, (v % 4) * C:(v % 4 + 1) * C],
                                            vD[:, v].rearrange("p h a -> p (h a)"), k.wv[:, :], start=True, stop=True)
                    if v % 4 == 3:
                        last.then_inc(v_ps, 1)


def attention_phase(nc, k):
    stack, sb, sem = phase_scope(nc)
    with stack:
        nt = NormTranspose(nc, k, "a_", sb, sem)
        qT = sb("qT", [P, 2, TP])
        nm = sb("nm", [P, 2, P], BF16)
        eb = sb("eb", [P, 3, FR, P])
        t1 = sb("t1", [P, 6, P])
        t2 = sb("t2", [P, 3, P])
        t3 = sb("t3", [P, P])
        den = sb("den", [P, 2, P])
        rd = sb("rd", [P, 2, P])
        aT = sb("aT", [P, 2, P])
        q_ps, q_ready, l_ps, m_ready, shifted, e_ready = (
            sem(x) for x in ("q_ps", "q_ready", "l_ps", "nm_ready", "shifted", "e_ready"))
        tree, summed, rd_ready, w_ready, a_ps, a_ready, o_ps, o_ready = (
            sem(x) for x in ("tree", "summed", "rd_ready", "aw_ready", "a_ps", "a_ready", "ao_ps", "ao_ready"))
        counted = sem("ao_counted")
        ST = 2 * NC
        slots = {1: 2, 3: 3, NC + 1: 0, NC + 3: 1}
        big = k.big[:].rearrange("p b c d -> p (b c) d")

        def lbanks(j):
            o = 3 * (j % 2) * 512
            return k.psf[:, o:o + FR * P].rearrange("p (v t) -> p v t", t=P)

        def slot(i, j, last_pair):
            g = slots.get(j)
            if g is None or (g < 2 and last_pair):
                return None
            return (i, g) if g >= 2 else (i + 1, g)

        def over_steps(eng, step):
            for j in range(ST):
                step(0, j, j, False)
            with eng.Fori(1, PAIRS - 1) as i:
                for j in range(ST):
                    step(i, j, ST, False)
            for j in range(ST + 3):
                step(PAIRS - 1, j, ST, True)

        with nc.Block() as block:
            @block.vector
            def _(dve):
                def query(i, g, bank):
                    dve.wait_ge(q_ps, i * 4 + (g + 1))
                    nc.vector.tensor_scalar(qT[:, g // 2, (g % 2) * GW:(g % 2 + 1) * GW], k.ps[:, bank, 0:GW],
                                            k.bq[:, 0:1], 0.125, ALU.add, ALU.mult).then_inc(q_ready, 1)

                def step(i, j, past, last_pair):
                    if j < ST:
                        dve.wait_ge(l_ps, i * ST + (j + 1))
                        nc.vector.tensor_reduce(nm[:, j % 2, :], lbanks(j).rearrange("p v t -> p t v"), AX_X,
                                                ALU.max, negate=True).then_inc(m_ready, 1)
                    before = slot(i, j - 1, last_pair)
                    if before:
                        query(before[0], before[1], 7)
                    nxt = slot(i, j + 1, last_pair)
                    if nxt:
                        nt.norm(nxt[0], nxt[1], k.h)
                    if past >= 1 and j <= ST:
                        w = j - 1
                        dve.wait_ge(summed, i * ST + (w + 1))
                        nc.vector.reciprocal(rd[:, w % 2, :], den[:, w % 2, :]).then_inc(rd_ready, 1)
                        dve.wait_ge(rd_ready, i * ST + (w + 1))
                        nc.vector.tensor_tensor(eb[:, w % 3], eb[:, w % 3],
                                                rd[:, w % 2, None, :].to_broadcast([P, FR, P]),
                                                ALU.mult).then_inc(w_ready, 1)
                    if past >= 3:
                        dve.wait_ge(o_ps, i * ST + (j - 3 + 1))
                        nc.vector.tensor_tensor(big[:, i * ST + (j - 3), :], k.ps[:, 7, 0:P], k.bo1[:, :],
                                                ALU.add).then_inc(o_ready, 1)
                    if past >= 4:
                        dve.wait_ge(o_ready, i * ST + (j - 4 + 1))
                        nc.vector.bn_stats(k.st[:, i * ST + (j - 4), :], big[:, i * ST + (j - 4), :]).then_inc(counted, 1)

                for g in range(2):
                    nt.norm(0, g, k.h)
                for g in range(2):
                    query(0, g, 4 + g)
                over_steps(dve, step)
                dve.wait_ge(o_ready, NCH)
                nc.vector.bn_stats(k.st[:, NCH - 1, :], big[:, NCH - 1, :]).then_inc(counted, 1)
                dve.wait_ge(counted, NCH)

            @block.scalar
            def _(act):
                def step(i, j, past, last_pair):
                    now = slot(i, j, last_pair)
                    if now:
                        nt.move(act, now[0], now[1], 7, k.g1[:, 0:1], k.b1n[:, 0:1])
                    if past >= 2 and j < ST + 2:
                        act.wait_ge(a_ps, i * ST + (j - 2 + 1))
                        nc.scalar.activation(aT[:, j % 2, :], k.ps[:, 6, 0:P], ACT.Copy).then_inc(a_ready, 1)
                    if j < ST:
                        act.wait_ge(shifted, i * ST + (j + 1))
                        nc.scalar.activation(eb[:, j % 3], lbanks(j), ACT.Exp).then_inc(e_ready, 1)

                for g in range(2):
                    nt.move(act, 0, g, 6 + g, k.g1[:, 0:1], k.b1n[:, 0:1])
                over_steps(act, step)

            @block.gpsimd
            def _(pool):
                with pool.Fori(0, PAIRS) as i:
                    for j in range(ST):
                        e = eb[:, j % 3]
                        pool.wait_ge(e_ready, i * ST + (j + 1))
                        nc.gpsimd.tensor_tensor(t1[:], e[:, 0:6], e[:, 6:12], ALU.add).then_inc(tree, 1)
                        pool.wait_ge(tree, i * (3 * ST) + (3 * j + 1))
                        nc.gpsimd.tensor_tensor(t2[:], t1[:, 0:3], t1[:, 3:6], ALU.add).then_inc(tree, 1)
                        pool.wait_ge(tree, i * (3 * ST) + (3 * j + 2))
                        nc.gpsimd.tensor_tensor(t3[:], t2[:, 0], t2[:, 1], ALU.add).then_inc(tree, 1)
                        pool.wait_ge(tree, i * (3 * ST) + (3 * j + 3))
                        nc.gpsimd.tensor_tensor(den[:, j % 2, :], t3[:], t2[:, 2], ALU.add).then_inc(summed, 1)

            @block.tensor
            def _(pe):
                def query(i, g, bank):
                    pe.wait_ge(nt.moved, i * 4 + (g + 1))
                    nc.tensor.matmul(k.ps[:, bank, 0:GW], k.wq[:, :], nt.xT[:, g // 2, (g % 2) * GW:(g % 2 + 1) * GW],
                                     start=True, stop=True).then_inc(q_ps, 1)

                def step(i, j, past, last_pair):
                    now, before = slot(i, j, last_pair), slot(i, j - 1, last_pair)
                    if j < ST:
                        if j % NC == 0:
                            pe.wait_ge(q_ready, i * 4 + (2 + 2 * (j // NC)))
                        if past >= 2:
                            pe.wait_ge(e_ready, i * ST + (j - 1))
                        for v in range(FR):
                            last = nc.tensor.matmul(lbanks(j)[:, v, :], k.Kbd[:, v, :],
                                                    qT[:, j // NC, (j % NC) * P:(j % NC + 1) * P],
                                                    start=(v % 4 == 0), stop=True, skip_group_check=True)
                        last.then_inc(l_ps, 1)
                    if now or before:
                        if past >= 4:
                            pe.wait_ge(o_ready, i * ST + (j - 3))
                    if now:
                        if past < 4 and j > 1:
                            pe.wait_ge(q_ready, now[0] * 4 + now[1])
                        nt.turn(pe, now[0], now[1], 7)
                    if before:
                        query(before[0], before[1], 7)
                    if past >= 2 and j < ST + 2:
                        a = j - 2
                        pe.wait_ge(w_ready, i * ST + (a + 1))
                        if past >= 3:
                            pe.wait_ge(a_ready, i * ST + a)
                        for v in range(FR):
                            last = nc.tensor.matmul(k.ps[:, 6, 0:P], k.Vbd[:, v, :],
                                                    eb[:, a % 3, v, :], start=(v == 0), stop=(v == FR - 1))
                        last.then_inc(a_ps, 1)
                    if past >= 3:
                        o = j - 3
                        pe.wait_ge(a_ready, i * ST + (o + 1))
                        if past >= 4:
                            pe.wait_ge(o_ready, i * ST + o)
                        else:
                            pe.wait_ge(q_ready, 3)
                        if now:
                            pe.wait_ge(nt.moved, now[0] * 4 + (now[1] + 1))
                        if before:
                            pe.wait_ge(q_ready, before[0] * 4 + (before[1] + 1))
                        nc.tensor.matmul(k.ps[:, 7, 0:P], aT[:, o % 2, :], k.wo1[:, :],
                                         start=True, stop=True).then_inc(o_ps, 1)
                    if j < ST:
                        pe.wait_ge(m_ready, i * ST + (j + 1))
                        for s in range(3):
                            last = nc.tensor.matmul(
                                lbanks(j)[:, s * 4:(s + 1) * 4, :], k.identb[:, :],
                                nm[:, j % 2, None, :].to_broadcast([P, 4, P]), start=False, stop=True,
                                skip_group_check=True)
                        last.then_inc(shifted, 1)

                for g in range(2):
                    nt.turn(pe, 0, g, 6 + g)
                for g in range(2):
                    query(0, g, 4 + g)
                over_steps(pe, step)


def attention_out_phase(nc, k):
    stack, sb, sem = phase_scope(nc)
    with stack:
        ol = sb("ol", [P, 4, GC, P])
        og = sb("og", [P, 4, GC, P])
        oT = sb("oT", [P, 4, GC, P])
        bsum = sb("bsum", [P, C])
        normed, normed_v, timed, scaled, ot_ps, ot_ready, l_ps, z1, counted = (
            sem(x) for x in ("on_normed", "on_normed_v", "on_timed", "on_scaled", "ot_ps", "ot_ready", "lin_ps", "z1",
                             "z_counted"))

        def wait_normed(eng, i, g):
            eng.wait_ge(normed_v if g >= 2 else normed, i * 2 + (g % 2 + 1))

        def bc(row):
            return row[:, None, :].to_broadcast([P, GC, P])

        with nc.Block() as block:
            @block.vector
            def _(dve):
                def norm_by_vector(i, g):
                    for j in range(GC):
                        at = i * (2 * NC) + (g * GC + j)
                        last = nc.vector.tensor_scalar(
                            ol[:, g, j, :], k.big[:, i * 2 + g // 2, (g % 2) * GC + j, :],
                            k.rstd[:, bass.ds(at, 1)], k.mean[:, bass.ds(at, 1)], ALU.mult, ALU.add)
                    last.then_inc(normed_v, 1)

                def body(i, last_pair):
                    for g in range(4):
                        b, c0 = i * 2 + g // 2, (g % 2) * GC
                        dve.wait_ge(l_ps, i * 4 + (g + 1))
                        nc.vector.tensor_tensor(k.big[:, b, c0:c0 + GC, :],
                                                k.ps[:, 4 + g, 0:GW].rearrange("p (c t) -> p c t", t=P),
                                                og[:, g], ALU.add).then_inc(z1, 1)
                        if g >= 2 and not last_pair:
                            norm_by_vector(i + 1, g)
                    for g in range(4):
                        dve.wait_ge(z1, i * 4 + (g + 5))
                        for j in range(GC):
                            last = nc.vector.bn_stats(k.st[:, i * (2 * NC) + (g * GC + j), :],
                                                      k.big[:, i * 2 + g // 2, (g % 2) * GC + j, :])
                        last.then_inc(counted, 1)

                nc.vector.tensor_tensor(bsum[:], k.b2n[:], k.bl[:], ALU.add).then_inc(counted, 1)
                dve.sem_inc(z1, 4)
                for g in (2, 3):
                    norm_by_vector(0, g)
                over_pairs(dve, body)
                dve.wait_ge(counted, 4 * PAIRS + 1)

            @block.gpsimd
            def _(pool):
                pool.wait_ge(counted, 1)
                with pool.Fori(0, PAIRS) as i:
                    for g in range(4):
                        wait_normed(pool, i, g)
                        pool.wait_ge(z1, i * 4 + (g + 1))
                        nc.gpsimd.tensor_tensor(og[:, g], ol[:, g], bc(k.g2), ALU.mult).then_inc(timed, 1)
                        pool.wait_ge(timed, i * 4 + (g + 1))
                        nc.gpsimd.tensor_tensor(og[:, g], og[:, g], bc(bsum), ALU.add).then_inc(scaled, 1)

            @block.tensor
            def _(pe):
                with pe.Fori(0, PAIRS) as i:
                    for g in range(5):
                        if g < 4:
                            wait_normed(pe, i, g)
                            for j in range(GC):
                                last = nc.tensor.transpose(k.ps[:, g, j * P:(j + 1) * P], ol[:, g, j, :],
                                                           k.ident[:, :])
                            last.then_inc(ot_ps, 1)
                        if g:
                            q = g - 1
                            pe.wait_ge(ot_ready, i * 4 + (q + 1))
                            pe.wait_ge(scaled, i * 4 + (q + 1))
                            for j in range(GC):
                                last = nc.tensor.matmul(k.ps[:, 4 + q, j * P:(j + 1) * P], oT[:, q, j, :],
                                                        k.wl[:, :], start=True, stop=True)
                            last.then_inc(l_ps, 1)

            @block.scalar
            def _(act):
                def norm(i, g):
                    for j in range(GC):
                        at = i * (2 * NC) + (g * GC + j)
                        last = nc.scalar.activation(
                            ol[:, g, j, :], k.big[:, i * 2 + g // 2, (g % 2) * GC + j, :], ACT.Identity,
                            scale=k.rstd[:, bass.ds(at, 1)], bias=k.mean[:, bass.ds(at, 1)])
                    last.then_inc(normed, 1)

                def body(i, last_pair):
                    for g in range(4):
                        act.wait_ge(ot_ps, i * 4 + (g + 1))
                        nc.scalar.activation(oT[:, g].rearrange("p c t -> p (c t)"), k.ps[:, g, 0:GW],
                                             ACT.Identity, scale=k.g2c[:, 0:1], bias=k.b2c[:, 0:1]).then_inc(ot_ready, 1)
                    if not last_pair:
                        for g in range(2):
                            act.wait_ge(timed, i * 4 + (g + 1))
                            norm(i + 1, g)

                for g in range(2):
                    norm(0, g)
                over_pairs(act, body)


def attention_add_phase(nc, k):
    stack, sb, sem = phase_scope(nc)
    with stack:
        ol = sb("ol3", [P, 4, GC, P])
        normed, timed, scaled, biased, added, counted = (
            sem(x) for x in ("an_normed", "an_timed", "an_scaled", "an_biased", "an_added", "an_counted"))

        def bc(row):
            return row[:, None, :].to_broadcast([P, GC, P])

        with nc.Block() as block:
            @block.vector
            def _(dve):
                def body(i, last_pair):
                    for g in range(4):
                        b, c0 = i * 2 + g // 2, (g % 2) * GC
                        hh = k.h[:, b, c0:c0 + GC, :]
                        dve.wait_ge(scaled, i * 4 + (g + 1))
                        if g >= 2:
                            nc.vector.tensor_tensor(ol[:, g], ol[:, g], bc(k.b3n), ALU.add).then_inc(biased, 1)
                            dve.wait_ge(biased, i * 2 + (g - 1))
                        nc.vector.tensor_tensor(hh, hh, ol[:, g], ALU.add).then_inc(added, 1)
                    for g in range(4):
                        dve.wait_ge(added, i * 4 + (g + 1))
                        for j in range(GC):
                            last = nc.vector.bn_stats(k.st[:, i * (2 * NC) + (g * GC + j), :],
                                                      k.h[:, i * 2 + g // 2, (g % 2) * GC + j, :])
                        last.then_inc(counted, 1)

                over_pairs(dve, body)
                dve.wait_ge(counted, 4 * PAIRS)

            @block.scalar
            def _(act):
                def norm(i, g):
                    for j in range(GC):
                        at = i * (2 * NC) + (g * GC + j)
                        last = nc.scalar.activation(
                            ol[:, g, j, :], k.big[:, i * 2 + g // 2, (g % 2) * GC + j, :], ACT.Identity,
                            scale=k.rstd[:, bass.ds(at, 1)], bias=k.mean[:, bass.ds(at, 1)])
                    last.then_inc(normed, 1)

                def body(i, last_pair):
                    for g in range(4):
                        if not last_pair:
                            act.wait_ge(added, i * 4 + (g + 1))
                            norm(i + 1, g)

                for g in range(4):
                    norm(0, g)
                over_pairs(act, body)

            @block.gpsimd
            def _(pool):
                with pool.Fori(0, PAIRS) as i:
                    for g in range(4):
                        pool.wait_ge(normed, i * 4 + (g + 1))
                        if g >= 2:
                            nc.gpsimd.tensor_tensor(ol[:, g], ol[:, g], bc(k.g3), ALU.mult).then_inc(scaled, 1)
                        else:
                            nc.gpsimd.tensor_tensor(ol[:, g], ol[:, g], bc(k.g3), ALU.mult).then_inc(timed, 1)
                            pool.wait_ge(timed, i * 2 + (g + 1))
                            nc.gpsimd.tensor_tensor(ol[:, g], ol[:, g], bc(k.b3n), ALU.add).then_inc(scaled, 1)


def token_choice_phase(nc, k):
    stack, sb, sem = phase_scope(nc)
    with stack:
        nt = NormTranspose(nc, k, "t_", sb, sem)
        lg = sb("lg", [P, NCH, E1])
        l2 = sb("l2", [P, NCH, E1])
        oh = sb("oh", [P, 2, NCH, E1])
        pr = sb("pr", [P, NCH, E1])
        mx = sb("mx", [P, 2, NCH])
        pm = sb("pm", [P, NCH])
        wt = sb("wt", [P, NC, B, E1])
        wT = sb("wT", [P, NC, P])
        rb = sb("rb", [P, 4, TP])
        lg_ps, biased, chain, expd, wt_ps, wt_ready = (
            sem(x) for x in ("tl_ps", "biased", "t_chain", "t_exp", "wt_ps", "wt_ready"))
        by_chunk = wt[:].rearrange("p c b e -> p b c e")
        WT_DONE = 17

        halves = split_room("e1_", sb, sem, 2 * E1)

        with nc.Block() as block:
            @block.gpsimd
            def _(pool):
                split_weights(nc, pool, k.w1_1, halves)

            @block.vector
            def _(dve):
                def body(i, last_pair):
                    if not last_pair:
                        nt.next_pair(dve, i, k.h)
                    dve.wait_ge(lg_ps, i + 1)
                    nc.vector.tensor_tensor(lg[:, bass.ds(i * 12, 12), :],
                                            k.ps[:, 4, 0:12 * E1].rearrange("p (m e) -> p m e", e=E1),
                                            k.gate_b[:, None, :].to_broadcast([P, 12, E1]), ALU.add).then_inc(biased, 1)

                dve.sem_inc(biased, 1)
                nt.vector(dve, 0, k.h)
                over_pairs(dve, body)
                dve.wait_ge(biased, PAIRS + 1)
                n = [0]

                def link(ins):
                    n[0] += 1
                    ins.then_inc(chain, 1)
                    dve.wait_ge(chain, n[0])

                prio = k.prio[:, None, :].to_broadcast([P, NCH, E1])

                def wide(a):
                    return a[:, :, None].to_broadcast([P, NCH, E1])

                for q in range(2):
                    src = lg if q == 0 else l2
                    link(nc.vector.tensor_reduce(mx[:, q, :], src[:], AX_X, ALU.max))
                    link(nc.vector.tensor_tensor(pr[:], src[:], wide(mx[:, q, :]), ALU.is_equal))
                    link(nc.vector.tensor_tensor(pr[:], pr[:], prio, ALU.mult))
                    link(nc.vector.tensor_reduce(pm[:], pr[:], AX_X, ALU.max))
                    link(nc.vector.tensor_tensor(oh[:, q], prio, wide(pm[:, :]), ALU.is_equal))
                    if q == 0:
                        link(nc.vector.scalar_tensor_tensor(out=l2[:], in0=oh[:, 0], scalar=-3.0e38, in1=lg[:],
                                                            op0=ALU.mult, op1=ALU.add))
                link(nc.vector.tensor_tensor(pm[:], mx[:, 1, :], mx[:, 0, :], ALU.subtract))
                assert n[0] == 12
                dve.wait_ge(expd, 1)
                link(nc.vector.tensor_scalar(pm[:], mx[:, 0, :], 1.0, None, ALU.add))
                link(nc.vector.reciprocal(mx[:, 1, :], pm[:]))
                link(nc.vector.tensor_tensor(mx[:, 0, :], mx[:, 0, :], mx[:, 1, :], ALU.mult))
                link(nc.vector.tensor_tensor(l2[:], oh[:, 1], wide(mx[:, 0, :]), ALU.mult))
                link(nc.vector.tensor_tensor(pr[:], oh[:, 0], wide(mx[:, 1, :]), ALU.mult))
                nc.vector.tensor_tensor(by_chunk, l2[:].rearrange("p (b c) e -> p b c e", c=NC),
                                        pr[:].rearrange("p (b c) e -> p b c e", c=NC), ALU.add).then_inc(chain, 1)
                assert n[0] == WT_DONE

            @block.scalar
            def _(act):
                with act.Fori(0, PAIRS) as i:
                    nt.scalar(act, i)
                act.wait_ge(chain, 12)
                nc.scalar.activation(mx[:, 0, :], pm[:], ACT.Exp).then_inc(expd, 1)
                act.wait_ge(wt_ps, 1)
                nc.scalar.activation(wT[:].rearrange("p c t -> p (c t)"), k.psf[:, 0:NC * P], ACT.Copy).then_inc(wt_ready, 1)
                act.wait_ge(wt_ready, 1)

            @block.tensor
            def _(pe):
                with pe.Fori(0, PAIRS) as i:
                    nt.tensor(pe, i)
                    pe.wait_ge(biased, i + 1)
                    for m in range(12):
                        if m % GC == 0:
                            pe.wait_ge(nt.moved, i * 4 + (m // GC + 1))
                        last = nc.tensor.matmul(k.ps[:, 4, m * E1:(m + 1) * E1],
                                                nt.xT[:, m // NC, (m % NC) * P:(m % NC + 1) * P],
                                                k.gate1[:, :], start=True, stop=True)
                    last.then_inc(lg_ps, 1)
                pe.wait_ge(chain, WT_DONE + 1)
                for c in range(NC):
                    last = nc.tensor.transpose(k.psf[:, c * P:(c + 1) * P], wt[:, c].rearrange("p b e -> p (b e)"),
                                               k.ident[:, :])
                last.then_inc(wt_ps, 1)

        expert_block(nc, k, "e1_", sb, sem, nt, rb, E1, 2, ACT.Relu, halves, k.b1_1, k.w2_1,
                     lambda i, c, par, e, n: by_chunk_flat(wt)[0:n, bass.ds(i * (2 * E1) + (c * B * E1 + par * E1 + e), 1)])

        b2_ps, b2_added, stored = sem("b2b_ps"), sem("b2b_added"), k.stored
        with nc.Block() as block:
            @block.tensor
            def _(pe):
                for c in range(NC):
                    n = rows(c)
                    for s in range(4):
                        q = c * 4 + s
                        if q >= 8:
                            pe.wait_ge(b2_added, q - 7)
                        nc.tensor.matmul(k.ps[0:n, q % 8, :], wT[:, c, 0:n],
                                         k.b2_1[:, s * 4:(s + 1) * 4, :].rearrange("p b d -> p (b d)"),
                                         start=True, stop=True).then_inc(b2_ps, 1)

            @block.vector
            def _(dve):
                for c in range(NC):
                    n = rows(c)
                    for s in range(4):
                        q = c * 4 + s
                        dve.wait_ge(b2_ps, q + 1)
                        hh = k.h[0:n, s * 4:(s + 1) * 4, c, :]
                        nc.vector.tensor_tensor(hh, hh, k.ps[0:n, q % 8, :].rearrange("p (b d) -> p b d", d=C),
                                                ALU.add).then_inc(b2_added, 1)

            @block.sync
            def _(sp):
                for c in range(NC):
                    sp.wait_ge(b2_added, 4 * (c + 1))
                    store_chunk(sp, k, c).then_inc(stored, 16)
                sp.wait_ge(stored, 16 * NC)


def by_chunk_flat(wt):
    return wt[:].rearrange("p c b e -> p (c b e)")


def store_chunk(sp, k, c):
    n = rows(c)
    return sp.dma_start(k.out[:, c * P:c * P + n, :].rearrange("b t d -> t b d"), k.h[0:n, :, c, :])


def audio_tower(nc, a, out):
    k = Ctx()
    with ExitStack() as ctx:
        def sb(name, shape, dt=F32):
            return ctx.enter_context(nc.sbuf_tensor(name, shape, dt))

        k.out = out
        k.xT = a["xT"]
        k.ps = ctx.enter_context(nc.psum_tensor("banks", [P, 8, 512], F32))[:]
        k.psf = k.ps.rearrange("p b n -> p (b n)")
        k.h = sb("h", [P, B, NC, C])
        k.mean = sb("mean", [P, NCH])
        k.rstd = sb("rstd", [P, NCH])
        k.st = sb("st", [P, NCH, 6])
        k.eps = sb("eps", [P, 1])
        k.w_in = ctx.enter_context(nc.semaphore("w_in"))
        k.rest_in = ctx.enter_context(nc.semaphore("rest_in"))
        k.stored = ctx.enter_context(nc.semaphore("stored"))
        k.norm_chain, k.norm_rooted = (
            ctx.enter_context(nc.semaphore(x)) for x in ("norm_chain", "norm_rooted"))
        k.norm_past = (0, 0)

        first, rest = [], []

        def load(name, shape, dram, group=rest, dt=F32):
            t = sb(name, shape, dt)
            group.append((t[:], dram))
            return t

        cw = a["L0_tok_WT"]
        k.wc01 = load("wc01", [P, C], cw[0:128, :], first)
        k.wc23 = load("wc23", [P, C], cw[128:256, :], first)
        k.wc4 = load("wc4", [64, C], cw[256:320, :], first)

        def col(name, src, group=rest):
            return load(name, [P, 1], a[src].rearrange("(p a) -> p a", a=1), group)

        def row(name, src, lo=0, n=C):
            return load(name, [P, n], a[src][lo:lo + n].partition_broadcast(P))

        k.conv_b = col("conv_b", "L0_tok_b", first)
        k.gamma = col("gamma", "L0_tok_gamma", first)
        k.beta = col("beta", "L0_tok_beta", first)
        k.ident = load("ident", [P, P], a["ident"], first)
        k.cmask = load("cmask", [P, NL + 1, HALF], a["cmask"])
        k.upper = load("upper", [P, P], a["upper"])
        k.prio = load("prio", [P, E1], a["prio"].partition_broadcast(P))
        k.wkvl = sb("wkvl", [P, 2 * C + 1])
        rest.append((k.wkvl[:, 0:2 * C], a["L0_attn_WgT"][:, C:3 * C]))
        rest.append((k.wkvl[:, 2 * C:], a["L0_attn_WlrT"]))
        k.kvl_b = sb("kvl_b", [P, 2 * C + 1])
        rest.append((k.kvl_b[:, 0:2 * C], a["L0_attn_bg"][C:3 * C].partition_broadcast(P)))
        rest.append((k.kvl_b[:, 2 * C:], a["L0_attn_blr"].partition_broadcast(P)))
        k.wqb = sb("wqb", [P, C + 1])
        rest.append((k.wqb[:, 0:C], a["L0_attn_Wg"][0:C, :]))
        rest.append((k.wqb[:, C:], a["L0_attn_bg"][0:C].rearrange("(p a) -> p a", a=1)))
        k.wo0 = load("wo0", [P, C], a["L0_attn_WoT"])
        k.bo0 = row("bo0", "L0_attn_bo")
        k.gate0 = load("gate0", [P, E0], a["L0_ffn_gate_weight"])
        k.w1_0 = load("w1_0", [P, E0, P], a["L0_ffn_w1"].rearrange("e d f -> d e f"))
        k.w2_0 = load("w2_0", [P, E0, C], a["L0_ffn_w2"].rearrange("e f d -> f e d"))
        k.b1_0 = load("b1_0", [P, E0], a["L0_ffn_b1T"])
        k.b2_0 = sb("b2_0", [P, 8, C])
        k.b2_1 = sb("b2_1", [P, B, C])
        k.video = load("video", [P, NC, C], a["video"].rearrange("(c p) d -> p c d", p=P))
        k.wq = load("wq", [P, C], a["L1_attn_WqT"])
        k.wk = load("wk", [P, C], a["L1_attn_WkT"])
        k.wv = load("wv", [P, C], a["L1_attn_WvT"])
        k.wo1 = load("wo1", [P, C], a["L1_attn_WoT"])
        k.wl = load("wl", [P, C], a["L1_attn_WlT"])
        k.g1 = col("g1", "L1_attn_ln1_g")
        k.b1n = col("b1n", "L1_attn_ln1_b")
        k.bq = col("bq", "L1_attn_bq")
        k.bk = col("bk", "L1_attn_bk")
        k.bv = row("bv", "L1_attn_bv")
        k.bo1 = row("bo1", "L1_attn_bo")
        k.g2 = row("g2", "L1_attn_ln2_g")
        k.b2n = row("b2n", "L1_attn_ln2_b")
        k.g2c = col("g2c", "L1_attn_ln2_g")
        k.b2c = col("b2c", "L1_attn_ln2_b")
        k.bl = row("bl", "L1_attn_bl")
        k.g3 = row("g3", "L1_attn_ln3_g")
        k.b3n = row("b3n", "L1_attn_ln3_b")
        k.gate1 = load("gate1", [P, E1], a["L1_ffn_gate_w"])
        k.gate_b = row("gate_b", "L1_ffn_gate_b", 0, E1)
        k.w1_1 = load("w1_1", [P, 2 * E1, P], a["L1_ffn_w1T"])
        k.w2_1 = load("w2_1", [P, 2 * E1, C], a["L1_ffn_w2"].rearrange("e (f p) d -> p (e f) d", p=P))
        k.b1_1 = load("b1_1", [P, 2 * E1], a["L1_ffn_b1T"])
        block_diagonal = [(k.b2_0[b * E0:(b + 1) * E0, b, :], a["L0_ffn_b2"]) for b in range(8)]
        block_diagonal += [(k.b2_1[b * E1:(b + 1) * E1, b, :], a["L1_ffn_b2"]) for b in range(B)]
        k.first_loads, k.rest_loads, k.zeroed_loads = first, rest, block_diagonal

        k.identb = sb("identb", [P, P], BF16)
        conv_phase(nc, k)
        norm_phase(nc, k, "n0")
        delta_phase(nc, k)
        norm_phase(nc, k, "n1")
        expert_choice_phase(nc, k)
        norm_phase(nc, k, "n2", twice=True)
        with ExitStack() as att:
            k.big = att.enter_context(nc.sbuf_tensor("o_all", [P, B, NC, C], F32))
            k.Kbd, k.Vbd = k.w1_0[:, 0:FR, :], k.w2_0[:, 0:FR, :]
            video_phase(nc, k)
            attention_phase(nc, k)
            norm_phase(nc, k, "n3", shift=True)
            attention_out_phase(nc, k)
            norm_phase(nc, k, "n4", shift=True)
            attention_add_phase(nc, k)
        norm_phase(nc, k, "n5")
        token_choice_phase(nc, k)


def shape_constants():
    t = np.arange(P)
    masks = []
    for s in (1,) + LEVELS:
        same = (t[:, None] // (2 * s)) == (t[None, :] // (2 * s))
        lower = same & (t[:, None] % (2 * s) >= s)
        masks.append(lower[:, t % (2 * s) < s].astype(np.float32))
    cmask = np.ascontiguousarray(np.stack(masks, axis=1))
    return {
        "ident": np.eye(P, dtype=np.float32),
        "cmask": cmask,
        "upper": np.triu(np.ones((P, P), np.float32), 1),
        "prio": np.arange(E1, 0, -1).astype(np.float32),
    }


def kernel(**inputs):
    import concourse.bacc as bacc
    from concourse.bass_utils import run_bass_kernel_spmd

    x = {n: np.asarray(v) for n, v in inputs.items()}
    lay = {
        "xT": x["x"].transpose(2, 0, 1),
        "L0_tok_WT": x["L0_tok_W"].T,
        "L0_attn_WgT": x["L0_attn_Wg"].T,
        "L0_attn_WlrT": x["L0_attn_Wlr"].T,
        "L0_attn_WoT": x["L0_attn_Wo"].T,
        "L0_ffn_b1T": x["L0_ffn_b1"].T,
        "video": x["L1_attn_video_embeds"].transpose(1, 0, 2).reshape(FR * NV, C),
        "L1_attn_WqT": x["L1_attn_Wq"].T,
        "L1_attn_WkT": x["L1_attn_Wk"].T,
        "L1_attn_WvT": x["L1_attn_Wv"].T,
        "L1_attn_WoT": x["L1_attn_Wo"].T,
        "L1_attn_WlT": x["L1_attn_Wl"].T,
        "L1_ffn_w1T": x["L1_ffn_w1"].transpose(1, 0, 2).reshape(C, 2 * E1, P),
        "L1_ffn_b1T": x["L1_ffn_b1"].reshape(2 * E1, P).T,
    }
    for name in ("L0_tok_b", "L0_tok_gamma", "L0_tok_beta", "L0_attn_bg", "L0_attn_blr", "L0_attn_Wg", "L0_attn_bo",
                 "L0_ffn_gate_weight", "L0_ffn_w1", "L0_ffn_w2", "L0_ffn_b2", "L1_attn_ln1_g", "L1_attn_ln1_b",
                 "L1_attn_bq", "L1_attn_bk", "L1_attn_bv", "L1_attn_bo", "L1_attn_bl", "L1_attn_ln2_g",
                 "L1_attn_ln2_b", "L1_attn_ln3_g", "L1_attn_ln3_b", "L1_ffn_gate_w", "L1_ffn_gate_b", "L1_ffn_w2",
                 "L1_ffn_b2"):
        lay[name] = x[name]
    lay.update(shape_constants())
    lay = {n: np.ascontiguousarray(v) for n, v in lay.items()}

    nc = bacc.Bacc("TRN2", target_bir_lowering=False, num_devices=1)
    aps = {n: nc.dram_tensor(f"in_{n}", v.shape, mybir.dt.from_np(v.dtype), kind="ExternalInput").ap()
           for n, v in lay.items()}
    out = nc.dram_tensor("out", (B, T, C), F32, kind="ExternalOutput").ap()
    audio_tower(nc, aps, out)
    r = run_bass_kernel_spmd(nc, [{f"in_{n}": v for n, v in lay.items()}], core_ids=[0])
    return r.results[0]["out"]
```
